# Optimizing a Trainium2 kernel written in Bass

```python
import numpy as np
import jax
import jax.numpy as jnp

def _softmax(x, axis=-1):
    return jax.nn.softmax(x, axis=axis)

def _gelu(x):
    return jax.nn.gelu(x, approximate=True)

def _silu(x):
    return jax.nn.silu(x)

def _sigmoid(x):
    return jax.nn.sigmoid(x)

def _layernorm(x, axis=-1, eps=1e-05):
    m = jnp.mean(x, axis=axis, keepdims=True)
    v = jnp.var(x, axis=axis, keepdims=True)
    return (x - m) / jnp.sqrt(v + eps)

def _scatter_add(tgt, idx, src, axis=0):
    return tgt.at[idx].add(src)

def _segment_sum(src, seg, n):
    return jax.ops.segment_sum(src, seg, n)
kernel_name = 'mk_adaln_ffn_d2_seqx_r8_fcacf7'

def setup_inputs(seed: int=0):
    np.random.seed(seed)
    _w = jnp.asarray

    def _rec_inputs():
        import jax
        import jax.numpy as jnp
        _rk = jax.random.key(seed)
        x = 7.22e-05 + 1 * jax.random.normal(jax.random.fold_in(_rk, 1), (32, 128, 128), jnp.float32)
        _lenS = 128 - jax.random.randint(jax.random.fold_in(_rk, 7), (32,), 0, max(1, 128 // 4) + 1, jnp.int32)
        _lenS2 = 128 - jax.random.randint(jax.random.fold_in(_rk, 8), (32,), 0, max(1, 128 // 4) + 1, jnp.int32)
        cond_512 = 0.0061147 + 1.02565 * jax.random.normal(jax.random.fold_in(_rk, 11), (32, 64), jnp.float32)
        itok_BxS_0_999 = jax.random.randint(jax.random.fold_in(_rk, 12), (32, 128), 0, 125, jnp.int32)
        itok_BxS_0_4 = jax.random.randint(jax.random.fold_in(_rk, 13), (32, 128), 0, 5, jnp.int32)
        cond_64 = 0.0990542 + 1.04422 * jax.random.normal(jax.random.fold_in(_rk, 15), (32, 64), jnp.float32)
        fside_Bx32_0 = -0.136436 + 0.990155 * jax.random.normal(jax.random.fold_in(_rk, 16), (32, 32), jnp.float32)
        _validS = jnp.arange(128)[None, :] < _lenS[:, None]
        _validS2 = jnp.arange(128)[None, :] < _lenS2[:, None]
        _causal = jnp.tril(jnp.ones((128, 128), dtype=bool))
        mask_BxS_ik0 = jnp.where(jnp.broadcast_to(_validS[:, :], (32, 128)), 0, 1).astype(jnp.int32)
        return (x, cond_512, itok_BxS_0_999, itok_BxS_0_4, cond_64, fside_Bx32_0, mask_BxS_ik0)
    x, cond_512, itok_BxS_0_999, itok_BxS_0_4, cond_64, fside_Bx32_0, mask_BxS_ik0 = _rec_inputs()

    def _L0_cond_setup():
        import jax, jax.numpy as jnp
        import numpy as np
        import math
        HEAD_NUM = 16
        EPS = 1e-08

        def modulated_linear(x, s, aff_w, aff_b, w, b):
            style = s @ aff_w.T + aff_b
            w_mod = w[None, :, :] * style[:, None, :]
            demod = jax.lax.rsqrt(jnp.sum(w_mod * w_mod, axis=2) + EPS)
            w_mod = w_mod * demod[:, :, None]
            return jnp.einsum('bni,boi->bno', x, w_mod) + b
        key = jax.random.key(seed)
        ks = jax.random.split(key, 6)
        B, N, F, S = (8, 128, 128, 64)
        return {'x': jax.random.normal(ks[0], (B, N, F), dtype=jnp.float32), 's': jax.random.normal(ks[1], (B, S), dtype=jnp.float32), 'k_aff_w': jax.random.normal(ks[2], (F, S), dtype=jnp.float32) * 0.02, 'k_aff_b': jnp.ones((F,), dtype=jnp.float32), 'k_w': jax.random.normal(ks[3], (F, F), dtype=jnp.float32) * 0.02, 'k_b': jnp.zeros((F,), dtype=jnp.float32), 'o_aff_w': jax.random.normal(ks[4], (F, S), dtype=jnp.float32) * 0.02, 'o_aff_b': jnp.ones((F,), dtype=jnp.float32), 'o_w': jax.random.normal(ks[5], (F, F), dtype=jnp.float32) * 0.02, 'o_b': jnp.zeros((F,), dtype=jnp.float32)}
    _L0_cond_all = _L0_cond_setup()
    _L0_cond_in = {k: v for k, v in _L0_cond_all.items() if k in ('k_aff_w', 'k_aff_b', 'k_w', 'k_b', 'o_aff_w', 'o_aff_b', 'o_w', 'o_b')}
    del _L0_cond_all

    def _L0_ffn_setup():
        import jax, jax.numpy as jnp
        import numpy as np
        B, T, C, H, E, MIN_E = (4, 256, 128, 128, 16, 2)
        IS_CAUSAL = False

        def _forward(hidden_states, sim_matrix, gates, q_proj, k_proj, v_proj, o_proj):
            b, t, c = hidden_states.shape
            n = b * t
            x = hidden_states.reshape(n, c)
            xn = x / jnp.maximum(jnp.linalg.norm(x, axis=-1, keepdims=True), 1e-12)
            sn = sim_matrix / jnp.maximum(jnp.linalg.norm(sim_matrix, axis=0, keepdims=True), 1e-12)
            logits = xn @ sn - jax.nn.sigmoid(gates)
            gated = jax.nn.relu(logits)
            hard = (gated > 0).astype(gated.dtype)
            mask = gated + jax.lax.stop_gradient(hard - gated)
            inactive = jnp.sum(hard, axis=1) == 0
            _, fb_idx = jax.lax.top_k(logits, MIN_E)
            fb = jnp.zeros((n, logits.shape[1]), gated.dtype).at[jnp.arange(n)[:, None], fb_idx].set(1.0)
            put = jax.lax.stop_gradient(inactive[:, None].astype(gated.dtype) * fb)
            mask = mask * (1.0 - put) + put
            masked = jnp.where(mask > 0, gated, -jnp.inf)
            w = jax.nn.softmax(masked, axis=-1)

            def moe_proj(p):
                y = jnp.einsum('nc,ech->neh', x, p)
                return jnp.einsum('ne,neh->nh', w, y)
            q = moe_proj(q_proj).reshape(b, t, -1)
            k = moe_proj(k_proj).reshape(b, t, -1)
            v = moe_proj(v_proj).reshape(b, t, -1)
            h = q.shape[-1]
            scores = jnp.einsum('bth,bsh->bts', q, k) / jnp.sqrt(jnp.asarray(h, q.dtype))
            if IS_CAUSAL and t > 1:
                causal = jnp.tril(jnp.ones((t, t), bool))
                scores = jnp.where(causal[None], scores, -jnp.inf)
            attn = jax.nn.softmax(scores, axis=-1)
            o = jnp.einsum('bts,bsh->bth', attn, v).reshape(n, h)
            z = jnp.einsum('ne,nh->enh', w, o)
            out = jnp.einsum('enh,ehc->nc', z, o_proj)
            return out.reshape(b, t, c)
        key = jax.random.key(seed)
        ks = jax.random.split(key, 6)
        lim_qkv = float(np.sqrt(6.0 / (C + H)))
        inp = {'hidden_states': jax.random.normal(ks[0], (B, T, C), jnp.float32), 'sim_matrix': jax.random.normal(ks[1], (C, E), jnp.float32), 'gates': jnp.zeros((E,), jnp.float32), 'q_proj': jax.random.uniform(ks[2], (E, C, H), jnp.float32, -lim_qkv, lim_qkv), 'k_proj': jax.random.uniform(ks[3], (E, C, H), jnp.float32, -lim_qkv, lim_qkv), 'v_proj': jax.random.uniform(ks[4], (E, C, H), jnp.float32, -lim_qkv, lim_qkv), 'o_proj': jax.random.uniform(ks[5], (E, H, C), jnp.float32, -lim_qkv, lim_qkv)}
        return inp
    _L0_ffn_all = _L0_ffn_setup()
    _L0_ffn_in = {k: v for k, v in _L0_ffn_all.items() if k in ('sim_matrix', 'gates', 'q_proj', 'k_proj', 'v_proj', 'o_proj')}
    del _L0_ffn_all

    def _L1_cond_setup():
        import jax, jax.numpy as jnp
        import numpy as np
        EPS = 1e-05

        def _ln(x, g, b):
            m = jnp.mean(x, axis=-1, keepdims=True)
            v = jnp.mean((x - m) ** 2, axis=-1, keepdims=True)
            return (x - m) * jax.lax.rsqrt(v + EPS) * g + b

        def _mlp_ln(s, W1, b1, W2, b2, g, b):
            h = jax.nn.silu(s @ W1 + b1) @ W2 + b2
            return _ln(h, g, b)
        key = jax.random.key(seed)
        B, S, D = (4, 256, 128)
        MEM, NOI, RES = (64, 64, 32)
        ks = jax.random.split(key, 40)
        ki = iter(range(40))

        def nrm(shape, scale=0.02):
            return jax.random.normal(ks[next(ki)], shape, jnp.float32) * scale

        def gamma(shape):
            return jnp.ones(shape, jnp.float32) + nrm(shape)
        inp = {'x': jax.random.normal(ks[next(ki)], (B, S, D), jnp.float32), 'pathway_ids': jax.random.randint(ks[next(ki)], (B, S), 0, 125), 'compartment_ids': jax.random.randint(ks[next(ki)], (B, S), 0, 5), 'time_steps': jax.random.randint(ks[next(ki)], (B, S), 0, 5), 'scale_type': jax.random.randint(ks[next(ki)], (B, S), 0, 3), 'memory_state': jax.random.normal(ks[next(ki)], (B, MEM), jnp.float32), 'noise_state': jax.random.normal(ks[next(ki)], (B, NOI), jnp.float32), 'resource_state': jax.random.normal(ks[next(ki)], (B, RES), jnp.float32), 'pw_g': gamma((125, D)), 'pw_b': nrm((125, D)), 'cp_g': gamma((5, D)), 'cp_b': nrm((5, D)), 'tm_g': gamma((5, D)), 'tm_b': nrm((5, D)), 'ms_g': gamma((3, D)), 'ms_b': nrm((3, D)), 'mem_W1': nrm((MEM, D)), 'mem_b1': jnp.zeros((D,)), 'mem_W2': nrm((D, D)), 'mem_b2': jnp.zeros((D,)), 'mem_g': gamma((D,)), 'mem_be': jnp.zeros((D,)), 'noi_W1': nrm((NOI, D)), 'noi_b1': jnp.zeros((D,)), 'noi_W2': nrm((D, D)), 'noi_b2': jnp.zeros((D,)), 'noi_g': gamma((D,)), 'noi_be': jnp.zeros((D,)), 'res_W1': nrm((RES, D)), 'res_b1': jnp.zeros((D,)), 'res_W2': nrm((D, D)), 'res_b2': jnp.zeros((D,)), 'res_g': gamma((D,)), 'res_be': jnp.zeros((D,)), 'int_W1': nrm((6 * D, D)), 'int_b1': jnp.zeros((D,)), 'int_W2': nrm((D, D)), 'int_b2': jnp.zeros((D,)), 'int_g': gamma((D,)), 'int_be': jnp.zeros((D,)), 'aw': jnp.ones((6,), jnp.float32) / 6.0}
        return inp
    _L1_cond_all = _L1_cond_setup()
    _L1_cond_in = {k: v for k, v in _L1_cond_all.items() if k in ('pw_g', 'pw_b', 'cp_g', 'cp_b', 'tm_g', 'tm_b', 'ms_g', 'ms_b', 'mem_W1', 'mem_b1', 'mem_W2', 'mem_b2', 'mem_g', 'mem_be', 'noi_W1', 'noi_b1', 'noi_W2', 'noi_b2', 'noi_g', 'noi_be', 'res_W1', 'res_b1', 'res_W2', 'res_b2', 'res_g', 'res_be', 'int_W1', 'int_b1', 'int_W2', 'int_b2', 'int_g', 'int_be', 'aw')}
    del _L1_cond_all

    def _L1_ffn_setup():
        import jax, jax.numpy as jnp
        import numpy as np
        from jax import lax
        DIM = 128
        HID = 256
        E = 8
        K = 2
        B, T = (2, 64)
        key = jax.random.key(seed)
        ks = jax.random.split(key, 5)
        scale = 1.0 / np.sqrt(DIM)
        x = jax.random.normal(ks[0], (B, T, DIM), dtype=jnp.float32)
        router_w = jax.random.normal(ks[1], (E, DIM), dtype=jnp.float32) * scale
        w_gate = jax.random.normal(ks[2], (E, HID, DIM), dtype=jnp.float32) * scale
        w_up = jax.random.normal(ks[3], (E, HID, DIM), dtype=jnp.float32) * scale
        w_down = jax.random.normal(ks[4], (E, DIM, HID), dtype=jnp.float32) * (1.0 / np.sqrt(HID))
        return {'x': x, 'router_w': router_w, 'w_gate': w_gate, 'w_up': w_up, 'w_down': w_down}
    _L1_ffn_all = _L1_ffn_setup()
    _L1_ffn_in = {k: v for k, v in _L1_ffn_all.items() if k in ('router_w', 'w_gate', 'w_up', 'w_down')}
    del _L1_ffn_all
    return {'x': x, 'cond_512': cond_512, 'itok_BxS_0_999': itok_BxS_0_999, 'itok_BxS_0_4': itok_BxS_0_4, 'cond_64': cond_64, 'fside_Bx32_0': fside_Bx32_0, 'mask_BxS_ik0': mask_BxS_ik0, 'L0_cond_k_aff_w': _L0_cond_in['k_aff_w'], 'L0_cond_k_aff_b': _L0_cond_in['k_aff_b'], 'L0_cond_k_w': _L0_cond_in['k_w'], 'L0_cond_k_b': _L0_cond_in['k_b'], 'L0_cond_o_aff_w': _L0_cond_in['o_aff_w'], 'L0_cond_o_aff_b': _L0_cond_in['o_aff_b'], 'L0_cond_o_w': _L0_cond_in['o_w'], 'L0_cond_o_b': _L0_cond_in['o_b'], 'L0_ffn_sim_matrix': _L0_ffn_in['sim_matrix'], 'L0_ffn_gates': _L0_ffn_in['gates'], 'L0_ffn_q_proj': _L0_ffn_in['q_proj'], 'L0_ffn_k_proj': _L0_ffn_in['k_proj'], 'L0_ffn_v_proj': _L0_ffn_in['v_proj'], 'L0_ffn_o_proj': _L0_ffn_in['o_proj'], 'L1_cond_pw_g': _L1_cond_in['pw_g'], 'L1_cond_pw_b': _L1_cond_in['pw_b'], 'L1_cond_cp_g': _L1_cond_in['cp_g'], 'L1_cond_cp_b': _L1_cond_in['cp_b'], 'L1_cond_tm_g': _L1_cond_in['tm_g'], 'L1_cond_tm_b': _L1_cond_in['tm_b'], 'L1_cond_ms_g': _L1_cond_in['ms_g'], 'L1_cond_ms_b': _L1_cond_in['ms_b'], 'L1_cond_mem_W1': _L1_cond_in['mem_W1'], 'L1_cond_mem_b1': _L1_cond_in['mem_b1'], 'L1_cond_mem_W2': _L1_cond_in['mem_W2'], 'L1_cond_mem_b2': _L1_cond_in['mem_b2'], 'L1_cond_mem_g': _L1_cond_in['mem_g'], 'L1_cond_mem_be': _L1_cond_in['mem_be'], 'L1_cond_noi_W1': _L1_cond_in['noi_W1'], 'L1_cond_noi_b1': _L1_cond_in['noi_b1'], 'L1_cond_noi_W2': _L1_cond_in['noi_W2'], 'L1_cond_noi_b2': _L1_cond_in['noi_b2'], 'L1_cond_noi_g': _L1_cond_in['noi_g'], 'L1_cond_noi_be': _L1_cond_in['noi_be'], 'L1_cond_res_W1': _L1_cond_in['res_W1'], 'L1_cond_res_b1': _L1_cond_in['res_b1'], 'L1_cond_res_W2': _L1_cond_in['res_W2'], 'L1_cond_res_b2': _L1_cond_in['res_b2'], 'L1_cond_res_g': _L1_cond_in['res_g'], 'L1_cond_res_be': _L1_cond_in['res_be'], 'L1_cond_int_W1': _L1_cond_in['int_W1'], 'L1_cond_int_b1': _L1_cond_in['int_b1'], 'L1_cond_int_W2': _L1_cond_in['int_W2'], 'L1_cond_int_b2': _L1_cond_in['int_b2'], 'L1_cond_int_g': _L1_cond_in['int_g'], 'L1_cond_int_be': _L1_cond_in['int_be'], 'L1_cond_aw': _L1_cond_in['aw'], 'L1_ffn_router_w': _L1_ffn_in['router_w'], 'L1_ffn_w_gate': _L1_ffn_in['w_gate'], 'L1_ffn_w_up': _L1_ffn_in['w_up'], 'L1_ffn_w_down': _L1_ffn_in['w_down']}

def reference(x, cond_512, itok_BxS_0_999, itok_BxS_0_4, cond_64, fside_Bx32_0, mask_BxS_ik0, L0_cond_k_aff_w, L0_cond_k_aff_b, L0_cond_k_w, L0_cond_k_b, L0_cond_o_aff_w, L0_cond_o_aff_b, L0_cond_o_w, L0_cond_o_b, L0_ffn_sim_matrix, L0_ffn_gates, L0_ffn_q_proj, L0_ffn_k_proj, L0_ffn_v_proj, L0_ffn_o_proj, L1_cond_pw_g, L1_cond_pw_b, L1_cond_cp_g, L1_cond_cp_b, L1_cond_tm_g, L1_cond_tm_b, L1_cond_ms_g, L1_cond_ms_b, L1_cond_mem_W1, L1_cond_mem_b1, L1_cond_mem_W2, L1_cond_mem_b2, L1_cond_mem_g, L1_cond_mem_be, L1_cond_noi_W1, L1_cond_noi_b1, L1_cond_noi_W2, L1_cond_noi_b2, L1_cond_noi_g, L1_cond_noi_be, L1_cond_res_W1, L1_cond_res_b1, L1_cond_res_W2, L1_cond_res_b2, L1_cond_res_g, L1_cond_res_be, L1_cond_int_W1, L1_cond_int_b1, L1_cond_int_W2, L1_cond_int_b2, L1_cond_int_g, L1_cond_int_be, L1_cond_aw, L1_ffn_router_w, L1_ffn_w_gate, L1_ffn_w_up, L1_ffn_w_down):
    import jax
    import jax.numpy as jnp

    def _L0_cond_ref(x, s, k_aff_w, k_aff_b, k_w, k_b, o_aff_w, o_aff_b, o_w, o_b):
        import jax, jax.numpy as jnp
        import numpy as np
        import math
        HEAD_NUM = 16
        EPS = 1e-08

        def modulated_linear(x, s, aff_w, aff_b, w, b):
            style = s @ aff_w.T + aff_b
            w_mod = w[None, :, :] * style[:, None, :]
            demod = jax.lax.rsqrt(jnp.sum(w_mod * w_mod, axis=2) + EPS)
            w_mod = w_mod * demod[:, :, None]
            return jnp.einsum('bni,boi->bno', x, w_mod) + b
        B, N, F = x.shape
        H = HEAD_NUM
        D = F // H
        kx = modulated_linear(x, s, k_aff_w, k_aff_b, k_w, k_b)
        kx = kx.reshape(B, N, H, D)
        q = k = v = kx
        scores = jnp.einsum('bnhd,bnjd->bnhj', q, k) / math.sqrt(D)
        A = jax.nn.softmax(scores, axis=-1)
        out = jnp.einsum('bnhj,bnjd->bnhd', A, v).reshape(B, N, F)
        out = modulated_linear(out, s, o_aff_w, o_aff_b, o_w, o_b)
        return out

    def _L0_ffn_ref(hidden_states, sim_matrix, gates, q_proj, k_proj, v_proj, o_proj):
        import jax, jax.numpy as jnp
        import numpy as np
        B, T, C, H, E, MIN_E = (4, 256, 128, 128, 16, 2)
        IS_CAUSAL = False

        def _forward(hidden_states, sim_matrix, gates, q_proj, k_proj, v_proj, o_proj):
            b, t, c = hidden_states.shape
            n = b * t
            x = hidden_states.reshape(n, c)
            xn = x / jnp.maximum(jnp.linalg.norm(x, axis=-1, keepdims=True), 1e-12)
            sn = sim_matrix / jnp.maximum(jnp.linalg.norm(sim_matrix, axis=0, keepdims=True), 1e-12)
            logits = xn @ sn - jax.nn.sigmoid(gates)
            gated = jax.nn.relu(logits)
            hard = (gated > 0).astype(gated.dtype)
            mask = gated + jax.lax.stop_gradient(hard - gated)
            inactive = jnp.sum(hard, axis=1) == 0
            _, fb_idx = jax.lax.top_k(logits, MIN_E)
            fb = jnp.zeros((n, logits.shape[1]), gated.dtype).at[jnp.arange(n)[:, None], fb_idx].set(1.0)
            put = jax.lax.stop_gradient(inactive[:, None].astype(gated.dtype) * fb)
            mask = mask * (1.0 - put) + put
            masked = jnp.where(mask > 0, gated, -jnp.inf)
            w = jax.nn.softmax(masked, axis=-1)

            def moe_proj(p):
                y = jnp.einsum('nc,ech->neh', x, p)
                return jnp.einsum('ne,neh->nh', w, y)
            q = moe_proj(q_proj).reshape(b, t, -1)
            k = moe_proj(k_proj).reshape(b, t, -1)
            v = moe_proj(v_proj).reshape(b, t, -1)
            h = q.shape[-1]
            scores = jnp.einsum('bth,bsh->bts', q, k) / jnp.sqrt(jnp.asarray(h, q.dtype))
            if IS_CAUSAL and t > 1:
                causal = jnp.tril(jnp.ones((t, t), bool))
                scores = jnp.where(causal[None], scores, -jnp.inf)
            attn = jax.nn.softmax(scores, axis=-1)
            o = jnp.einsum('bts,bsh->bth', attn, v).reshape(n, h)
            z = jnp.einsum('ne,nh->enh', w, o)
            out = jnp.einsum('enh,ehc->nc', z, o_proj)
            return out.reshape(b, t, c)
        return _forward(hidden_states, sim_matrix, gates, q_proj, k_proj, v_proj, o_proj)

    def _L1_cond_ref(x, pathway_ids, compartment_ids, time_steps, scale_type, memory_state, noise_state, resource_state, pw_g, pw_b, cp_g, cp_b, tm_g, tm_b, ms_g, ms_b, mem_W1, mem_b1, mem_W2, mem_b2, mem_g, mem_be, noi_W1, noi_b1, noi_W2, noi_b2, noi_g, noi_be, res_W1, res_b1, res_W2, res_b2, res_g, res_be, int_W1, int_b1, int_W2, int_b2, int_g, int_be, aw):
        import jax, jax.numpy as jnp
        import numpy as np
        EPS = 1e-05

        def _ln(x, g, b):
            m = jnp.mean(x, axis=-1, keepdims=True)
            v = jnp.mean((x - m) ** 2, axis=-1, keepdims=True)
            return (x - m) * jax.lax.rsqrt(v + EPS) * g + b

        def _mlp_ln(s, W1, b1, W2, b2, g, b):
            h = jax.nn.silu(s @ W1 + b1) @ W2 + b2
            return _ln(h, g, b)
        h = _ln(x, pw_g[pathway_ids], pw_b[pathway_ids])
        h = _ln(h, cp_g[compartment_ids], cp_b[compartment_ids])
        t = _ln(x, tm_g[time_steps], tm_b[time_steps])
        m = x + _mlp_ln(memory_state, mem_W1, mem_b1, mem_W2, mem_b2, mem_g, mem_be)[:, None, :]
        n = x + _mlp_ln(noise_state, noi_W1, noi_b1, noi_W2, noi_b2, noi_g, noi_be)[:, None, :]
        r = x + _mlp_ln(resource_state, res_W1, res_b1, res_W2, res_b2, res_g, res_be)[:, None, :]
        s = _ln(x, ms_g[scale_type], ms_b[scale_type])
        w = jax.nn.softmax(aw)
        cat = jnp.concatenate([w[0] * h, w[1] * t, w[2] * m, w[3] * n, w[4] * r, w[5] * s], axis=-1)
        return _mlp_ln(cat, int_W1, int_b1, int_W2, int_b2, int_g, int_be)

    def _L1_ffn_ref(x, router_w, w_gate, w_up, w_down):
        import jax, jax.numpy as jnp
        import numpy as np
        from jax import lax
        DIM = 128
        HID = 256
        E = 8
        K = 2
        B, T = (2, 64)
        Bb, Tt, D = x.shape
        N = Bb * Tt
        xf = x.reshape(N, D)
        logits = xf @ router_w.T
        routing = jax.nn.softmax(logits, axis=-1)
        top_w, top_i = lax.top_k(routing, K)
        top_w = top_w / jnp.sum(top_w, axis=-1, keepdims=True)
        combine = jnp.zeros((N, E), dtype=x.dtype)
        combine = combine.at[jnp.arange(N)[:, None], top_i].add(top_w)
        g = jnp.einsum('nd,ehd->neh', xf, w_gate)
        u = jnp.einsum('nd,ehd->neh', xf, w_up)
        h = jax.nn.silu(g) * u
        y = jnp.einsum('neh,edh->ned', h, w_down)
        out = jnp.einsum('ned,ne->nd', y, combine)
        return out.reshape(Bb, Tt, D)
    x = x + _L0_ffn_ref(_L0_cond_ref(x, cond_512, L0_cond_k_aff_w, L0_cond_k_aff_b, L0_cond_k_w, L0_cond_k_b, L0_cond_o_aff_w, L0_cond_o_aff_b, L0_cond_o_w, L0_cond_o_b), L0_ffn_sim_matrix, L0_ffn_gates, L0_ffn_q_proj, L0_ffn_k_proj, L0_ffn_v_proj, L0_ffn_o_proj)
    x = x + _L1_ffn_ref(_L1_cond_ref(x, itok_BxS_0_999, itok_BxS_0_4, itok_BxS_0_4, mask_BxS_ik0, cond_512, cond_64, fside_Bx32_0, L1_cond_pw_g, L1_cond_pw_b, L1_cond_cp_g, L1_cond_cp_b, L1_cond_tm_g, L1_cond_tm_b, L1_cond_ms_g, L1_cond_ms_b, L1_cond_mem_W1, L1_cond_mem_b1, L1_cond_mem_W2, L1_cond_mem_b2, L1_cond_mem_g, L1_cond_mem_be, L1_cond_noi_W1, L1_cond_noi_b1, L1_cond_noi_W2, L1_cond_noi_b2, L1_cond_noi_g, L1_cond_noi_be, L1_cond_res_W1, L1_cond_res_b1, L1_cond_res_W2, L1_cond_res_b2, L1_cond_res_g, L1_cond_res_be, L1_cond_int_W1, L1_cond_int_b1, L1_cond_int_W2, L1_cond_int_b2, L1_cond_int_g, L1_cond_int_be, L1_cond_aw), L1_ffn_router_w, L1_ffn_w_gate, L1_ffn_w_up, L1_ffn_w_down)
    return x

_drawn_inputs = setup_inputs


def setup_inputs(seed=0):
    import zlib

    import numpy as np

    out = dict(_drawn_inputs(seed))
    spreads = {'L0_cond_k_aff_b': (1.0, 0.2),
     'L0_cond_k_b': (0.0, 0.1),
     'L0_cond_o_aff_b': (1.0, 0.2),
     'L0_cond_o_b': (0.0, 0.1),
     'L0_ffn_gates': (0.0, 0.1),
     'L1_cond_mem_b1': (0.0, 0.764),
     'L1_cond_mem_b2': (0.0, 0.1),
     'L1_cond_mem_be': (0.0, 0.584),
     'L1_cond_noi_b1': (0.0, 0.8),
     'L1_cond_noi_b2': (0.0, 0.1),
     'L1_cond_noi_be': (0.0, 1.474),
     'L1_cond_res_b1': (0.0, 0.407),
     'L1_cond_res_b2': (0.0, 0.1),
     'L1_cond_res_be': (0.0, 0.707),
     'L1_cond_int_b1': (0.0, 0.1),
     'L1_cond_int_b2': (0.0, 0.1),
     'L1_cond_int_be': (0.0, 0.1),
     'L1_cond_aw': (0.1666666716337204, 0.6)}
    factors = {'cond_64': 3.553,
     'fside_Bx32_0': 4.065,
     'L0_ffn_q_proj': 4.353,
     'L0_ffn_k_proj': 4.428,
     'L1_cond_pw_g': 30.62,
     'L1_cond_pw_b': 28.799,
     'L1_cond_cp_g': 31.352,
     'L1_cond_cp_b': 31.268,
     'L1_cond_tm_g': 25.642,
     'L1_cond_tm_b': 31.232,
     'L1_cond_ms_g': 36.224,
     'L1_cond_ms_b': 23.876,
     'L1_cond_mem_W1': 2.672,
     'L1_cond_mem_g': 29.897,
     'L1_cond_noi_W1': 2.989,
     'L1_cond_noi_g': 27.276,
     'L1_cond_res_W1': 4.383,
     'L1_cond_res_W2': 2.959,
     'L1_cond_res_g': 28.494}
    for name, (base, spread) in spreads.items():
        noise = np.random.default_rng([zlib.crc32(name.encode()), seed]).standard_normal(out[name].shape)
        drawn = base * np.exp(spread * noise) if base else spread * noise
        out[name] = jnp.asarray(drawn.astype(out[name].dtype))
    for name, factor in factors.items():
        out[name] = (out[name] * factor).astype(out[name].dtype)
    return out
```

```python
from contextlib import ExitStack

import concourse.bass as bass
from concourse import mybir

F32 = mybir.dt.float32
F32R = mybir.dt.float32r
I32 = mybir.dt.int32
U32 = mybir.dt.uint32
ALU = mybir.AluOpType
ACT = mybir.ActivationFunctionType
AX = mybir.AxisListType.X

P = 128
NBATCH = 32
NTOK = NBATCH * P
TILES = 4
BLK = TILES * P
NBLK = NTOK // BLK
HEADS = 16
HD = P // HEADS
E0 = 16
E1 = 8
HID = 256
CH1 = E1 * HID // P
LO = 32
RSQRT_SEED = 0x5F3759DF


class Stream:

    def __init__(self, sem):
        self.sem, self.count, self.queue = sem, 0, []

    def do(self, call, *after, signal=True):
        self.queue.append((after, call, signal))
        if signal:
            self.count += 1
            return (self.sem, self.count)
        return None

    def mark(self):
        return (self.sem, self.count)

    def dma(self, call, sem_mark, *after):
        self.queue.append((after, call, sem_mark[0]))
        return sem_mark

    def play(self, eng):
        reached = {}
        for after, call, signal in self.queue:
            for m in after:
                if m is not None and m[1] > reached.get(id(m[0]), 0):
                    eng.wait_ge(m[0], m[1])
                    reached[id(m[0])] = m[1]
            if call is None:
                continue
            ins = call(eng)
            if signal is True:
                ins.then_inc(self.sem, 1)
            elif signal is not False:
                ins.then_inc(signal, 16)


class Place:

    def __init__(self, ap):
        self.ap, self.free = ap, ()

    def __getitem__(self, key):
        return self.ap[key]


def view(ap, offset, dims):
    return bass.AP(ap.tensor, ap.offset + offset, [list(ap.ap[0])] + dims)


def interleave(*streams):
    steps = [[g, n, 0] for g, n in streams]
    while steps:
        s = min(steps, key=lambda s: (s[2] + 0.5) / s[1])
        s[2] += 1
        if next(s[0], "end") == "end":
            steps.remove(s)


def build_program(nc, ins, out):
    ctx = ExitStack()
    with ctx:
        stack = [ctx]
        layer = [""]

        def sb(name, shape, dt=F32):
            return Place(stack[-1].enter_context(nc.sbuf_tensor(layer[0] + name, shape, dt))[:])

        nsem = [0]

        def semaphore(name):
            nsem[0] += 1
            return ctx.enter_context(nc.semaphore(name))

        banks = [Place(ctx.enter_context(nc.psum_tensor(f"bank{i}", [P, 512], F32))[:]) for i in range(8)]

        PE = Stream(semaphore("pe_done"))
        DVE = Stream(semaphore("dve_done"))
        ACTE = Stream(semaphore("act_done"))
        POOL = Stream(semaphore("pool_done"))
        SP = Stream(semaphore("sp_done"))

        def load(name, dst, src, *after):
            return SP.dma(lambda e: e.dma_start(dst, src), (semaphore("ld_" + name), 16), *after)

        def mm(dst, lhsT, rhs, *after, start=True, stop=True, signal=True):
            return PE.do(lambda e: e.matmul(dst, lhsT, rhs, start=start, stop=stop), *after, signal=signal)

        def tt(S, dst, a, b, op, *after):
            return S.do(lambda e: e.tensor_tensor(dst, a, b, op), *after)

        def ts(S, dst, a, s1, op0, *after, s2=None, op1=None):
            if op1 is None:
                return S.do(lambda e: e.tensor_scalar(dst, a, s1, None, op0), *after)
            return S.do(lambda e: e.tensor_scalar(dst, a, s1, s2, op0, op1), *after)

        def act(dst, a, func, *after, bias=0.0, scale=1.0, accum=None):
            if accum is None:
                return ACTE.do(lambda e: e.activation(dst, a, func, bias=bias, scale=scale), *after)
            return ACTE.do(lambda e: e.activation(dst, a, func, bias=bias, scale=scale, accum_out=accum), *after)

        def reduce(dst, a, op, *after):
            return DVE.do(lambda e: e.tensor_reduce(dst, a, AX, op), *after)

        def dup(n, name, shape, dt=F32):
            return [sb(f"{name}{i}", shape, dt) for i in range(n)]

        const = sb("const", [P, 272])
        ident, ones, iota = const[:, 0:128], const[:, 128:256], const[:, 256:272]
        sel_raw = sb("sel_raw", [LO + E0, E0])
        sel = sb("sel", [LO + E0, E0, P], F32R)
        x1 = sb("x1", [P, NBATCH, P])
        p0 = sb("p0", [P, 298])
        aw = sb("aw", [P, 6])
        gu_raw = sb("gu_raw", [P, 2, CH1, P])
        p1 = sb("p1", [P, 1833])
        tabs_raw = sb("tabs_raw", [LO + 8, 3, P])
        idval = sb("idval", [LO + 8, 1])
        tok_ids = sb("tok_ids", [P, NBATCH], I32)

        scope_a = ctx.enter_context(ExitStack())
        stack.append(scope_a)
        layer[0] = "l0_"
        p64 = sb("p64", [64, 288])

        ld_const = load("const", const.ap, ins["c_const"])
        ld_p64 = load("p64", p64.ap, ins["p64"])
        ld_p0 = load("p0", p0.ap, ins["p0"])
        xT = dup(2, "xT", [P, BLK])
        ld_x = [None] * NBLK

        def load_xT(b):
            dst = xT[b % 2]
            ld_x[b] = load(f"xT{b}", dst.ap, ins["xT"][:, b * BLK:(b + 1) * BLK], *dst.free)

        load_xT(0)
        ld_sel = load("sel", sel_raw.ap, ins["c_sel"])

        wqkv = [sb(f"wqkv{h}", [P, E0, 3, P], F32R) for h in ("hi", "lo")]
        wo = [sb(f"wo{h}", [P, E0, P], F32R) for h in ("hi", "lo")]
        av = stage = dup(2, "av", [P, 8 * HD * HEADS])

        kwT, owT = p0[:, 0:128], p0[:, 128:256]
        k_aff_b, k_b, o_aff_b, o_b = (p0[:, 256 + i:257 + i] for i in range(4))
        gates_rows, aw_rows, sim = p0[:, 260:276], p0[:, 276:282], p0[:, 282:298]

        style = sb("style", [P, 2, NBATCH])
        sq_w = sb("sq_w", [P, 2, P])
        sq_style = sb("sq_style", [P, 2, NBATCH])
        sq_sim = sb("sq_sim", [P, E0])
        norms = sb("norms", [P, 80])
        nrm_tmp = sb("nrm_tmp", [P, 3, 80])
        sn = sb("sn", [P, E0])
        sig_gates = sb("sig_gates", [P, 2, E0])
        aw_tmp = sb("aw_tmp", [P, 4, 6])

        def rsqrt(S, x, tmp, *after):
            half, a, y = tmp
            t = DVE.do(lambda e: e.tensor_scalar(a.bitcast(I32), x.bitcast(I32), 1, None,
                                                 ALU.logical_shift_right), *after)
            t = ts(DVE, y.bitcast(I32), a.bitcast(I32), -1.0, ALU.mult, t, s2=float(RSQRT_SEED), op1=ALU.add)
            h = ts(S, half, x, -0.5, ALU.mult, t)
            for step in range(3):
                t = tt(S, a, y, y, ALU.mult, t, h)
                t = tt(S, a, a, half, ALU.mult, t)
                t = ts(S, a, a, 1.5, ALU.add, t)
                t = tt(S, x if step == 2 else y, y, a, ALU.mult, t)
            return t

        setup_bank = banks[6]
        for i in range(2):
            t = mm(setup_bank[:, 32 * i:32 * i + 32], p64[:, 128 * i:128 * i + 128], p64[:, 256:288],
                   ld_p64, signal=i == 1)
        for i, b in enumerate((k_aff_b, o_aff_b)):
            t_style = ts(DVE, style[:, i, :], setup_bank[:, 32 * i:32 * i + 32], b, ALU.add, t, ld_p0)
        tt(DVE, sq_w[:, 0, :], kwT, kwT, ALU.mult, ld_p0)
        tt(DVE, sq_w[:, 1, :], owT, owT, ALU.mult)
        tt(DVE, sq_sim.ap, sim, sim, ALU.mult)
        t_sq = tt(DVE, sq_style.ap, style.ap, style.ap, ALU.mult, t_style)
        for i in range(2):
            mm(setup_bank[:, 64 + 32 * i:96 + 32 * i], sq_w[:, i, :], sq_style[:, i, :], t_sq, signal=False)
        t = mm(setup_bank[:, 128:144], ones, sq_sim.ap, ld_const)
        t1 = ts(DVE, norms[:, 0:64], setup_bank[:, 64:128], 1e-8, ALU.add, t)
        t2 = ts(DVE, norms[:, 64:80], setup_bank[:, 128:144], 1e-24, ALU.max, t)
        setup_bank.free = (t2,)
        t_norms = rsqrt(DVE, norms.ap, [nrm_tmp[:, i, :] for i in range(3)], t1, t2)
        demod = [norms[:, 0:32], norms[:, 32:64]]
        t_sn = tt(DVE, sn.ap, sim, norms[:, 64:80], ALU.mult, t_norms)
        t = act(sig_gates[:, 1, :], gates_rows, ACT.Tanh, ld_p0, scale=0.5)
        t_sig = ts(DVE, sig_gates[:, 0, :], sig_gates[:, 1, :], 0.5, ALU.mult, t, s2=0.5, op1=ALU.add)
        t = reduce(aw_tmp[:, 0, 0:1], aw_rows, ALU.max, ld_p0)
        t = ts(DVE, aw_tmp[:, 1, :], aw_rows, aw_tmp[:, 0, 0:1], ALU.subtract, t)
        t = act(aw_tmp[:, 2, :], aw_tmp[:, 1, :], ACT.Exp, t, accum=aw_tmp[:, 3, 0:1])
        t = DVE.do(lambda e: e.reciprocal(aw_tmp[:, 3, 1:2], aw_tmp[:, 3, 0:1]), t)
        t_aw = ts(DVE, aw.ap, aw_tmp[:, 2, :], aw_tmp[:, 3, 1:2], ALU.mult, t)
        t_sel = DVE.do(lambda e: e.tensor_copy(
            sel.ap, sel_raw[:, :].unsqueeze(2).broadcast_to([LO + E0, E0, P])), ld_sel)

        xsT = sb("xsT", [P, BLK])
        kT = sb("kT", [P, BLK])
        kk = sb("kk", [P, TILES, 2 * P])
        prod = sb("prod", [P, 9, P])
        dbl = sb("dbl", [P, TILES, 7, 32])
        sc = sb("sc", [P, TILES, HEADS, HEADS])
        mx = sb("mx", [P, TILES, HEADS])
        den = sb("den", [P, TILES, HEADS])
        osum = sb("osum", [P, TILES, P])
        oT = sb("oT", [P, BLK])
        x0T = dup(2, "x0T", [P, BLK])
        x0sq = sb("x0sq", [P, BLK])
        lg = sb("lg", [P, TILES, E0 + 1])
        rt = sb("rt", [P, TILES, 8, E0])
        rs = sb("rs", [P, 8, TILES])
        top = sb("top", [P, TILES, 8])
        topi = sb("topi", [P, TILES, 8], U32)
        whl = dup(2, "whl", [P, TILES, LO + E0])
        w_tok = dup(3, "w_tok", [P, TILES, E0])
        wT = dup(2, "wT", [LO + E0, BLK], F32R)
        ready_x0T = [None] * NBLK
        ready_w = [None] * NBLK
        ready_wT = [None] * NBLK
        t_whl0 = [POOL.do(lambda e, w=w: e.memset(w.ap, 0.0)) for w in whl]

        def bc(ap, n):
            return ap.unsqueeze(2).broadcast_to([P, TILES, n])

        def across(ap, n):
            return ap.unsqueeze(1).broadcast_to([P, TILES, n])

        def head_attention(b):
            s1 = banks[7]
            src = xT[b % 2]
            for j in range(TILES):
                col = TILES * b + j
                t = act(xsT[:, j * P:(j + 1) * P], src[:, j * P:(j + 1) * P], ACT.Copy, ld_x[b], t_style,
                        *xsT.free, scale=style[:, 0, col:col + 1])
            src.free = (t,)
            if b + 1 < NBLK:
                load_xT(b + 1)
            yield
            t = mm(s1.ap, kwT, xsT.ap, t, *s1.free)
            xsT.free = (t,)
            for j in range(TILES):
                col = TILES * b + j
                t = act(kT[:, j * P:(j + 1) * P], s1[:, j * P:(j + 1) * P], ACT.Identity, t, t_norms, *kT.free,
                        scale=demod[0][:, col:col + 1], bias=k_b)
            yield
            for j in range(TILES):
                t = PE.do(lambda e, j=j: e.transpose(s1[:, j * P:(j + 1) * P], kT[:, j * P:(j + 1) * P], ident),
                          t, ld_const, signal=j == TILES - 1) or t
            kT.free = (t,)
            s1v = s1[:, :].rearrange("p (t f) -> p t f", t=TILES)
            act(kk[:, :, 0:P], s1v, ACT.Copy, t, *kk.free)
            t_kk = act(kk[:, :, P:2 * P], s1v, ACT.Copy)
            s1.free = (t_kk,)
            yield
            t_sc = None
            for j in range(TILES):
                k0 = kk[:, j, 0:P]
                t = tt(DVE, prod.ap, view(k0, 0, [[0, 9], [1, P]]), view(k0, 0, [[HD, 9], [1, P]]), ALU.mult,
                       t_kk, *prod.free)
                yield
                t_sc = reduce(sc[:, j, 0:9, :], prod[:, :, :].rearrange("p r (h d) -> p r h d", d=HD), ALU.add,
                              t, *sc.free)
                prod.free = (t_sc,)
                yield
            act(dbl[:, :, :, 0:HEADS], sc[:, :, 1:8, :], ACT.Copy, t_sc, *dbl.free)
            t = act(dbl[:, :, :, HEADS:], sc[:, :, 1:8, :], ACT.Copy)
            yield
            t = ACTE.do(lambda e: e.activation(
                sc[:, :, 9:16, :], view(dbl.ap, 6 * 32 + 9, [[7 * 32, TILES], [-31, 7], [1, HEADS]]), ACT.Copy), t)
            dbl.free = (t,)
            yield
            t = reduce(mx.ap, sc[:, :, :, :].rearrange("p t s h -> p t h s"), ALU.max, t, *mx.free)
            yield
            t = tt(DVE, sc.ap, sc.ap, view(mx.ap, 0, [[HEADS, TILES], [0, HEADS], [1, HEADS]]), ALU.subtract, t)
            mx.free = (t,)
            yield
            t_e = act(sc.ap, sc.ap, ACT.Exp, t, scale=HD ** -0.5)
            t = reduce(den.ap, sc[:, :, :, :].rearrange("p t s h -> p t h s"), ALU.add, t_e, *den.free)
            yield
            t_den = DVE.do(lambda e: e.reciprocal(den.ap, den.ap), t)
            n = 0
            reads = None
            for j in range(TILES):
                for half in range(2):
                    q = av[n % 2]
                    n += 1
                    h0 = 8 * half
                    a = view(sc[:, j, 0, h0:h0 + 1], 0, [[1, 8], [0, HD], [HEADS, HEADS]])
                    v = view(kk[:, j, HD * h0:HD * h0 + 1], 0, [[HD, 8], [1, HD], [HD, HEADS]])
                    q4 = q[:, :].rearrange("p (h d s) -> p h d s", h=8, d=HD)
                    t_q = tt(POOL, q4, a, v, ALU.mult, t_e, t_kk, *q.free)
                    yield
                    t = reduce(osum[:, j, HD * h0:HD * h0 + 64], q[:, :].rearrange("p (n s) -> p n s", s=HEADS),
                               ALU.add, t_q, *osum.free)
                    q.free = (t,)
            sc.free = (t_q, t)
            kk.free = (t_q,)
            yield
            on = osum[:, :, :].rearrange("p t (h d) -> p t h d", d=HD)
            t = tt(DVE, on, on, den[:, :, :].unsqueeze(3).broadcast_to([P, TILES, HEADS, HD]), ALU.mult, t, t_den)
            den.free = (t,)
            yield
            for j in range(TILES):
                t = PE.do(lambda e, j=j: e.transpose(s1[:, j * P:(j + 1) * P], osum[:, j, :], ident),
                          t, *s1.free, signal=j == TILES - 1) or t
            osum.free = (t,)
            for j in range(TILES):
                col = TILES * b + j
                t = act(oT[:, j * P:(j + 1) * P], s1[:, j * P:(j + 1) * P], ACT.Copy, t, *oT.free,
                        scale=style[:, 1, col:col + 1])
            yield
            t = mm(s1.ap, owT, oT.ap, t)
            oT.free = (t,)
            x0 = x0T[b % 2]
            for j in range(TILES):
                col = TILES * b + j
                t = act(x0[:, j * P:(j + 1) * P], s1[:, j * P:(j + 1) * P], ACT.Identity, t, *x0.free,
                        scale=demod[1][:, col:col + 1], bias=o_b)
            ready_x0T[b] = t
            yield
            t = act(x0sq.ap, x0.ap, ACT.Square, t, *x0sq.free)
            for j in range(TILES):
                mm(s1[:, 32 * j:32 * j + E0], x0[:, j * P:(j + 1) * P], sn.ap, t, t_sn, signal=False)
                t_l = mm(s1[:, 32 * j + E0:32 * j + E0 + 1], x0sq[:, j * P:(j + 1) * P], ones[:, 0:1], t,
                         signal=j == TILES - 1)
            x0sq.free = (t_l,)
            x0.free = (t_l,)
            t = DVE.do(lambda e: e.tensor_copy(
                lg.ap, s1[:, 0:128].rearrange("p (t n) -> p t n", t=TILES)[:, :, 0:E0 + 1]), t_l, *lg.free)
            s1.free = (t,)
            yield
            r = [rs[:, i, :] for i in range(8)]
            t = ts(DVE, r[0], lg[:, :, E0], 1e-24, ALU.max, t, *rs.free)
            yield
            half, a, y = r[1], r[2], r[3]
            t = DVE.do(lambda e: e.tensor_scalar(a.bitcast(I32), r[0].bitcast(I32), 1, None,
                                                 ALU.logical_shift_right), t)
            yield
            t = ts(DVE, y.bitcast(I32), a.bitcast(I32), -1.0, ALU.mult, t, s2=float(RSQRT_SEED), op1=ALU.add)
            yield
            t = ts(POOL, half, r[0], -0.5, ALU.mult, t)
            for step in range(3):
                t = tt(POOL, a, y, y, ALU.mult, t)
                t = tt(POOL, a, a, half, ALU.mult, t)
                t = ts(POOL, a, a, 1.5, ALU.add, t)
                t = tt(POOL, y, y, a, ALU.mult, t)
                yield
            R = [rt[:, :, i, :] for i in range(8)]
            t = tt(POOL, R[0], lg[:, :, 0:E0], bc(y, E0), ALU.mult, t, *rt.free)
            lg.free = (t,)
            t_log = tt(POOL, R[0], R[0], across(sig_gates[:, 0, :], E0), ALU.subtract, t, t_sig)
            yield
            for j in range(TILES):
                t_top = DVE.do(lambda e, j=j: e.max(top[:, j, :], R[0][:, j, :]), t_log, *top.free)
            yield
            t = t_top
            for j in range(TILES):
                t = DVE.do(lambda e, j=j: e.max_index(topi[:, j, :], top[:, j, :], R[0][:, j, :]), t_top)
            t = DVE.do(lambda e: e.tensor_copy(rs[:, 4:6, :], topi[:, :, 0:2].rearrange("p t k -> p k t")), t)
            yield
            t_i = ts(DVE, r[6], top[:, :, 0], 0.0, ALU.is_le, t_top)
            t_g = ts(DVE, r[7], top[:, :, 0], 0.0, ALU.max, t_top)
            top.free = (t_g, t)
            t_h = ts(DVE, R[3], R[0], 0.0, ALU.is_gt, t_log)
            t1 = tt(DVE, R[1], across(iota, E0), bc(r[4], E0), ALU.is_equal, t)
            t2 = tt(DVE, R[2], across(iota, E0), bc(r[5], E0), ALU.is_equal, t)
            yield
            t = tt(POOL, R[1], R[1], R[2], ALU.add, t1, t2)
            t = tt(POOL, R[1], R[1], bc(r[6], E0), ALU.mult, t, t_i)
            t_m = tt(POOL, R[1], R[1], R[3], ALU.add, t, t_h)
            t = ts(POOL, R[4], R[0], 0.0, ALU.max, t_log)
            t = tt(POOL, R[4], R[4], bc(r[7], E0), ALU.subtract, t, t_g)
            yield
            t = act(R[5], R[4], ACT.Exp, t)
            t = tt(POOL, R[5], R[5], R[1], ALU.mult, t, t_m)
            yield
            t = reduce(r[1], R[5], ALU.add, t)
            t = DVE.do(lambda e: e.reciprocal(r[2], r[1]), t)
            yield
            w = w_tok[b % 3]
            t = ready_w[b] = tt(POOL, w.ap, R[5], bc(r[2], E0), ALU.mult, t, *w.free)
            rt.free = rs.free = (t,)
            wp = whl[b % 2]
            t = ACTE.do(lambda e: e.activation(wp[:, :, 0:E0].bitcast(F32R), w.ap, ACT.Copy), t, t_whl0[b % 2],
                        *wp.free)
            t = tt(POOL, wp[:, :, LO:LO + E0], w.ap, wp[:, :, 0:E0], ALU.subtract, t)
            yield
            for j in range(TILES):
                t = PE.do(lambda e, j=j: e.transpose(s1[0:LO + E0, j * P:(j + 1) * P], wp[:, j, :], ident),
                          t, *s1.free, signal=j == TILES - 1) or t
            wp.free = (t,)
            wst = wT[b % 2]
            t = ready_wT[b] = act(wst.ap, s1[0:LO + E0, :], ACT.Copy, t, *wst.free)
            s1.free = (t,)
            yield

        z = dup(3, "z", [P, BLK])
        zh = dup(3, "zh", [P, BLK], F32R)
        zl = dup(3, "zl", [P, BLK], F32R)
        qkv_done = [None] * NBLK
        ready_expert = {}

        def scaled_split(n, src, weightsT, e, bank, *after):
            zi, hi, lo = z[n % 3], zh[n % 3], zl[n % 3]
            rows = weightsT.shape[0]
            t = mm(bank.ap, sel[0:rows, e, :], weightsT, *after, t_sel, *bank.free)
            t = tt(DVE, zi.ap, src, bank.ap, ALU.mult, t, *zi.free)
            bank.free = (t,)
            t_hi = act(hi.ap, zi.ap, ACT.Copy, t, *hi.free)
            t_lo = tt(POOL, lo.ap, zi.ap, hi[:, :].bitcast(F32), ALU.subtract, t_hi, *lo.free)
            zi.free = (t_lo,)
            return t, t_hi, t_lo

        count_z = [0]

        def project(b):
            x0, wst = x0T[b % 2], wT[b % 2]
            made = {}

            def produce(e):
                n = count_z[0]
                count_z[0] += 1
                made[e] = (n, scaled_split(n, x0.ap, wst.ap, e, banks[3 + n % 2], ready_x0T[b], ready_wT[b]))

            def consume(e):
                n, (_, t_hi, t_lo) = made[e]
                hi, lo = zh[n % 3], zl[n % 3]
                for i in range(3):
                    first = banks[i].free if e == 0 else ()
                    mm(banks[i].ap, wqkv[0][:, e, i, :], hi.ap, t_hi, ready_expert[e], *first,
                       start=e == 0, stop=False, signal=False)
                    mm(banks[i].ap, wqkv[1][:, e, i, :], hi.ap, start=False, stop=False, signal=False)
                for i in range(3):
                    t = mm(banks[i].ap, wqkv[0][:, e, i, :], lo.ap, t_lo, start=False, stop=e == E0 - 1,
                           signal=i == 2)
                hi.free = lo.free = (t,)
                return t

            for e in range(2):
                produce(e)
            yield
            for e in range(E0):
                if e + 2 < E0:
                    produce(e + 2)
                yield
                t = consume(e)
                yield
            x0.free = x0.free + (made[E0 - 1][1][0],)
            wst.free = (PE.mark(),)
            qkv_done[b] = t

        qT = dup(3, "qT", [P, BLK])
        pexp = sb("pexp", [P, TILES, P])
        pT = sb("pT", [P, BLK])
        v_tok = sb("v_tok", [P, TILES, P])
        ohl = [sb("oh", [P, BLK], F32R), sb("ol", [P, BLK], F32R)]
        sm = sb("sm", [P, 4, TILES])
        w_out = sb("w_out", [P, TILES, E0])
        ld_x1 = load("x1", x1.ap, ins["x_tok"])
        x1_done = [None] * NBLK

        def row_attention(b):
            at, ob = banks[6], banks[5]
            for i in range(3):
                t = act(qT[i].ap, banks[i].ap, ACT.Copy, qkv_done[b], *qT[i].free)
                banks[i].free = (t,)
            yield
            for j in range(TILES):
                c = slice(j * P, (j + 1) * P)
                t = mm(at[:, c], qT[0][:, c], qT[1][:, c], t, *at.free, signal=j == TILES - 1) or t
            qT[0].free = qT[1].free = (t,)
            av4 = at[:, :].rearrange("p (t s) -> p t s", t=TILES)
            yield
            t = reduce(sm[:, 0, :], av4, ALU.max, t, *sm.free)
            t = ts(DVE, sm[:, 1, :], sm[:, 0, :], -P ** -0.5, ALU.mult, t)
            yield
            for j in range(TILES):
                t = act(pexp[:, j, :], av4[:, j, :], ACT.Exp, t, *pexp.free, scale=P ** -0.5,
                        bias=sm[:, 1, j:j + 1], accum=sm[:, 2, j:j + 1])
            yield
            t1 = DVE.do(lambda e: e.reciprocal(sm[:, 3, :], sm[:, 2, :]), t)
            w = w_tok[b % 3]
            t_w = tt(DVE, w_out.ap, w.ap, bc(sm[:, 3, :], E0), ALU.mult, t1, ready_w[b], *w_out.free)
            w.free = sm.free = (t_w,)
            for j in range(TILES):
                t = PE.do(lambda e, j=j: e.transpose(at[:, j * P:(j + 1) * P], pexp[:, j, :], ident), t,
                          signal=j == TILES - 1) or t
            pexp.free = (t,)
            t = act(pT.ap, at.ap, ACT.Copy, t, *pT.free)
            yield
            for j in range(TILES):
                t = PE.do(lambda e, j=j: e.transpose(at[:, j * P:(j + 1) * P], qT[2][:, j * P:(j + 1) * P], ident), t,
                          signal=j == TILES - 1) or t
            qT[2].free = (t,)
            t = act(v_tok[:, :, :].rearrange("p t h -> p (t h)"), at.ap, ACT.Copy, t, *v_tok.free)
            yield
            for j in range(TILES):
                c = slice(j * P, (j + 1) * P)
                t = mm(at[:, c], v_tok[:, j, :], pT[:, c], t, signal=j == TILES - 1) or t
            pT.free = v_tok.free = (t,)
            t = act(ohl[0].ap, at.ap, ACT.Copy, t, *ohl[0].free)
            t = tt(DVE, ohl[1].ap, at.ap, ohl[0][:, :].bitcast(F32), ALU.subtract, t, *ohl[1].free)
            at.free = (t,)
            yield
            for j in range(TILES):
                acc = x1[:, TILES * b + j, :]
                c = slice(j * P, (j + 1) * P)
                t_acc = ld_x1
                for g in range(E0 // 4):
                    es = slice(4 * g, 4 * g + 4)
                    mm(ob.ap, ohl[0][:, c], wo[0][:, es, :], t, *ob.free, ready_expert["o"], start=True, stop=False,
                       signal=False)
                    mm(ob.ap, ohl[0][:, c], wo[1][:, es, :], start=False, stop=False, signal=False)
                    t_o = mm(ob.ap, ohl[1][:, c], wo[0][:, es, :], start=False, stop=True)
                    yield
                    for k in range(4):
                        ee = 4 * g + k
                        t_acc = DVE.do(lambda e, k=k, ee=ee, acc=acc, j=j: e.scalar_tensor_tensor(
                            out=acc, in0=ob[:, k * P:(k + 1) * P], scalar=w_out[:, j, ee:ee + 1], in1=acc,
                            op0=ALU.mult, op1=ALU.add), t_o, t_acc, t_w)
                    ob.free = (t_acc,)
            ohl[0].free = ohl[1].free = (t_o,)
            w_out.free = (t_acc,)
            x1_done[b] = t_acc

        def split_weights():
            n = 0
            for name, src, hl, cols in (("qkv", ins["w_qkv"], wqkv, E0 * 3 * P), ("o", ins["w_o"], wo, E0 * P)):
                flat = [h.ap.rearrange("p e i h -> p (e i h)") if name == "qkv" else
                        h.ap.rearrange("p e h -> p (e h)") for h in hl]
                step = 768 if name == "qkv" else 1024
                for c in range(0, cols, step):
                    s = stage[n % 2]
                    n += 1
                    t = load(f"{name}{c}", s[:, 0:step], src[:, c:c + step], *s.free)
                    t = act(flat[0][:, c:c + step], s[:, 0:step], ACT.Copy, t)
                    t = tt(DVE, flat[1][:, c:c + step], s[:, 0:step], flat[0][:, c:c + step].bitcast(F32),
                           ALU.subtract, t)
                    s.free = (t,)
                    if name == "qkv":
                        for e in range(c // (3 * P), (c + step) // (3 * P)):
                            ready_expert[e] = t
                    else:
                        ready_expert["o"] = t
                    yield

        ld_gu = load("gu", gu_raw.ap, ins["w_gu"])
        ld_p1 = load("p1", p1.ap, ins["p1"])
        ld_tabs = load("tabs", tabs_raw.ap, ins["tabs"])
        ld_idval = load("idval", idval.ap, ins["c_idval"])
        ld_tok = load("tok", tok_ids.ap, ins["tok_ids"])

        for i in range(NBLK + 2):
            streams = []
            if i < NBLK:
                streams.append((head_attention(i), 41))
            if i == 0:
                streams.append((split_weights(), 10))
            if 0 <= i - 1 < NBLK:
                streams.append((project(i - 1), 33))
            if 0 <= i - 2 < NBLK:
                streams.append((row_attention(i - 2), 24))
            interleave(*streams)

        everything = [s.mark() for s in (PE, DVE, ACTE, POOL)]
        for s in (PE, DVE, ACTE, POOL, SP):
            s.do(None, *everything, signal=False)
        scope_a.close()
        stack.pop()
        layer[0] = "l1_"
        for bk in banks:
            bk.free = ()

        wgu = [sb(f"wgu{h}", [P, 2, CH1, P], F32R) for h in ("hi", "lo")]
        wdn = [sb(f"wdn{h}", [P, CH1, P], F32R) for h in ("hi", "lo")]
        W1 = p1[:, 0:768].rearrange("p (k o) -> p k o", k=6)
        W2, routerT, b2_rows = p1[:, 768:896], p1[:, 896:904], p1[:, 904:1032]
        mlp_W2 = [p1[:, 1032 + 128 * i:1160 + 128 * i] for i in range(3)]
        mlp_b2 = [p1[0:NBATCH, 1416 + 128 * i:1544 + 128 * i] for i in range(3)]
        col = {n: p1[:, 1800 + i:1801 + i] for i, n in enumerate(
            ("int_b1", "int_g", "int_be", "b1_0", "b1_1", "b1_2", "g_0", "be_0", "g_1", "be_1", "g_2", "be_2"))}
        cp_bT, tm_bT, ms_bT = p1[:, 1812:1817], p1[:, 1817:1822], p1[:, 1822:1825]
        ms_col = p1[:, 1825:1833]

        dn_raw = sb("dn_raw", [P, CH1, P])
        pm64 = sb("pm64", [64, 320])
        pm32 = sb("pm32", [32, 160])
        ld_pm64 = load("pm64", pm64.ap, ins["pm64"])
        ld_pm32 = load("pm32", pm32.ap, ins["pm32"])
        ld_dn = load("dn", dn_raw.ap, ins["w_dn"])
        cond_in = [(pm64[:, 0:128], pm64[:, 256:288], ld_pm64), (pm64[:, 128:256], pm64[:, 288:320], ld_pm64),
                   (pm32[:, 0:128], pm32[:, 128:160], ld_pm32)]

        def halves(raw, hi, lo, t, S):
            t = act(hi, raw, ACT.Copy, t)
            return tt(S, lo, raw, hi.bitcast(F32), ALU.subtract, t)

        mlp_h = sb("mlp_h", [P, 3, NBATCH])
        mlp_o = sb("mlp_o", [NBATCH, 3, P])
        mlp_st = sb("mlp_st", [NBATCH, 3, 6])
        mlp_mv = sb("mlp_mv", [NBATCH, 3, 2])
        mlp_var = sb("mlp_var", [NBATCH, 4, 3])
        mlp_T = sb("mlp_T", [P, 3, NBATCH])
        W1w = sb("W1w", [P, 6, P])
        Wx = sb("Wx", [P, P])
        base = sb("base", [P, NBATCH])
        tabT = sb("tabT", [P, 3, LO + 8])
        tabs = [sb("tabs_hl", [LO + 8, 4, P], F32R), sb("tabs_tmp", [LO + 8, 4, P], F32R)]
        bias_raw = sb("bias_raw", [LO + 8, P])

        for k in range(6):
            t = ts(DVE, W1w[:, k, :], W1[:, k, :], aw[:, k:k + 1], ALU.mult, t_aw, ld_p1)
        t = tt(DVE, Wx.ap, W1w[:, 2, :], W1w[:, 3, :], ALU.add, t)
        t_W1 = tt(DVE, Wx.ap, Wx.ap, W1w[:, 4, :], ALU.add, t)
        sb_bank, sb2 = banks[6], banks[7]
        for i, (w, s, ld) in enumerate(cond_in):
            t = mm(sb_bank[:, 32 * i:32 * i + 32], w, s, ld, signal=i == 2)
        for i in range(3):
            t = act(mlp_h[:, i, :], sb_bank[:, 32 * i:32 * i + 32], ACT.Silu, t, ld_p1, bias=col[f"b1_{i}"])
        for i in range(3):
            t = mm(sb_bank[0:NBATCH, 128 * i:128 * i + 128], mlp_h[:, i, :], mlp_W2[i], t, signal=i == 2) or t
        for i in range(3):
            t = tt(DVE, mlp_o[:, i, :], sb_bank[0:NBATCH, 128 * i:128 * i + 128], mlp_b2[i], ALU.add, t)
        for i in range(3):
            t = DVE.do(lambda e, i=i: e.bn_stats(mlp_st[:, i, :], mlp_o[:, i, :]), t)
        for i in range(3):
            t = DVE.do(lambda e, i=i: e.bn_aggr(mlp_mv[:, i, :], mlp_st[:, i, :]), t)
        t = ts(DVE, mlp_var[:, 0, :], mlp_mv[:, :, 1], 1e-5, ALU.add, t)
        t = rsqrt(DVE, mlp_var[:, 0, :], [mlp_var[:, 1 + i, :] for i in range(3)], t)
        for i in range(3):
            t = ts(DVE, mlp_o[:, i, :], mlp_o[:, i, :], mlp_mv[:, i, 0:1], ALU.subtract, t,
                   s2=mlp_var[:, 0, i:i + 1], op1=ALU.mult)
        for i in range(3):
            t = PE.do(lambda e, i=i: e.transpose(sb_bank[:, 32 * i:32 * i + 32], mlp_o[:, i, :],
                                                 ident[0:NBATCH, 0:NBATCH]), t, signal=i == 2) or t
        for i in range(3):
            t = act(mlp_T[:, i, :], sb_bank[:, 32 * i:32 * i + 32], ACT.Identity, t, scale=col[f"g_{i}"],
                    bias=col[f"be_{i}"])
        for i in range(3):
            t = mm(sb_bank[:, 0:NBATCH], W1w[:, 2 + i, :], mlp_T[:, i, :], t, t_W1, start=i == 0, stop=i == 2,
                   signal=i == 2) or t
        t_base = ts(DVE, base.ap, sb_bank[:, 0:NBATCH], col["int_b1"], ALU.add, t)
        sb_bank.free = (t_base,)
        t = POOL.do(lambda e: e.memset(tabT.ap, 0.0))
        for k, (src, at, n) in enumerate(((cp_bT, 0, 5), (tm_bT, 0, 5), (ms_bT, 5, 3))):
            for o in (0, LO):
                t = DVE.do(lambda e, k=k, src=src, at=at, n=n, o=o: e.tensor_copy(
                    tabT[:, k, o + at:o + at + n], src), t, ld_p1)
        for k, i in enumerate((0, 1, 5)):
            t = mm(sb2[0:LO + 8, 0:P], tabT[:, k, :], W1w[:, i, :], t, t_W1, start=k == 0, stop=k == 2,
                   signal=k == 2) or t
        t = DVE.do(lambda e: e.tensor_copy(bias_raw.ap, sb2[0:LO + 8, 0:P]), t)
        sb2.free = (t,)
        raws = [tabs_raw[:, k, :] for k in range(3)] + [bias_raw.ap]
        t_hi = t
        for k in range(4):
            t_hi = DVE.do(lambda e, k=k: e.tensor_copy(tabs[0][:, k, :], raws[k]), t, ld_tabs)
        for k in range(4):
            t1 = DVE.do(lambda e, k=k: e.tensor_copy(tabs[1][:, k, :], raws[k]), t_hi)
        for k in range(4):
            t_tabs = tt(DVE, tabs[0][LO:LO + 8, k, :], raws[k][LO:LO + 8, :],
                        tabs[1][LO:LO + 8, k, :].bitcast(F32), ALU.subtract, t1)
        t_gu = {}
        for g in range(4):
            for i in range(2):
                c = slice(4 * g, 4 * g + 4)
                t_gu[g, i] = halves(gu_raw[:, i, c, :], wgu[0][:, i, c, :], wgu[1][:, i, c, :], ld_gu,
                                    POOL if i else DVE)
        t_dn = halves(dn_raw[:, 0:8, :], wdn[0][:, 0:8, :], wdn[1][:, 0:8, :], ld_dn, DVE)
        t_dn2 = halves(dn_raw[:, 8:16, :], wdn[0][:, 8:16, :], wdn[1][:, 8:16, :], ld_dn, POOL)

        ids = dup(2, "ids", [LO + 8, BLK], I32)
        onehot = sb("onehot", [LO + 8, BLK], F32R)
        pw = dup(2, "pw", [P, TILES, 2 * P])
        st = sb("st", [P, TILES, 6])
        mv = sb("mv", [P, TILES, 2])
        nr = sb("nr", [P, 4, TILES])
        z1 = sb("z1", [P, TILES, P])
        z2 = sb("z2", [P, TILES, P])
        fT = dup(3, "fT", [P, BLK])
        gT = dup(3, "gT", [P, BLK])
        s1T = sb("s1T", [P, BLK])
        h2 = sb("h2", [P, TILES, P])
        yT = dup(2, "yT", [P, BLK])
        yh = dup(2, "yh", [P, BLK], F32R)
        yl = dup(2, "yl", [P, BLK], F32R)
        rl = sb("rl", [P, TILES, E1])
        top1 = sb("top1", [P, TILES, 8])
        topi1 = sb("topi1", [P, TILES, 8], U32)
        r1 = sb("r1", [P, 6, TILES])
        R1 = sb("R1", [P, TILES, 3, E1])
        chl = sb("chl", [P, TILES, LO + E1])
        cT = dup(2, "cT", [LO + E1, BLK], F32R)
        z = dup(3, "zb", [P, BLK])
        zh = dup(3, "zbh", [P, BLK], F32R)
        zl = dup(3, "zbl", [P, BLK], F32R)
        ready_y = [None] * NBLK
        ready_yl = [None] * NBLK
        ready_cT = [None] * NBLK
        t_chl0 = POOL.do(lambda e: e.memset(chl.ap, 0.0))
        ld_ids, ld_pw = [None] * NBLK, [None] * NBLK

        def fetch(b):
            if b >= NBLK:
                return
            ld_ids[b] = load(f"ids{b}", ids[b % 2].ap, ins["ids"][:, b * BLK:(b + 1) * BLK], *ids[b % 2].free)
            s = semaphore(f"ld_pw{b}")
            for j in range(TILES):
                c = TILES * b + j
                ld_pw[b] = POOL.dma(lambda e, j=j, c=c: e.indirect_dma_start(
                    pw[b % 2][:, j, :], None, ins["pw"],
                    bass.IndirectOffsetOnAxis(ap=tok_ids[:, c:c + 1].bitcast(U32), axis=0)),
                    (s, 16 * (j + 1)), ld_tok, *pw[b % 2].free)

        def norm(src, dst, t, *free):
            for j in range(TILES):
                t1 = DVE.do(lambda e, j=j: e.bn_stats(st[:, j, :], src[:, j, :]), t, *st.free)
            yield
            for j in range(TILES):
                t1 = DVE.do(lambda e, j=j: e.bn_aggr(mv[:, j, :], st[:, j, :]), t1, *mv.free)
            yield
            v, half, a, y = (nr[:, i, :] for i in range(4))
            t1 = ts(DVE, v, mv[:, :, 1], 1e-5, ALU.add, t1)
            yield
            t1 = DVE.do(lambda e: e.tensor_scalar(a.bitcast(I32), v.bitcast(I32), 1, None,
                                                  ALU.logical_shift_right), t1)
            yield
            t1 = ts(DVE, y.bitcast(I32), a.bitcast(I32), -1.0, ALU.mult, t1, s2=float(RSQRT_SEED), op1=ALU.add)
            t1 = ts(POOL, half, v, -0.5, ALU.mult, t1)
            yield
            for _ in range(3):
                t1 = tt(POOL, a, y, y, ALU.mult, t1)
                t1 = tt(POOL, a, a, half, ALU.mult, t1)
                t1 = ts(POOL, a, a, 1.5, ALU.add, t1)
                t1 = tt(POOL, y, y, a, ALU.mult, t1)
                yield
            for j in range(TILES):
                t2 = ts(DVE, dst[:, j, :], src[:, j, :], mv[:, j, 0:1], ALU.subtract, t1, *free,
                        s2=nr[:, 3, j:j + 1], op1=ALU.mult)
            st.free = mv.free = nr.free = (t2,)
            yield
            return t2

        def transposed(bank, src, t):
            for j in range(TILES):
                t = PE.do(lambda e, j=j: e.transpose(bank[:, j * P:(j + 1) * P], src[:, j, :], ident), t,
                          *bank.free, signal=j == TILES - 1) or t
            return t

        def condition(b):
            A, B = banks[6], banks[7]
            x = x1[:, TILES * b:TILES * (b + 1), :]
            t_z1 = yield from norm(x, z1, x1_done[b], *z1.free)
            g = pw[b % 2]
            t = tt(POOL, z2.ap, z1.ap, g[:, :, 0:P], ALU.mult, t_z1, ld_pw[b], *z2.free)
            t = tt(POOL, z2.ap, z2.ap, g[:, :, P:2 * P], ALU.add, t)
            g.free = (t,)
            t_oh = ts(DVE, onehot.ap, ids[b % 2].ap, idval[:, 0:1], ALU.is_equal, ld_ids[b], ld_idval, *onehot.free)
            ids[b % 2].free = (t_oh,)
            fetch(b + 1)
            yield
            t1 = transposed(A, z1, t_z1)
            t1 = act(fT[1].ap, A.ap, ACT.Copy, t1, *fT[1].free)
            A.free = (t1,)
            z1.free = (t, t1)
            yield
            t2 = transposed(B, x, x1_done[b])
            t2 = act(fT[2].ap, B.ap, ACT.Copy, t2, *fT[2].free)
            B.free = (t2,)
            yield
            for k, bank in ((1, A), (2, B)):
                tg = mm(bank.ap, tabs[0][:, k, :], onehot.ap, t_oh, t_tabs, *bank.free)
                tg = tt(DVE, gT[k].ap, fT[1].ap, bank.ap, ALU.mult, tg, t1, *gT[k].free)
                bank.free = (tg,)
                yield
            fT[1].free = (tg,)
            t_z2 = yield from norm(z2, z2, t)
            t = transposed(A, z2, t_z2)
            t = act(fT[0].ap, A.ap, ACT.Copy, t, *fT[0].free)
            A.free = (t,)
            z2.free = (t,)
            yield
            tg = mm(B.ap, tabs[0][:, 0, :], onehot.ap, *B.free)
            tg = tt(DVE, gT[0].ap, fT[0].ap, B.ap, ALU.mult, tg, t, *gT[0].free)
            fT[0].free = (tg,)
            B.free = (tg,)
            yield
            mm(A.ap, tabs[0][:, 3, :], onehot.ap, *A.free, start=True, stop=False, signal=False)
            mm(A.ap, Wx.ap, fT[2].ap, t2, t_W1, start=False, stop=False, signal=False)
            mm(A.ap, W1w[:, 1, :], gT[1].ap, tg, start=False, stop=False, signal=False)
            mm(A.ap, W1w[:, 5, :], gT[2].ap, start=False, stop=False, signal=False)
            yield
            t = mm(A.ap, W1w[:, 0, :], gT[0].ap, tg, start=False, stop=True)
            onehot.free = fT[2].free = (t,)
            for k in range(3):
                gT[k].free = (t,)
            for j in range(TILES):
                c = TILES * b + j
                t = act(s1T[:, j * P:(j + 1) * P], A[:, j * P:(j + 1) * P], ACT.Silu, t, t_base, *s1T.free,
                        bias=base[:, c:c + 1])
            A.free = (t,)
            yield
            for j in range(TILES):
                t = mm(B[:, j * P:(j + 1) * P], s1T[:, j * P:(j + 1) * P], W2, t, *B.free,
                       signal=j == TILES - 1) or t
            s1T.free = (t,)
            yield
            t = tt(DVE, h2.ap, B[:, :].rearrange("p (t f) -> p t f", t=TILES), across(b2_rows, P), ALU.add, t,
                   *h2.free)
            B.free = (t,)
            t = yield from norm(h2, h2, t)
            t = transposed(A, h2, t)
            h2.free = (t,)
            y = yT[b % 2]
            t = act(y.ap, A.ap, ACT.Identity, t, *y.free, scale=col["int_g"], bias=col["int_be"])
            A.free = (t,)
            ready_y[b] = t
            t_h = act(yh[b % 2].ap, y.ap, ACT.Copy, t, *yh[b % 2].free)
            ready_yl[b] = tt(POOL, yl[b % 2].ap, y.ap, yh[b % 2][:, :].bitcast(F32), ALU.subtract, t_h,
                             *yl[b % 2].free)
            yield
            for j in range(TILES):
                t = mm(B[:, E1 * j:E1 * (j + 1)], y[:, j * P:(j + 1) * P], routerT, t, *B.free,
                       signal=j == TILES - 1) or t
            t = DVE.do(lambda e: e.tensor_copy(rl.ap, B[:, 0:TILES * E1].rearrange("p (t n) -> p t n", t=TILES)),
                       t, *rl.free)
            B.free = (t,)
            yield
            for j in range(TILES):
                t_top = DVE.do(lambda e, j=j: e.max(top1[:, j, :], rl[:, j, :]), t, *top1.free)
            yield
            for j in range(TILES):
                t = DVE.do(lambda e, j=j: e.max_index(topi1[:, j, :], top1[:, j, :], rl[:, j, :]), t_top)
            t = DVE.do(lambda e: e.tensor_copy(r1[:, 0:2, :], topi1[:, :, 0:2].rearrange("p t k -> p k t")), t,
                       *r1.free)
            rl.free = (t,)
            t_d = tt(DVE, r1[:, 2, :], top1[:, :, 0], top1[:, :, 1], ALU.subtract, t_top)
            top1.free = (t_d,)
            yield
            t_d = act(r1[:, 3, :], r1[:, 2, :], ACT.Tanh, t_d, scale=0.5)
            t1 = ts(DVE, r1[:, 4, :], r1[:, 3, :], 0.5, ALU.mult, t_d, s2=0.5, op1=ALU.add)
            t2 = ts(DVE, r1[:, 5, :], r1[:, 3, :], -0.5, ALU.mult, t_d, s2=0.5, op1=ALU.add)
            i8 = across(iota[:, 0:E1], E1)
            t3 = tt(DVE, R1[:, :, 0, :], i8, bc(r1[:, 0, :], E1), ALU.is_equal, t, *R1.free)
            t4 = tt(DVE, R1[:, :, 1, :], i8, bc(r1[:, 1, :], E1), ALU.is_equal, t)
            yield
            t = tt(POOL, R1[:, :, 0, :], R1[:, :, 0, :], bc(r1[:, 4, :], E1), ALU.mult, t1, t3)
            t5 = tt(POOL, R1[:, :, 1, :], R1[:, :, 1, :], bc(r1[:, 5, :], E1), ALU.mult, t2, t4)
            t = tt(POOL, R1[:, :, 2, :], R1[:, :, 0, :], R1[:, :, 1, :], ALU.add, t, t5)
            r1.free = (t,)
            t = act(chl[:, :, 0:E1].bitcast(F32R), R1[:, :, 2, :], ACT.Copy, t, t_chl0, *chl.free)
            t = tt(POOL, chl[:, :, LO:LO + E1], R1[:, :, 2, :], chl[:, :, 0:E1], ALU.subtract, t)
            R1.free = (t,)
            yield
            for j in range(TILES):
                t = PE.do(lambda e, j=j: e.transpose(A[0:LO + E1, j * P:(j + 1) * P], chl[:, j, :], ident), t,
                          *A.free, signal=j == TILES - 1) or t
            chl.free = (t,)
            c = cT[b % 2]
            ready_cT[b] = t = act(c.ap, A[0:LO + E1, :], ACT.Copy, t, *c.free)
            A.free = (t,)
            yield

        sg = dup(2, "sg", [P, BLK])
        hp = dup(2, "hp", [P, BLK])
        hh = dup(2, "hh", [P, BLK], F32R)
        hl = dup(2, "hl", [P, BLK], F32R)
        ffT = sb("ffT", [P, BLK])
        s_out = semaphore("out_written")

        def experts(b):
            y, yhi, ylo, c = yT[b % 2], yh[b % 2], yl[b % 2], cT[b % 2]
            made, hidden = {}, {}
            dn = banks[5]

            def produce(e):
                n = count_z[0]
                count_z[0] += 1
                made[e] = (n, scaled_split_1(n, y.ap, c.ap, e))

            def scaled_split_1(n, src, weightsT, e):
                bank = banks[4]
                zi, hi, lo = z[n % 3], zh[n % 3], zl[n % 3]
                t = mm(bank.ap, sel[0:LO + E1, e, :], weightsT, ready_cT[b], *bank.free)
                t = tt(DVE, zi.ap, src, bank.ap, ALU.mult, t, ready_y[b], *zi.free)
                bank.free = (t,)
                t_hi = act(hi.ap, zi.ap, ACT.Copy, t, *hi.free)
                t_lo = tt(POOL, lo.ap, zi.ap, hi[:, :].bitcast(F32), ALU.subtract, t_hi, *lo.free)
                zi.free = (t_lo,)
                return t, t_hi, t_lo

            def up(j):
                e = j // 2
                n, (_, t_hi, t_lo) = made[e]
                g, u = banks[j % 2], banks[2 + j % 2]
                mm(g.ap, wgu[0][:, 0, j, :], yhi.ap, ready_yl[b], t_gu[j // 4, 0], *g.free, start=True, stop=False,
                   signal=False)
                mm(g.ap, wgu[1][:, 0, j, :], yhi.ap, start=False, stop=False, signal=False)
                t_g = mm(g.ap, wgu[0][:, 0, j, :], ylo.ap, start=False, stop=True)
                mm(u.ap, wgu[0][:, 1, j, :], zh[n % 3].ap, t_hi, t_gu[j // 4, 1], *u.free, start=True, stop=False,
                   signal=False)
                mm(u.ap, wgu[1][:, 1, j, :], zh[n % 3].ap, start=False, stop=False, signal=False)
                t_u = mm(u.ap, wgu[0][:, 1, j, :], zl[n % 3].ap, t_lo, start=False, stop=True)
                if j % 2:
                    zh[n % 3].free = zl[n % 3].free = (t_u,)
                s, h, hi, lo = sg[j % 2], hp[j % 2], hh[j % 2], hl[j % 2]
                t = act(s.ap, g.ap, ACT.Silu, t_g, *s.free)
                g.free = (t,)
                t = tt(DVE, h.ap, s.ap, u.ap, ALU.mult, t, t_u, *h.free)
                s.free = u.free = (t,)
                t_h = act(hi.ap, h.ap, ACT.Copy, t, *hi.free)
                t_l = tt(POOL, lo.ap, h.ap, hi[:, :].bitcast(F32), ALU.subtract, t_h, *lo.free)
                h.free = (t_l,)
                hidden[j] = (t_h, t_l)

            def down(j):
                t_h, t_l = hidden[j]
                hi, lo = hh[j % 2], hl[j % 2]
                first = dn.free if j == 0 else ()
                mm(dn.ap, wdn[0][:, j, :], hi.ap, t_h, t_dn, t_dn2, *first, start=j == 0, stop=False, signal=False)
                mm(dn.ap, wdn[1][:, j, :], hi.ap, start=False, stop=False, signal=False)
                t = mm(dn.ap, wdn[0][:, j, :], lo.ap, t_l, start=False, stop=j == CH1 - 1)
                hi.free = lo.free = (t,)
                return t

            produce(0)
            produce(1)
            yield
            for j in range(CH1):
                up(j)
                if j % 2 == 1 and j // 2 + 2 < E1:
                    produce(j // 2 + 2)
                yield
                if j >= 1:
                    t = down(j - 1)
                yield
            y.free = (made[E1 - 1][1][0],)
            yhi.free = ylo.free = c.free = (PE.mark(),)
            t = down(CH1 - 1)
            yield
            t = act(ffT.ap, dn.ap, ACT.Copy, t, *ffT.free)
            for j in range(TILES):
                t = PE.do(lambda e, j=j: e.transpose(dn[:, j * P:(j + 1) * P], ffT[:, j * P:(j + 1) * P], ident), t,
                          signal=j == TILES - 1) or t
            ffT.free = (t,)
            yield
            rows = slice(TILES * b, TILES * (b + 1))
            t = tt(DVE, x1[:, rows, :], x1[:, rows, :], dn[:, :].rearrange("p (t f) -> p t f", t=TILES), ALU.add, t)
            dn.free = (t,)
            SP.dma(lambda e: e.dma_start(out[rows, :, :].rearrange("b p d -> p b d"), x1[:, rows, :]),
                   (s_out, 16 * (b + 1)), t)
            yield

        fetch(0)
        for i in range(NBLK + 1):
            streams = []
            if i < NBLK:
                streams.append((condition(i), 51))
            if i >= 1:
                streams.append((experts(i - 1), 36))
            interleave(*streams)
        SP.do(None, (s_out, 16 * NBLK), signal=False)

        block = ctx.enter_context(nc.Block())

        @block.tensor
        def _(e):
            PE.play(e)

        @block.vector
        def _(e):
            DVE.play(e)

        @block.scalar
        def _(e):
            ACTE.play(e)

        @block.gpsimd
        def _(e):
            POOL.play(e)

        @block.sync
        def _(e):
            SP.play(e)


def layout(np, v):
    f = {k: np.asarray(a) for k, a in v.items()}
    cat = np.concatenate
    z = np.float32(0)

    def rows(a, n):
        return np.broadcast_to(a.reshape(1, -1), (n, a.size))

    def column(a):
        return a.reshape(-1, 1)

    x = f["x"]
    ins = {
        "xT": x.reshape(NTOK, P).T,
        "x_tok": x.transpose(1, 0, 2),
        "p64": cat([f["L0_cond_k_aff_w"].T, f["L0_cond_o_aff_w"].T, f["cond_512"].T], 1),
        "p0": cat([f["L0_cond_k_w"].T, f["L0_cond_o_w"].T, column(f["L0_cond_k_aff_b"]), column(f["L0_cond_k_b"]),
                   column(f["L0_cond_o_aff_b"]), column(f["L0_cond_o_b"]), rows(f["L0_ffn_gates"], P),
                   rows(f["L1_cond_aw"], P), f["L0_ffn_sim_matrix"]], 1),
        "w_qkv": np.stack([f["L0_ffn_q_proj"], f["L0_ffn_k_proj"], f["L0_ffn_v_proj"]], 1)
                   .transpose(2, 0, 1, 3).reshape(P, -1),
        "w_o": f["L0_ffn_o_proj"].transpose(1, 0, 2).reshape(P, -1),
        "w_gu": np.stack([f["L1_ffn_w_gate"].reshape(CH1, P, P), f["L1_ffn_w_up"].reshape(CH1, P, P)], 0)
                  .transpose(3, 0, 1, 2),
        "w_dn": f["L1_ffn_w_down"].reshape(E1, P, 2, P).transpose(3, 0, 2, 1).reshape(P, CH1, P),
    }
    pre = "L1_cond_"
    mlps = ("mem", "noi", "res")
    ins["p1"] = cat(
        [f[pre + "int_W1"].reshape(6, P, P).transpose(1, 0, 2).reshape(P, -1), f[pre + "int_W2"],
         f["L1_ffn_router_w"].T, rows(f[pre + "int_b2"], P)]
        + [f[pre + m + "_W2"] for m in mlps] + [rows(f[pre + m + "_b2"], P) for m in mlps]
        + [column(f[pre + n]) for n in ("int_b1", "int_g", "int_be", "mem_b1", "noi_b1", "res_b1", "mem_g", "mem_be",
                                        "noi_g", "noi_be", "res_g", "res_be")]
        + [f[pre + "cp_b"].T, f[pre + "tm_b"].T, f[pre + "ms_b"].T, np.zeros((P, 8), np.float32)], 1)
    tabs = np.zeros((LO + 8, 3, P), np.float32)
    ids = np.zeros((LO + 8, NTOK), f["itok_BxS_0_4"].dtype)
    for o in (0, LO):
        tabs[o:o + 5, 0], tabs[o:o + 5, 1], tabs[o + 5:o + 8, 2] = f[pre + "cp_g"], f[pre + "tm_g"], f[pre + "ms_g"]
        ids[o:o + 5], ids[o + 5:o + 8] = f["itok_BxS_0_4"].reshape(-1), f["mask_BxS_ik0"].reshape(-1)
    ins["tabs"], ins["ids"] = tabs, ids
    ins["pw"] = cat([f[pre + "pw_g"], f[pre + "pw_b"]], 1)
    ins["tok_ids"] = f["itok_BxS_0_999"].T
    ins["pm64"] = cat([f[pre + "mem_W1"], f[pre + "noi_W1"], f["cond_512"].T, f["cond_64"].T], 1)
    ins["pm32"] = cat([f[pre + "res_W1"], f["fside_Bx32_0"].T], 1)
    ins["c_const"] = cat([np.eye(P), np.ones((P, P)), np.broadcast_to(np.arange(16.0), (P, 16))], 1) \
        .astype(np.float32)
    sel = np.zeros((LO + E0, E0), np.float32)
    sel[np.arange(E0), np.arange(E0)] = sel[LO + np.arange(E0), np.arange(E0)] = 1
    val = np.full((LO + 8, 1), -1, np.float32)
    for o in (0, LO):
        val[o:o + 8, 0] = [0, 1, 2, 3, 4, 0, 1, 2]
    ins["c_sel"], ins["c_idval"] = sel, val
    return {k: np.ascontiguousarray(a) for k, a in ins.items()}


def kernel(**inputs):
    import numpy as np
    import concourse.bacc as bacc
    from concourse.bass_utils import run_bass_kernel_spmd

    nc = bacc.Bacc("TRN2", target_bir_lowering=False, num_devices=1)
    arrays = layout(np, inputs)
    ins = {k: nc.dram_tensor("in_" + k, a.shape, mybir.dt.from_np(a.dtype), kind="ExternalInput").ap()
           for k, a in arrays.items()}
    out = nc.dram_tensor("out_0", (NBATCH, P, P), F32, kind="ExternalOutput").ap()
    build_program(nc, ins, out)
    r = run_bass_kernel_spmd(nc, [{"in_" + k: a for k, a in arrays.items()}], core_ids=[0])
    return r.results[0]["out_0"]
```

```python
from contextlib import ExitStack

import concourse.bass as bass
from concourse import mybir

F32 = mybir.dt.float32
F32R = mybir.dt.float32r
I32 = mybir.dt.int32
U32 = mybir.dt.uint32
ALU = mybir.AluOpType
ACT = mybir.ActivationFunctionType
AX = mybir.AxisListType.X

P = 128
NBATCH = 32
NTOK = NBATCH * P
TILES = 4
BLK = TILES * P
NBLK = NTOK // BLK
HEADS = 16
HD = P // HEADS
E0 = 16
E1 = 8
HID = 256
CH1 = E1 * HID // P
LO = 32
RSQRT_SEED = 0x5F3759DF


class Stream:

    expected = {}
    latest = 0.0

    def __init__(self, sem, fixed=0.0, per=0.0):
        self.sem, self.count, self.queue = sem, 0, []
        self.fixed, self.per, self.clock = fixed, per, 0.0

    def do(self, call, *after, signal=True, n=16):
        self.queue.append((after, call, signal))
        begin = max([self.clock] + [Stream.expected.get(m, 0.0) + 0.06 for m in after if m is not None])
        self.clock = begin + self.fixed + self.per * n
        if signal:
            self.count += 1
            mark = (self.sem, self.count)
            Stream.expected[mark] = self.clock
            Stream.latest = max(Stream.latest, self.clock)
            return mark
        return None

    def mark(self):
        return (self.sem, self.count)

    def dma(self, call, sem_mark, *after):
        self.queue.append((after, call, sem_mark[0]))
        begin = max([self.clock] + [Stream.expected.get(m, 0.0) for m in after if m is not None])
        self.clock = begin + 0.1
        Stream.expected[sem_mark] = begin + 3.0
        return sem_mark

    def play(self, eng):
        reached = {}
        for after, call, signal in self.queue:
            for m in after:
                if m is not None and m[1] > reached.get(id(m[0]), 0):
                    eng.wait_ge(m[0], m[1])
                    reached[id(m[0])] = m[1]
            if call is None:
                continue
            ins = call(eng)
            if signal is True:
                ins.then_inc(self.sem, 1)
            elif signal is not False:
                ins.then_inc(signal, 16)


class Place:

    def __init__(self, ap):
        self.ap, self.free, self.held = ap, (), False

    def __getitem__(self, key):
        return self.ap[key]

    def grab(self):
        yield lambda: not self.held
        self.held = True

    def drop(self, *marks):
        self.free, self.held = marks, False


AHEAD = "ahead"


def view(ap, offset, dims):
    return bass.AP(ap.tensor, ap.offset + offset, [list(ap.ap[0])] + dims)


def weave(*emitters):
    waiting = [[g, 0.0, None] for g in emitters]
    while waiting:
        open_now = []
        for w in waiting:
            met = w[2]() if w[2] else True
            if met:
                if met is not True:
                    w[1] = max(w[1], Stream.expected.get(met, 0.0))
                w[2] = None
                open_now.append(w)
        w = min(open_now, key=lambda w: w[1])
        Stream.latest = w[1]
        said = next(w[0], "end")
        if said == "end":
            waiting.remove(w)
        elif isinstance(said, tuple):
            w[2] = said[1]
        else:
            w[1], w[2] = Stream.latest, said


def build_program(nc, ins, out):
    ctx = ExitStack()
    with ctx:
        stack = [ctx]
        layer = [""]

        def sb(name, shape, dt=F32):
            return Place(stack[-1].enter_context(nc.sbuf_tensor(layer[0] + name, shape, dt))[:])

        nsem = [0]

        def semaphore(name):
            nsem[0] += 1
            return ctx.enter_context(nc.semaphore(name))

        banks = [Place(ctx.enter_context(nc.psum_tensor(f"bank{i}", [P, 512], F32))[:]) for i in range(8)]

        PE = Stream(semaphore("pe_done"), 0.003, 0.00042)
        DVE = Stream(semaphore("dve_done"), 0.065, 0.00104)
        ACTE = Stream(semaphore("act_done"), 0.1, 0.00083)
        POOL = Stream(semaphore("pool_done"), 0.06, 0.00228)
        SP = Stream(semaphore("sp_done"))

        def load(name, dst, src, *after):
            return SP.dma(lambda e: e.dma_start(dst, src), (semaphore("ld_" + name), 16), *after)

        def size(ap):
            n = 1
            for _, count in list(ap.ap)[1:]:
                n *= count
            return n

        def mm(dst, lhsT, rhs, *after, start=True, stop=True, signal=True):
            return PE.do(lambda e: e.matmul(dst, lhsT, rhs, start=start, stop=stop), *after, signal=signal,
                         n=size(dst) * (1 if rhs.dtype == F32R else 4))

        def turn(dst, src, eye, *after, signal=True):
            return PE.do(lambda e: e.transpose(dst, src, eye), *after, signal=signal, n=128)

        def turn_tiles(bank, src, t, *after):
            for j in range(TILES):
                m = turn(bank[:, j * P:(j + 1) * P], src[j], ident, t, *after, signal=j == TILES - 1)
            return m

        def tt(S, dst, a, b, op, *after):
            return S.do(lambda e: e.tensor_tensor(dst, a, b, op), *after, n=size(dst))

        def ts(S, dst, a, s1, op0, *after, s2=None, op1=None):
            if op1 is None:
                return S.do(lambda e: e.tensor_scalar(dst, a, s1, None, op0), *after, n=size(dst))
            return S.do(lambda e: e.tensor_scalar(dst, a, s1, s2, op0, op1), *after, n=size(dst))

        def act(dst, a, func, *after, bias=0.0, scale=1.0, accum=None):
            if accum is None:
                return ACTE.do(lambda e: e.activation(dst, a, func, bias=bias, scale=scale), *after, n=size(dst))
            return ACTE.do(lambda e: e.activation(dst, a, func, bias=bias, scale=scale, accum_out=accum), *after,
                           n=size(dst) + 100)

        def reduce(dst, a, op, *after):
            return DVE.do(lambda e: e.tensor_reduce(dst, a, AX, op), *after, n=size(a))

        def lighter(n):
            return DVE if DVE.clock + DVE.per * n + DVE.fixed < POOL.clock + POOL.per * n + POOL.fixed else POOL

        def squares(ap):
            return [ap[:, j * P:(j + 1) * P] for j in range(TILES)]

        def rows_of(ap):
            return [ap[:, j, :] for j in range(TILES)]

        def dup(n, name, shape, dt=F32):
            return [sb(f"{name}{i}", shape, dt) for i in range(n)]

        const = sb("const", [P, 272])
        ident, ones, iota = const[:, 0:128], const[:, 128:256], const[:, 256:272]
        sel_raw = sb("sel_raw", [LO + E0, E0])
        sel = sb("sel", [LO + E0, E0, P], F32R)
        x1 = sb("x1", [P, NBATCH, P])
        p0 = sb("p0", [P, 298])
        aw = sb("aw", [P, 6])
        p1 = sb("p1", [P, 1833])
        tabs_raw = sb("tabs_raw", [LO + 8, 3, P])
        idval = sb("idval", [LO + 8, 1])
        tok_ids = sb("tok_ids", [P, NBATCH], I32)

        scope_a = ctx.enter_context(ExitStack())
        stack.append(scope_a)
        layer[0] = "l0_"
        p64 = sb("p64", [64, 288])

        ld_const = load("const", const.ap, ins["c_const"])
        ld_p64 = load("p64", p64.ap, ins["p64"])
        ld_p0 = load("p0", p0.ap, ins["p0"])
        xT = dup(2, "xT", [P, BLK])
        ld_x = [None] * NBLK

        def load_xT(b):
            dst = xT[b % 2]
            ld_x[b] = load(f"xT{b}", dst.ap, ins["xT"][:, b * BLK:(b + 1) * BLK], *dst.free)

        load_xT(0)
        ld_sel = load("sel", sel_raw.ap, ins["c_sel"])

        wqkv = [sb(f"wqkv{h}", [P, E0, 3, P], F32R) for h in ("hi", "lo")]
        wo = [sb(f"wo{h}", [P, E0, P], F32R) for h in ("hi", "lo")]
        av = stage = dup(2, "av", [P, 8 * HD * HEADS])

        kwT, owT = p0[:, 0:128], p0[:, 128:256]
        k_aff_b, k_b, o_aff_b, o_b = (p0[:, 256 + i:257 + i] for i in range(4))
        gates_rows, aw_rows, sim = p0[:, 260:276], p0[:, 276:282], p0[:, 282:298]

        style = sb("style", [P, 2, NBATCH])
        sq_w = sb("sq_w", [P, 2, P])
        sq_style = sb("sq_style", [P, 2, NBATCH])
        sq_sim = sb("sq_sim", [P, E0])
        norms = sb("norms", [P, 80])
        nrm_tmp = sb("nrm_tmp", [P, 3, 80])
        sn = sb("sn", [P, E0])
        sig_gates = sb("sig_gates", [P, 2, E0])
        aw_tmp = sb("aw_tmp", [P, 4, 6])

        def rsqrt(S, x, tmp, *after):
            half, a, y = tmp
            t = DVE.do(lambda e: e.tensor_scalar(a.bitcast(I32), x.bitcast(I32), 1, None,
                                                 ALU.logical_shift_right), *after)
            t = ts(DVE, y.bitcast(I32), a.bitcast(I32), -1.0, ALU.mult, t, s2=float(RSQRT_SEED), op1=ALU.add)
            h = ts(S, half, x, -0.5, ALU.mult, t)
            for step in range(3):
                t = tt(S, a, y, y, ALU.mult, t, h)
                t = tt(S, a, a, half, ALU.mult, t)
                t = ts(S, a, a, 1.5, ALU.add, t)
                t = tt(S, x if step == 2 else y, y, a, ALU.mult, t)
            return t

        setup_bank = banks[6]
        for i in range(2):
            t = mm(setup_bank[:, 32 * i:32 * i + 32], p64[:, 128 * i:128 * i + 128], p64[:, 256:288],
                   ld_p64, signal=i == 1)
        for i, b in enumerate((k_aff_b, o_aff_b)):
            t_style = ts(DVE, style[:, i, :], setup_bank[:, 32 * i:32 * i + 32], b, ALU.add, t, ld_p0)
        tt(DVE, sq_w[:, 0, :], kwT, kwT, ALU.mult, ld_p0)
        tt(DVE, sq_w[:, 1, :], owT, owT, ALU.mult)
        tt(DVE, sq_sim.ap, sim, sim, ALU.mult)
        t_sq = tt(DVE, sq_style.ap, style.ap, style.ap, ALU.mult, t_style)
        for i in range(2):
            mm(setup_bank[:, 64 + 32 * i:96 + 32 * i], sq_w[:, i, :], sq_style[:, i, :], t_sq, signal=False)
        t = mm(setup_bank[:, 128:144], ones, sq_sim.ap, ld_const)
        t1 = ts(DVE, norms[:, 0:64], setup_bank[:, 64:128], 1e-8, ALU.add, t)
        t2 = ts(DVE, norms[:, 64:80], setup_bank[:, 128:144], 1e-24, ALU.max, t)
        setup_bank.free = (t2,)
        t_norms = rsqrt(DVE, norms.ap, [nrm_tmp[:, i, :] for i in range(3)], t1, t2)
        demod = [norms[:, 0:32], norms[:, 32:64]]
        t_sn = tt(DVE, sn.ap, sim, norms[:, 64:80], ALU.mult, t_norms)
        t = act(sig_gates[:, 1, :], gates_rows, ACT.Tanh, ld_p0, scale=0.5)
        t_sig = ts(DVE, sig_gates[:, 0, :], sig_gates[:, 1, :], 0.5, ALU.mult, t, s2=0.5, op1=ALU.add)
        t = reduce(aw_tmp[:, 0, 0:1], aw_rows, ALU.max, ld_p0)
        t = ts(DVE, aw_tmp[:, 1, :], aw_rows, aw_tmp[:, 0, 0:1], ALU.subtract, t)
        t = act(aw_tmp[:, 2, :], aw_tmp[:, 1, :], ACT.Exp, t, accum=aw_tmp[:, 3, 0:1])
        t = DVE.do(lambda e: e.reciprocal(aw_tmp[:, 3, 1:2], aw_tmp[:, 3, 0:1]), t)
        t_aw = ts(DVE, aw.ap, aw_tmp[:, 2, :], aw_tmp[:, 3, 1:2], ALU.mult, t)
        t_sel = DVE.do(lambda e: e.tensor_copy(
            sel.ap, sel_raw[:, :].unsqueeze(2).broadcast_to([LO + E0, E0, P])), ld_sel)

        xsT = sb("xsT", [P, BLK])
        osT = sb("osT", [P, BLK])
        kT = sb("kT", [P, BLK])
        kks = dup(2, "kk", [P, TILES, 2 * P])
        prod = sb("prod", [P, 9, P])
        dbl = sb("dbl", [P, TILES, 7, 32])
        scs = dup(2, "sc", [P, TILES, HEADS, HEADS])
        mx = sb("mx", [P, TILES, HEADS])
        dens = dup(2, "den", [P, TILES, HEADS])
        osum = sb("osum", [P, TILES, P])
        x0T = dup(2, "x0T", [P, BLK])
        x0sq = sb("x0sq", [P, BLK])
        lg = sb("lg", [P, TILES, E0 + 1])
        rt = sb("rt", [P, TILES, 8, E0])
        rs = sb("rs", [P, 8, TILES])
        top = sb("top", [P, TILES, 8])
        topi = sb("topi", [P, TILES, 8], U32)
        whl = dup(2, "whl", [P, TILES, LO + E0])
        w_tok = dup(3, "w_tok", [P, TILES, E0])
        wT = dup(2, "wT", [LO + E0, BLK], F32R)
        ready_x0T = [None] * NBLK
        ready_w = [None] * NBLK
        ready_wT = [None] * NBLK
        t_whl0 = [POOL.do(lambda e, w=w: e.memset(w.ap, 0.0)) for w in whl]

        def bc(ap, n):
            return ap.unsqueeze(2).broadcast_to([P, TILES, n])

        def across(ap, n):
            return ap.unsqueeze(1).broadcast_to([P, TILES, n])

        z = dup(3, "z", [P, BLK])
        zh = dup(3, "zh", [P, BLK], F32R)
        zl = dup(3, "zl", [P, BLK], F32R)
        made = [0]
        consumed = {}
        split = {}
        x0_taken = [0]
        qkv_done = [None] * NBLK
        qkv_copied = [None] * NBLK
        o_ready = [None] * NBLK
        x1_done = [None] * NBLK
        ready_expert = {}

        head_weights = [None] * NBLK
        heads_done = [0]

        def head_scores():
            for b in range(NBLK):
                s1 = banks[7]
                yield lambda: heads_done[0] >= b - 1
                kk, sc, den = kks[b % 2], scs[b % 2], dens[b % 2]
                src = xT[b % 2]
                t_x = None
                for j in range(TILES):
                    col = TILES * b + j
                    t_x = act(xsT[:, j * P:(j + 1) * P], src[:, j * P:(j + 1) * P], ACT.Copy, ld_x[b], t_style,
                              *xsT.free, scale=style[:, 0, col:col + 1])
                src.free = (t_x,)
                if b + 1 < NBLK:
                    load_xT(b + 1)
                yield
                yield from s1.grab()
                t = mm(s1.ap, kwT, xsT.ap, t_x, *s1.free)
                xsT.free = (t,)
                yield
                for j in range(TILES):
                    col = TILES * b + j
                    t = act(kT[:, j * P:(j + 1) * P], s1[:, j * P:(j + 1) * P], ACT.Identity, t, t_norms, *kT.free,
                            scale=demod[0][:, col:col + 1], bias=k_b)
                yield
                t = turn_tiles(s1, squares(kT), t, ld_const)
                kT.free = (t,)
                yield
                s1v = s1[:, :].rearrange("p (t f) -> p t f", t=TILES)
                act(kk[:, :, 0:P], s1v, ACT.Copy, t, *kk.free)
                t_kk = act(kk[:, :, P:2 * P], s1v, ACT.Copy)
                s1.drop(t_kk)
                yield
                for j in range(TILES):
                    k0 = kk[:, j, 0:P]
                    t = tt(DVE, prod.ap, view(k0, 0, [[0, 9], [1, P]]), view(k0, 0, [[HD, 9], [1, P]]), ALU.mult,
                           t_kk, *prod.free)
                    yield
                    t_sc = reduce(sc[:, j, 0:9, :], prod[:, :, :].rearrange("p r (h d) -> p r h d", d=HD), ALU.add,
                                  t, *sc.free)
                    prod.free = (t_sc,)
                    yield
                act(dbl[:, :, :, 0:HEADS], sc[:, :, 1:8, :], ACT.Copy, t_sc, *dbl.free)
                t = act(dbl[:, :, :, HEADS:], sc[:, :, 1:8, :], ACT.Copy)
                yield
                t = act(sc[:, :, 9:16, :], view(dbl.ap, 6 * 32 + 9, [[7 * 32, TILES], [-31, 7], [1, HEADS]]),
                        ACT.Copy, t)
                dbl.free = (t,)
                yield
                t = reduce(mx.ap, sc[:, :, :, :].rearrange("p t s h -> p t h s"), ALU.max, t, *mx.free)
                yield
                t = tt(DVE, sc.ap, sc.ap, view(mx.ap, 0, [[HEADS, TILES], [0, HEADS], [1, HEADS]]), ALU.subtract, t)
                mx.free = (t,)
                yield
                t_e = act(sc.ap, sc.ap, ACT.Exp, t, scale=HD ** -0.5)
                yield
                t = reduce(den.ap, sc[:, :, :, :].rearrange("p t s h -> p t h s"), ALU.add, t_e, *den.free)
                t_den = DVE.do(lambda e, den=den: e.reciprocal(den.ap, den.ap), t)
                head_weights[b] = (t_e, t_kk, t_den)
                yield

        def head_values():
            for b in range(NBLK):
                yield lambda: head_weights[b] and head_weights[b][0]
                s1 = banks[7]
                kk, sc, den = kks[b % 2], scs[b % 2], dens[b % 2]
                t_e, t_kk, t_den = head_weights[b]
                pending, last = [], {}

                def add_shifts(q, j, h0, t_q):
                    t = reduce(osum[:, j, HD * h0:HD * h0 + 64], q[:, :].rearrange("p (n s) -> p n s", s=HEADS),
                               ALU.add, t_q, *osum.free)
                    q.free = (t,)
                    return t

                for n in range(2 * TILES):
                    j, h0, q = n // 2, 8 * (n % 2), av[n % 2]
                    a = view(sc[:, j, 0, h0:h0 + 1], 0, [[1, 8], [0, HD], [HEADS, HEADS]])
                    v = view(kk[:, j, HD * h0:HD * h0 + 1], 0, [[HD, 8], [1, HD], [HD, HEADS]])
                    q4 = q[:, :].rearrange("p (h d s) -> p h d s", h=8, d=HD)
                    S = lighter(8 * HD * HEADS)
                    t_q = tt(S, q4, a, v, ALU.mult, t_e, t_kk, *q.free)
                    last[S] = t_q
                    pending.append((q, j, h0, t_q))
                    if n:
                        yield
                        t = add_shifts(*pending.pop(0))
                yield
                t = add_shifts(*pending.pop(0))
                sc.free = kk.free = tuple(last.values())
                heads_done[0] += 1
                yield
                on = osum[:, :, :].rearrange("p t (h d) -> p t h d", d=HD)
                t = tt(DVE, on, on, den[:, :, :].unsqueeze(3).broadcast_to([P, TILES, HEADS, HD]), ALU.mult, t,
                       t_den)
                den.free = (t,)
                yield
                yield from s1.grab()
                t = turn_tiles(s1, rows_of(osum), t, *s1.free)
                osum.free = (t,)
                yield
                for j in range(TILES):
                    col = TILES * b + j
                    t = act(osT[:, j * P:(j + 1) * P], s1[:, j * P:(j + 1) * P], ACT.Copy, t, *osT.free,
                            scale=style[:, 1, col:col + 1])
                yield
                t = mm(s1.ap, owT, osT.ap, t)
                osT.free = (t,)
                yield lambda: x0_taken[0] >= b - 1
                x0 = x0T[b % 2]
                for j in range(TILES):
                    col = TILES * b + j
                    t = act(x0[:, j * P:(j + 1) * P], s1[:, j * P:(j + 1) * P], ACT.Identity, t, *x0.free,
                            scale=demod[1][:, col:col + 1], bias=o_b)
                s1.drop(t)
                ready_x0T[b] = t
                yield

        def route():
            for b in range(NBLK):
                yield lambda: ready_x0T[b]
                bank = banks[6]
                x0 = x0T[b % 2]
                t_x0 = ready_x0T[b]
                t = act(x0sq.ap, x0.ap, ACT.Square, t_x0, *x0sq.free)
                yield
                yield from bank.grab()
                for j in range(TILES):
                    mm(bank[:, 32 * j:32 * j + E0], x0[:, j * P:(j + 1) * P], sn.ap, t, t_sn, *bank.free,
                       signal=False)
                    t_l = mm(bank[:, 32 * j + E0:32 * j + E0 + 1], x0sq[:, j * P:(j + 1) * P], ones[:, 0:1], t,
                             signal=j == TILES - 1)
                x0sq.free = (t_l,)
                yield
                t = DVE.do(lambda e: e.tensor_copy(
                    lg.ap, bank[:, 0:128].rearrange("p (t n) -> p t n", t=TILES)[:, :, 0:E0 + 1]), t_l, *lg.free)
                bank.drop(t)
                yield
                r = [rs[:, i, :] for i in range(8)]
                t = ts(DVE, r[0], lg[:, :, E0], 1e-24, ALU.max, t, *rs.free)
                yield
                half, a, y = r[1], r[2], r[3]
                t1 = DVE.do(lambda e: e.tensor_scalar(a.bitcast(I32), r[0].bitcast(I32), 1, None,
                                                      ALU.logical_shift_right), t)
                ts(DVE, half, r[0], -0.5, ALU.mult, t)
                yield
                t = ts(DVE, y.bitcast(I32), a.bitcast(I32), -1.0, ALU.mult, t1, s2=float(RSQRT_SEED), op1=ALU.add)
                yield
                for step in range(3):
                    t = tt(DVE, a, y, y, ALU.mult, t)
                    yield
                    t = tt(DVE, a, a, half, ALU.mult, t)
                    yield
                    t = DVE.do(lambda e: e.scalar_tensor_tensor(out=y, in0=a, scalar=1.5, in1=y, op0=ALU.add,
                                                                op1=ALU.mult), t)
                    yield
                R = [rt[:, :, i, :] for i in range(8)]
                t = tt(DVE, R[0], lg[:, :, 0:E0], bc(y, E0), ALU.mult, t, *rt.free)
                lg.free = (t,)
                yield
                t_log = tt(DVE, R[0], R[0], across(sig_gates[:, 0, :], E0), ALU.subtract, t, t_sig)
                yield
                for j in range(TILES):
                    t_top = DVE.do(lambda e, j=j: e.max(top[:, j, :], R[0][:, j, :]), t_log, *top.free)
                yield
                for j in range(TILES):
                    t = DVE.do(lambda e, j=j: e.max_index(topi[:, j, :], top[:, j, :], R[0][:, j, :]), t_top)
                t_i = ts(DVE, r[6], top[:, :, 0], 0.0, ALU.is_le, t_top)
                t_g = ts(DVE, r[7], top[:, :, 0], 0.0, ALU.max, t_top)
                t = DVE.do(lambda e: e.tensor_copy(rs[:, 4:6, :], topi[:, :, 0:2].rearrange("p t k -> p k t")), t)
                top.free = (t_g, t)
                yield
                t1 = tt(DVE, R[1], across(iota, E0), bc(r[4], E0), ALU.is_equal, t)
                t2 = tt(DVE, R[2], across(iota, E0), bc(r[5], E0), ALU.is_equal, t)
                t4 = DVE.do(lambda e: e.scalar_tensor_tensor(out=R[4], in0=R[0], scalar=0.0, in1=bc(r[7], E0),
                                                             op0=ALU.max, op1=ALU.subtract), t_g, n=64)
                t_e = act(R[5], R[4], ACT.Exp, t4)
                yield
                t = tt(DVE, R[1], R[1], R[2], ALU.add, t1, t2)
                yield
                t = tt(DVE, R[1], R[1], bc(r[6], E0), ALU.mult, t, t_i)
                yield
                t_m = DVE.do(lambda e: e.scalar_tensor_tensor(out=R[1], in0=R[0], scalar=0.0, in1=R[1],
                                                              op0=ALU.is_gt, op1=ALU.add), t, n=64)
                yield
                t = tt(DVE, R[5], R[5], R[1], ALU.mult, t_e, t_m)
                yield
                t = reduce(r[1], R[5], ALU.add, t)
                yield
                t = DVE.do(lambda e: e.reciprocal(r[2], r[1]), t)
                yield lambda: b < 3 or o_ready[b - 3]
                w = w_tok[b % 3]
                t = t_w = tt(DVE, w.ap, R[5], bc(r[2], E0), ALU.mult, t, *w.free)
                rt.free = rs.free = (t,)
                wp = whl[b % 2]
                yield
                t = act(wp[:, :, 0:E0].bitcast(F32R), w.ap, ACT.Copy, t, t_whl0[b % 2], *wp.free)
                yield
                t = tt(DVE, wp[:, :, LO:LO + E0], w.ap, wp[:, :, 0:E0], ALU.subtract, t)
                yield
                yield from bank.grab()
                for j in range(TILES):
                    t1 = turn(bank[0:LO + E0, j * P:(j + 1) * P], wp[:, j, :], ident, t, *bank.free,
                              signal=j == TILES - 1)
                wp.free = (t1,)
                yield lambda: x0_taken[0] >= b - 1
                wst = wT[b % 2]
                t = act(wst.ap, bank[0:LO + E0, :], ACT.Copy, t1, *wst.free)
                bank.drop(t)
                ready_w[b] = t_w
                ready_wT[b] = t
                yield

        def scale_inputs():
            for b in range(NBLK):
                yield AHEAD, lambda: ready_wT[b]
                x0, wst = x0T[b % 2], wT[b % 2]
                for e in range(E0):
                    n = made[0]
                    yield AHEAD, lambda: n < 3 or consumed.get(n - 3)
                    bank = banks[3 + n % 2]
                    zi, hi, lo = z[n % 3], zh[n % 3], zl[n % 3]
                    t_w = mm(bank.ap, sel[:, e, :], wst.ap, ready_wT[b], t_sel, *bank.free)
                    t_z = tt(DVE, zi.ap, x0.ap, bank.ap, ALU.mult, t_w, ready_x0T[b], *zi.free)
                    bank.free = (t_z,)
                    t_hi = act(hi.ap, zi.ap, ACT.Copy, t_z, *hi.free)
                    t_lo = tt(lighter(BLK), lo.ap, zi.ap, hi[:, :].bitcast(F32), ALU.subtract, t_hi, *lo.free)
                    zi.free = (t_lo,)
                    split[n] = (t_hi, t_lo)
                    made[0] += 1
                x0.free = (t_z,)
                wst.free = (t_w,)
                x0_taken[0] += 1

        def project():
            n = 0
            for b in range(NBLK):
                yield lambda: b == 0 or qkv_copied[b - 1]
                for e in range(E0):
                    yield lambda: e in ready_expert and made[0] > n and split[n][1]
                    t_hi, t_lo = split[n]
                    hi, lo = zh[n % 3], zl[n % 3]
                    for i in range(3):
                        first = banks[i].free if e == 0 else ()
                        mm(banks[i].ap, wqkv[0][:, e, i, :], hi.ap, t_hi, ready_expert[e], *first,
                           start=e == 0, stop=False, signal=False)
                        mm(banks[i].ap, wqkv[1][:, e, i, :], hi.ap, start=False, stop=False, signal=False)
                    for i in range(3):
                        t = mm(banks[i].ap, wqkv[0][:, e, i, :], lo.ap, t_lo, start=False, stop=e == E0 - 1,
                               signal=i == 2)
                    hi.free = lo.free = (t,)
                    consumed[n] = t
                    n += 1
                qkv_done[b] = t

        qT = dup(3, "qT", [P, BLK])
        pexp = sb("pexp", [P, TILES, P])
        pT = sb("pT", [P, BLK])
        v_tok = sb("v_tok", [P, TILES, P])
        oh = dup(2, "oh", [P, BLK], F32R)
        ol = dup(2, "ol", [P, BLK], F32R)
        sm = sb("sm", [P, 4, TILES])
        w_out = dup(2, "w_out", [P, TILES, E0])
        ld_x1 = load("x1", x1.ap, ins["x_tok"])
        w_out_done = [None] * NBLK

        def row_attention():
            for b in range(NBLK):
                at = banks[6]
                yield lambda: qkv_done[b]
                for i in range(3):
                    t = act(qT[i].ap, banks[i].ap, ACT.Copy, qkv_done[b], *qT[i].free)
                    banks[i].free = (t,)
                qkv_copied[b] = t
                yield
                yield from at.grab()
                for j, (q, k) in enumerate(zip(squares(qT[0]), squares(qT[1]))):
                    t1 = mm(at[:, j * P:(j + 1) * P], q, k, t, *at.free, signal=j == TILES - 1)
                qT[0].free = qT[1].free = (t1,)
                av4 = at[:, :].rearrange("p (t s) -> p t s", t=TILES)
                yield
                t = reduce(sm[:, 0, :], av4, ALU.max, t1, *sm.free)
                yield
                t = ts(DVE, sm[:, 1, :], sm[:, 0, :], -P ** -0.5, ALU.mult, t)
                yield
                for j in range(TILES):
                    t = act(pexp[:, j, :], av4[:, j, :], ACT.Exp, t, *pexp.free, scale=P ** -0.5,
                            bias=sm[:, 1, j:j + 1], accum=sm[:, 2, j:j + 1])
                yield
                t1 = DVE.do(lambda e: e.reciprocal(sm[:, 3, :], sm[:, 2, :]), t)
                t = turn_tiles(at, rows_of(pexp), t)
                pexp.free = (t,)
                yield lambda: b < 2 or x1_done[b - 2]
                w = w_tok[b % 3]
                t_w = tt(DVE, w_out[b % 2].ap, w.ap, bc(sm[:, 3, :], E0), ALU.mult, t1, ready_w[b],
                         *w_out[b % 2].free)
                w.free = sm.free = (t_w,)
                t = act(pT.ap, at.ap, ACT.Copy, t, *pT.free)
                yield
                t = turn_tiles(at, squares(qT[2]), t)
                qT[2].free = (t,)
                yield
                t = act(v_tok[:, :, :].rearrange("p t h -> p (t h)"), at.ap, ACT.Copy, t, *v_tok.free)
                yield
                for j, pj in enumerate(squares(pT)):
                    t1 = mm(at[:, j * P:(j + 1) * P], v_tok[:, j, :], pj, t, signal=j == TILES - 1)
                pT.free = v_tok.free = (t1,)
                yield
                hi, lo = oh[b % 2], ol[b % 2]
                t = act(hi.ap, at.ap, ACT.Copy, t1, *hi.free)
                yield
                t = tt(DVE, lo.ap, at.ap, hi[:, :].bitcast(F32), ALU.subtract, t, *lo.free)
                at.drop(t)
                w_out_done[b] = t_w
                o_ready[b] = t
                yield

        def project_out():
            ob = banks[5]
            for b in range(NBLK):
                yield lambda: o_ready[b] and "o" in ready_expert
                hi, lo, w = oh[b % 2], ol[b % 2], w_out[b % 2]
                for j in range(TILES):
                    acc = x1[:, TILES * b + j, :]
                    c = slice(j * P, (j + 1) * P)
                    t_acc = ld_x1
                    for g in range(E0 // 4):
                        es = slice(4 * g, 4 * g + 4)
                        mm(ob.ap, hi[:, c], wo[0][:, es, :], o_ready[b], *ob.free, ready_expert["o"], start=True,
                           stop=False, signal=False)
                        mm(ob.ap, hi[:, c], wo[1][:, es, :], start=False, stop=False, signal=False)
                        t_o = mm(ob.ap, lo[:, c], wo[0][:, es, :], start=False, stop=True)
                        yield
                        for k in range(4):
                            ee = 4 * g + k
                            t_acc = DVE.do(lambda e, k=k, ee=ee, acc=acc, j=j, w=w: e.scalar_tensor_tensor(
                                out=acc, in0=ob[:, k * P:(k + 1) * P], scalar=w[:, j, ee:ee + 1], in1=acc,
                                op0=ALU.mult, op1=ALU.add), t_o, t_acc, w_out_done[b], n=128)
                        ob.free = (t_acc,)
                        yield
                hi.free = lo.free = (t_o,)
                w.free = (t_acc,)
                x1_done[b] = t_acc

        def split_weights():
            n = 0
            for name, src, hl, cols in (("qkv", ins["w_qkv"], wqkv, E0 * 3 * P), ("o", ins["w_o"], wo, E0 * P)):
                flat = [h.ap.rearrange("p e i h -> p (e i h)") if name == "qkv" else
                        h.ap.rearrange("p e h -> p (e h)") for h in hl]
                step = 768 if name == "qkv" else 1024
                for c in range(0, cols, step):
                    s = stage[n % 2]
                    n += 1
                    t = load(f"{name}{c}", s[:, 0:step], src[:, c:c + step], *s.free)
                    t = act(flat[0][:, c:c + step], s[:, 0:step], ACT.Copy, t)
                    t = tt(DVE, flat[1][:, c:c + step], s[:, 0:step], flat[0][:, c:c + step].bitcast(F32),
                           ALU.subtract, t)
                    s.free = (t,)
                    if name == "qkv":
                        for e in range(c // (3 * P), (c + step) // (3 * P)):
                            ready_expert[e] = t
                    else:
                        ready_expert["o"] = t
                    yield

        ld_p1 = load("p1", p1.ap, ins["p1"])
        ld_tabs = load("tabs", tabs_raw.ap, ins["tabs"])
        ld_idval = load("idval", idval.ap, ins["c_idval"])
        ld_tok = load("tok", tok_ids.ap, ins["tok_ids"])

        weave(split_weights(), head_scores(), head_values(), route(), scale_inputs(), project(), row_attention(), project_out())

        everything = [s.mark() for s in (PE, DVE, ACTE, POOL)]
        for s in (PE, DVE, ACTE, POOL, SP):
            s.do(None, *everything, signal=False)
        scope_a.close()
        stack.pop()
        layer[0] = "l1_"
        for bank in banks:
            bank.free, bank.held = (), False

        wgu = [sb(f"wgu{h}", [P, 2, CH1, P], F32R) for h in ("hi", "lo")]
        wdn = [sb(f"wdn{h}", [P, CH1, P], F32R) for h in ("hi", "lo")]
        W1 = p1[:, 0:768].rearrange("p (k o) -> p k o", k=6)
        W2, routerT, b2_rows = p1[:, 768:896], p1[:, 896:904], p1[:, 904:1032]
        mlp_W2 = [p1[:, 1032 + 128 * i:1160 + 128 * i] for i in range(3)]
        mlp_b2 = [p1[0:NBATCH, 1416 + 128 * i:1544 + 128 * i] for i in range(3)]
        col = {n: p1[:, 1800 + i:1801 + i] for i, n in enumerate(
            ("int_b1", "int_g", "int_be", "b1_0", "b1_1", "b1_2", "g_0", "be_0", "g_1", "be_1", "g_2", "be_2"))}
        cp_bT, tm_bT, ms_bT = p1[:, 1812:1817], p1[:, 1817:1822], p1[:, 1822:1825]
        ms_col = p1[:, 1825:1833]

        gu_raw = sb("gu_raw", [P, 2, CH1, P])
        dn_raw = sb("dn_raw", [P, CH1, P])
        pm64 = sb("pm64", [64, 320])
        pm32 = sb("pm32", [32, 160])
        ld_pm64 = load("pm64", pm64.ap, ins["pm64"])
        ld_pm32 = load("pm32", pm32.ap, ins["pm32"])
        ld_gu = load("gu", gu_raw.ap, ins["w_gu"])
        ld_dn = load("dn", dn_raw.ap, ins["w_dn"])
        cond_in = [(pm64[:, 0:128], pm64[:, 256:288], ld_pm64), (pm64[:, 128:256], pm64[:, 288:320], ld_pm64),
                   (pm32[:, 0:128], pm32[:, 128:160], ld_pm32)]

        def halves(raw, hi, lo, t, S):
            t = act(hi, raw, ACT.Copy, t)
            return tt(S, lo, raw, hi.bitcast(F32), ALU.subtract, t)

        mlp_h = sb("mlp_h", [P, 3, NBATCH])
        mlp_o = sb("mlp_o", [NBATCH, 3, P])
        mlp_st = sb("mlp_st", [NBATCH, 3, 6])
        mlp_mv = sb("mlp_mv", [NBATCH, 3, 2])
        mlp_var = sb("mlp_var", [NBATCH, 4, 3])
        mlp_T = sb("mlp_T", [P, 3, NBATCH])
        W1w = sb("W1w", [P, 6, P])
        Wx = sb("Wx", [P, P])
        base = sb("base", [P, NBATCH])
        tabT = sb("tabT", [P, 3, LO + 8])
        tabs = [sb("tabs_hl", [LO + 8, 4, P], F32R), sb("tabs_tmp", [LO + 8, 4, P], F32R)]
        bias_raw = sb("bias_raw", [LO + 8, P])

        marks = {}

        def setup_condition():
            for k in range(6):
                t = ts(DVE, W1w[:, k, :], W1[:, k, :], aw[:, k:k + 1], ALU.mult, t_aw, ld_p1)
            t = tt(DVE, Wx.ap, W1w[:, 2, :], W1w[:, 3, :], ALU.add, t)
            marks['W1'] = tt(DVE, Wx.ap, Wx.ap, W1w[:, 4, :], ALU.add, t)
            yield
            sb_bank, sb2 = banks[0], banks[1]
            for i, (w, s, ld) in enumerate(cond_in):
                t = mm(sb_bank[:, 32 * i:32 * i + 32], w, s, ld, signal=i == 2)
            yield
            for i in range(3):
                t = act(mlp_h[:, i, :], sb_bank[:, 32 * i:32 * i + 32], ACT.Silu, t, ld_p1, bias=col[f"b1_{i}"])
            for i in range(3):
                t = mm(sb_bank[0:NBATCH, 128 * i:128 * i + 128], mlp_h[:, i, :], mlp_W2[i], t, signal=i == 2) or t
            yield
            for i in range(3):
                t = tt(DVE, mlp_o[:, i, :], sb_bank[0:NBATCH, 128 * i:128 * i + 128], mlp_b2[i], ALU.add, t)
            for i in range(3):
                t = DVE.do(lambda e, i=i: e.bn_stats(mlp_st[:, i, :], mlp_o[:, i, :]), t)
            for i in range(3):
                t = DVE.do(lambda e, i=i: e.bn_aggr(mlp_mv[:, i, :], mlp_st[:, i, :]), t)
            yield
            t = ts(DVE, mlp_var[:, 0, :], mlp_mv[:, :, 1], 1e-5, ALU.add, t)
            t = rsqrt(DVE, mlp_var[:, 0, :], [mlp_var[:, 1 + i, :] for i in range(3)], t)
            for i in range(3):
                t = ts(DVE, mlp_o[:, i, :], mlp_o[:, i, :], mlp_mv[:, i, 0:1], ALU.subtract, t,
                       s2=mlp_var[:, 0, i:i + 1], op1=ALU.mult)
            yield
            for i in range(3):
                t = PE.do(lambda e, i=i: e.transpose(sb_bank[:, 32 * i:32 * i + 32], mlp_o[:, i, :],
                                                     ident[0:NBATCH, 0:NBATCH]), t, signal=i == 2) or t
            yield
            for i in range(3):
                t = act(mlp_T[:, i, :], sb_bank[:, 32 * i:32 * i + 32], ACT.Identity, t, scale=col[f"g_{i}"],
                        bias=col[f"be_{i}"])
            for i in range(3):
                t = mm(sb_bank[:, 0:NBATCH], W1w[:, 2 + i, :], mlp_T[:, i, :], t, marks['W1'], start=i == 0, stop=i == 2,
                       signal=i == 2) or t
            marks['base'] = ts(DVE, base.ap, sb_bank[:, 0:NBATCH], col["int_b1"], ALU.add, t)
            sb_bank.free = (marks['base'],)
            yield
            t = POOL.do(lambda e: e.memset(tabT.ap, 0.0))
            for k, (src, at, n) in enumerate(((cp_bT, 0, 5), (tm_bT, 0, 5), (ms_bT, 5, 3))):
                for o in (0, LO):
                    t = DVE.do(lambda e, k=k, src=src, at=at, n=n, o=o: e.tensor_copy(
                        tabT[:, k, o + at:o + at + n], src), t, ld_p1)
            for k, i in enumerate((0, 1, 5)):
                t = mm(sb2[0:LO + 8, 0:P], tabT[:, k, :], W1w[:, i, :], t, marks['W1'], start=k == 0, stop=k == 2,
                       signal=k == 2) or t
            t = DVE.do(lambda e: e.tensor_copy(bias_raw.ap, sb2[0:LO + 8, 0:P]), t)
            sb2.free = (t,)
            yield
            raws = [tabs_raw[:, k, :] for k in range(3)] + [bias_raw.ap]
            t_hi = t
            for k in range(4):
                t_hi = DVE.do(lambda e, k=k: e.tensor_copy(tabs[0][:, k, :], raws[k]), t, ld_tabs)
            for k in range(4):
                t1 = DVE.do(lambda e, k=k: e.tensor_copy(tabs[1][:, k, :], raws[k]), t_hi)
            for k in range(4):
                marks['tabs'] = tt(DVE, tabs[0][LO:LO + 8, k, :], raws[k][LO:LO + 8, :],
                            tabs[1][LO:LO + 8, k, :].bitcast(F32), ALU.subtract, t1)
        t_gu, t_dn = {}, {}

        def split_expert_weights():
            for g in range(4):
                c = slice(4 * g, 4 * g + 4)
                for i in range(2):
                    t_gu[g, i] = halves(gu_raw[:, i, c, :], wgu[0][:, i, c, :], wgu[1][:, i, c, :], ld_gu,
                                        POOL if i and g else DVE)
                    yield
                t_dn[g] = halves(dn_raw[:, c, :], wdn[0][:, c, :], wdn[1][:, c, :], ld_dn, POOL if g > 1 else DVE)
                yield

        ids = dup(2, "ids", [LO + 8, BLK], I32)
        onehot = sb("onehot", [LO + 8, BLK], F32R)
        pw = dup(2, "pw", [P, TILES, 2 * P])
        scratch_in, scratch_out = ([sb(f"stats{i}", [P, TILES, 6]), sb(f"mean_var{i}", [P, TILES, 2]),
                                    sb(f"rstd{i}", [P, 4, TILES])] for i in range(2))
        z1s = dup(2, "xn", [P, TILES, P])
        z2s = dup(2, "pn", [P, TILES, P])
        fT = dup(3, "fT", [P, BLK])
        gT = dup(3, "gT", [P, BLK])
        s1T = sb("s1T", [P, BLK])
        h2s = dup(2, "h2", [P, TILES, P])
        yT = dup(2, "yT", [P, BLK])
        yh = dup(2, "yh", [P, BLK], F32R)
        yl = dup(2, "yl", [P, BLK], F32R)
        rl = sb("rl", [P, TILES, E1])
        top1 = sb("top1", [P, TILES, 8])
        topi1 = sb("topi1", [P, TILES, 8], U32)
        r1 = sb("r1", [P, 6, TILES])
        R1 = sb("R1", [P, TILES, 3, E1])
        chl = sb("chl", [P, TILES, LO + E1])
        cT = dup(2, "cT", [LO + E1, BLK], F32R)
        z = dup(3, "z", [P, BLK])
        zh = dup(3, "zh", [P, BLK], F32R)
        zl = dup(3, "zl", [P, BLK], F32R)
        ready_y = [None] * NBLK
        ready_yl = [None] * NBLK
        ready_cT = [None] * NBLK
        t_chl0 = POOL.do(lambda e: e.memset(chl.ap, 0.0))
        ld_ids, ld_pw = [None] * NBLK, [None] * NBLK

        def fetch(b):
            if b >= NBLK:
                return
            ld_ids[b] = load(f"ids{b}", ids[b % 2].ap, ins["ids"][:, b * BLK:(b + 1) * BLK], *ids[b % 2].free)
            s = semaphore(f"ld_pw{b}")
            for j in range(TILES):
                c = TILES * b + j
                ld_pw[b] = POOL.dma(lambda e, j=j, c=c: e.indirect_dma_start(
                    pw[b % 2][:, j, :], None, ins["pw"],
                    bass.IndirectOffsetOnAxis(ap=tok_ids[:, c:c + 1].bitcast(U32), axis=0)),
                    (s, 16 * (j + 1)), ld_tok, *pw[b % 2].free)

        def norm(scratch, src, dst, t, *free):
            st, mv, nr = scratch
            for j in range(TILES):
                t1 = DVE.do(lambda e, j=j: e.bn_stats(st[:, j, :], src[:, j, :]), t, *st.free, n=128)
            yield
            for j in range(TILES):
                t1 = DVE.do(lambda e, j=j: e.bn_aggr(mv[:, j, :], st[:, j, :]), t1, *mv.free)
            yield
            v, half, a, y = (nr[:, i, :] for i in range(4))
            t1 = ts(DVE, v, mv[:, :, 1], 1e-5, ALU.add, t1, *nr.free)
            yield
            t2 = DVE.do(lambda e: e.tensor_scalar(a.bitcast(I32), v.bitcast(I32), 1, None,
                                                  ALU.logical_shift_right), t1)
            t1 = ts(DVE, half, v, -0.5, ALU.mult, t1)
            yield
            t1 = ts(DVE, y.bitcast(I32), a.bitcast(I32), -1.0, ALU.mult, t1, t2, s2=float(RSQRT_SEED), op1=ALU.add)
            yield
            for _ in range(3):
                t1 = tt(DVE, a, y, y, ALU.mult, t1)
                yield
                t1 = tt(DVE, a, a, half, ALU.mult, t1)
                yield
                t1 = DVE.do(lambda e: e.scalar_tensor_tensor(out=y, in0=a, scalar=1.5, in1=y, op0=ALU.add,
                                                             op1=ALU.mult), t1)
                yield
            for j in range(TILES):
                t2 = ts(DVE, dst[:, j, :], src[:, j, :], mv[:, j, 0:1], ALU.subtract, t1, *free,
                        s2=nr[:, 3, j:j + 1], op1=ALU.mult)
            st.free = mv.free = nr.free = (t2,)
            yield
            return t2

        y_taken = [0]
        g_taken = [0]

        def to_features(bank, src, dst, t, **kw):
            yield from bank.grab()
            t = turn_tiles(bank, rows_of(src), t, *bank.free)
            yield
            t1 = act(dst.ap, bank.ap, kw.pop("func", ACT.Copy), t, *dst.free, **kw)
            bank.drop(t1)
            return t, t1

        z_done, h_done = [None] * NBLK, [None] * NBLK
        f_taken = [0]
        h_taken = [0]

        def normalise_input():
            for b in range(NBLK):
                yield lambda: f_taken[0] >= b - 1
                x = x1[:, TILES * b:TILES * (b + 1), :]
                z1, z2, g = z1s[b % 2], z2s[b % 2], pw[b % 2]
                t_z1 = yield from norm(scratch_in, x, z1, x1_done[b], *z1.free)
                t = tt(POOL, z2.ap, z1.ap, g[:, :, 0:P], ALU.mult, t_z1, ld_pw[b], *z2.free)
                yield
                t_p = tt(POOL, z2.ap, z2.ap, g[:, :, P:2 * P], ALU.add, t)
                g.free = (t_p,)
                yield
                t = yield from norm(scratch_in, z2, z2, t_p)
                z_done[b] = (t, t_z1, t_p)

        def condition():
            A, B = banks[6], banks[7]
            for b in range(NBLK):
                yield lambda: z_done[b] and z_done[b][0]
                fetch(b + 1)
                t_z2, t_z1, t_p = z_done[b]
                z1, z2 = z1s[b % 2], z2s[b % 2]
                x = x1[:, TILES * b:TILES * (b + 1), :]
                t_oh = ts(DVE, onehot.ap, ids[b % 2].ap, idval[:, 0:1], ALU.is_equal, ld_ids[b], ld_idval,
                          *onehot.free)
                ids[b % 2].free = (t_oh,)
                t1, t_f1 = yield from to_features(A, z1, fT[1], t_z1)
                z1.free = (t_p, t1)
                t1, t_f0 = yield from to_features(B, z2, fT[0], t_z2)
                z2.free = (t1,)
                f_taken[0] += 1
                _, t_f2 = yield from to_features(A, x, fT[2], x1_done[b])
                yield lambda: "tabs" in marks and marks["tabs"]
                tg = [None] * 3
                for k, bank in ((1, B), (2, A), (0, B)):
                    f, t_f = (fT[0], t_f0) if k == 0 else (fT[1], t_f1)
                    yield from bank.grab()
                    t = mm(bank.ap, tabs[0][:, k, :], onehot.ap, t_oh, marks["tabs"], *bank.free)
                    yield
                    tg[k] = tt(DVE, gT[k].ap, f.ap, bank.ap, ALU.mult, t, t_f, *gT[k].free)
                    bank.drop(tg[k])
                    yield
                fT[1].free, fT[0].free = (tg[2],), (tg[0],)
                yield from A.grab()
                mm(A.ap, tabs[0][:, 3, :], onehot.ap, *A.free, start=True, stop=False, signal=False)
                mm(A.ap, Wx.ap, fT[2].ap, t_f2, marks["W1"], start=False, stop=False, signal=False)
                mm(A.ap, W1w[:, 1, :], gT[1].ap, tg[1], start=False, stop=False, signal=False)
                yield
                mm(A.ap, W1w[:, 5, :], gT[2].ap, tg[2], start=False, stop=False, signal=False)
                yield lambda: "base" in marks and marks["base"]
                t = mm(A.ap, W1w[:, 0, :], gT[0].ap, tg[0], start=False, stop=True)
                onehot.free = fT[2].free = (t,)
                for k in range(3):
                    gT[k].free = (t,)
                yield
                for j in range(TILES):
                    c = TILES * b + j
                    t = act(s1T[:, j * P:(j + 1) * P], A[:, j * P:(j + 1) * P], ACT.Silu, t, marks["base"],
                            *s1T.free, bias=base[:, c:c + 1])
                A.drop(t)
                yield
                yield from B.grab()
                for j, sj in enumerate(squares(s1T)):
                    t1 = mm(B[:, j * P:(j + 1) * P], sj, W2, t, *B.free, signal=j == TILES - 1)
                s1T.free = (t1,)
                yield lambda: h_taken[0] >= b - 1
                h2 = h2s[b % 2]
                t = tt(DVE, h2.ap, B[:, :].rearrange("p (t f) -> p t f", t=TILES), across(b2_rows, P), ALU.add, t1,
                       *h2.free)
                B.drop(t)
                h_done[b] = t
                yield

        def normalise_output():
            A = banks[6]
            for b in range(NBLK):
                yield lambda: h_done[b]
                h2 = h2s[b % 2]
                t = yield from norm(scratch_out, h2, h2, h_done[b])
                yield lambda: y_taken[0] >= b - 1 and g_taken[0] >= b - 1
                y = yT[b % 2]
                t, t_y = yield from to_features(A, h2, y, t, func=ACT.Identity, scale=col["int_g"],
                                                bias=col["int_be"])
                h2.free = (t,)
                h_taken[0] += 1
                yield
                t_h = act(yh[b % 2].ap, y.ap, ACT.Copy, t_y, *yh[b % 2].free)
                ready_y[b] = t_y
                yield
                ready_yl[b] = tt(lighter(BLK), yl[b % 2].ap, y.ap, yh[b % 2][:, :].bitcast(F32), ALU.subtract,
                                 t_h, *yl[b % 2].free)
                yield

        def choose():
            A, B = banks[6], banks[7]
            for b in range(NBLK):
                yield lambda: ready_y[b]
                y = yT[b % 2]
                yield from B.grab()
                for j, yj in enumerate(squares(y)):
                    t = mm(B[:, E1 * j:E1 * (j + 1)], yj, routerT, ready_y[b], *B.free, signal=j == TILES - 1)
                yield
                t = DVE.do(lambda e: e.tensor_copy(
                    rl.ap, B[:, 0:TILES * E1].rearrange("p (t n) -> p t n", t=TILES)), t, *rl.free)
                B.drop(t)
                yield
                for j in range(TILES):
                    t_top = DVE.do(lambda e, j=j: e.max(top1[:, j, :], rl[:, j, :]), t, *top1.free)
                yield
                for j in range(TILES):
                    t = DVE.do(lambda e, j=j: e.max_index(topi1[:, j, :], top1[:, j, :], rl[:, j, :]), t_top)
                t_d = tt(DVE, r1[:, 2, :], top1[:, :, 0], top1[:, :, 1], ALU.subtract, t_top, *r1.free)
                t = DVE.do(lambda e: e.tensor_copy(r1[:, 0:2, :], topi1[:, :, 0:2].rearrange("p t k -> p k t")), t)
                rl.free = (t,)
                top1.free = (t_d, t)
                t_d = act(r1[:, 3, :], r1[:, 2, :], ACT.Tanh, t_d, scale=0.5)
                yield
                i8 = across(iota[:, 0:E1], E1)
                t3 = tt(DVE, R1[:, :, 0, :], i8, bc(r1[:, 0, :], E1), ALU.is_equal, t, *R1.free)
                t4 = tt(DVE, R1[:, :, 1, :], i8, bc(r1[:, 1, :], E1), ALU.is_equal, t)
                t1 = ts(DVE, r1[:, 4, :], r1[:, 3, :], 0.5, ALU.mult, t_d, s2=0.5, op1=ALU.add)
                t2 = ts(DVE, r1[:, 5, :], r1[:, 3, :], -0.5, ALU.mult, t_d, s2=0.5, op1=ALU.add)
                yield
                t = tt(DVE, R1[:, :, 0, :], R1[:, :, 0, :], bc(r1[:, 4, :], E1), ALU.mult, t1, t3)
                t5 = tt(DVE, R1[:, :, 1, :], R1[:, :, 1, :], bc(r1[:, 5, :], E1), ALU.mult, t2, t4)
                yield
                t = tt(DVE, R1[:, :, 2, :], R1[:, :, 0, :], R1[:, :, 1, :], ALU.add, t, t5)
                r1.free = (t,)
                yield
                t = act(chl[:, :, 0:E1].bitcast(F32R), R1[:, :, 2, :], ACT.Copy, t, t_chl0, *chl.free)
                yield
                t = tt(DVE, chl[:, :, LO:LO + E1], R1[:, :, 2, :], chl[:, :, 0:E1], ALU.subtract, t)
                R1.free = (t,)
                yield
                yield from A.grab()
                for j in range(TILES):
                    t1 = turn(A[0:LO + E1, j * P:(j + 1) * P], chl[:, j, :], ident, t, *A.free,
                              signal=j == TILES - 1)
                chl.free = (t1,)
                yield lambda: y_taken[0] >= b - 1
                c = cT[b % 2]
                t = act(c.ap, A[0:LO + E1, :], ACT.Copy, t1, *c.free)
                A.drop(t)
                ready_cT[b] = t
                yield

        spare = [Place(gu_raw.ap.rearrange("p a c h -> p (a c h)")[:, i * BLK:(i + 1) * BLK]) for i in range(5)]
        sg, hp, ffT = spare[0:2], spare[2:4], spare[4]
        hh = dup(2, "hh", [P, BLK], F32R)
        hl = dup(2, "hl", [P, BLK], F32R)
        s_out = semaphore("out_written")
        hidden = {}
        first_made = made[0]
        downed = {}
        ff_copied = [None] * NBLK
        x_last = [None] * NBLK
        turned = [0]

        def scale_expert_inputs():
            for b in range(NBLK):
                yield AHEAD, lambda: ready_cT[b]
                y, c = yT[b % 2], cT[b % 2]
                for e in range(E1):
                    n = made[0]
                    yield AHEAD, lambda: n < first_made + 3 or consumed.get(n - 3)
                    bank = banks[4]
                    zi, hi, lo = z[n % 3], zh[n % 3], zl[n % 3]
                    t_w = mm(bank.ap, sel[0:LO + E1, e, :], c.ap, ready_cT[b], *bank.free)
                    t_z = tt(DVE, zi.ap, y.ap, bank.ap, ALU.mult, t_w, ready_y[b], *zi.free)
                    bank.free = (t_z,)
                    t_hi = act(hi.ap, zi.ap, ACT.Copy, t_z, *hi.free)
                    t_lo = tt(lighter(BLK), lo.ap, zi.ap, hi[:, :].bitcast(F32), ALU.subtract, t_hi, *lo.free)
                    zi.free = (t_lo,)
                    split[n] = (t_hi, t_lo)
                    made[0] += 1
                y.free = (t_z,)
                c.free = (t_w,)
                y_taken[0] += 1

        def gate_and_up():
            m = 0
            yield lambda: len(t_gu) == 8
            for place in spare:
                place.free = tuple(t_gu.values())
            for b in range(NBLK):
                yhi, ylo = yh[b % 2], yl[b % 2]
                yield lambda: ready_yl[b]
                for j in range(CH1):
                    g, u = banks[m % 2], banks[2 + m % 2]
                    s, h, hi, lo = sg[m % 2], hp[m % 2], hh[m % 2], hl[m % 2]
                    yield lambda: (j // 4, 1) in t_gu and (m < 2 or (m - 2) in downed)
                    mm(g.ap, wgu[0][:, 0, j, :], yhi.ap, ready_yl[b], t_gu[j // 4, 0], *g.free, start=True,
                       stop=False, signal=False)
                    mm(g.ap, wgu[1][:, 0, j, :], yhi.ap, start=False, stop=False, signal=False)
                    t_g = mm(g.ap, wgu[0][:, 0, j, :], ylo.ap, start=False, stop=True)
                    n = first_made + E1 * b + j // 2
                    yield lambda: n in split and split[n][1]
                    t_hi, t_lo = split[n]
                    zhi, zlo = zh[n % 3], zl[n % 3]
                    mm(u.ap, wgu[0][:, 1, j, :], zhi.ap, t_hi, t_gu[j // 4, 1], *u.free, start=True, stop=False,
                       signal=False)
                    mm(u.ap, wgu[1][:, 1, j, :], zhi.ap, start=False, stop=False, signal=False)
                    t_u = mm(u.ap, wgu[0][:, 1, j, :], zlo.ap, t_lo, start=False, stop=True)
                    if j % 2:
                        zhi.free = zlo.free = (t_u,)
                        consumed[n] = t_u
                    t = act(s.ap, g.ap, ACT.Silu, t_g, *s.free)
                    g.free = (t,)
                    t = tt(DVE, h.ap, s.ap, u.ap, ALU.mult, t, t_u, *h.free)
                    s.free = u.free = (t,)
                    t_h = act(hi.ap, h.ap, ACT.Copy, t, *hi.free)
                    t_l = tt(lighter(BLK), lo.ap, h.ap, hi[:, :].bitcast(F32), ALU.subtract, t_h, *lo.free)
                    h.free = (t_l,)
                    hidden[m] = (t_h, t_l)
                    m += 1
                    if j == CH1 - 1:
                        yhi.free = ylo.free = (t_g,)
                        g_taken[0] += 1
                    yield AHEAD, lambda: True

        def down():
            dn = banks[5]
            m = 0
            for b in range(NBLK):
                yield lambda: b == 0 or ff_copied[b - 1]
                for j in range(CH1):
                    yield lambda: j // 4 in t_dn and m in hidden and hidden[m][1]
                    t_h, t_l = hidden[m]
                    hi, lo = hh[m % 2], hl[m % 2]
                    first = dn.free if j == 0 else ()
                    mm(dn.ap, wdn[0][:, j, :], hi.ap, t_h, t_dn[j // 4], *first, start=j == 0, stop=False,
                       signal=False)
                    mm(dn.ap, wdn[1][:, j, :], hi.ap, start=False, stop=False, signal=False)
                    t = mm(dn.ap, wdn[0][:, j, :], lo.ap, t_l, start=False, stop=j == CH1 - 1)
                    hi.free = lo.free = (t,)
                    downed[m] = t
                    m += 1
                yield lambda: turned[0] >= b
                t = act(ffT.ap, dn.ap, ACT.Copy, t, *ffT.free)
                dn.free = (t,)
                ff_copied[b] = t
                x_last[b] = t

        def finish():
            for b in range(NBLK):
                yield lambda: x_last[b]
                bank = banks[7]
                yield from bank.grab()
                t = turn_tiles(bank, squares(ffT), x_last[b], *bank.free)
                ffT.free = (t,)
                turned[0] += 1
                yield
                rows = slice(TILES * b, TILES * (b + 1))
                t = tt(DVE, x1[:, rows, :], x1[:, rows, :], bank[:, :].rearrange("p (t f) -> p t f", t=TILES),
                       ALU.add, t)
                bank.drop(t)
                SP.dma(lambda e, rows=rows: e.dma_start(out[rows, :, :].rearrange("b p d -> p b d"), x1[:, rows, :]),
                       (s_out, 16 * (b + 1)), t)
                yield

        fetch(0)
        weave(setup_condition(), normalise_input(), condition(), normalise_output(), split_expert_weights(), choose(), scale_expert_inputs(),
              gate_and_up(), down(), finish())
        SP.do(None, (s_out, 16 * NBLK), signal=False)

        block = ctx.enter_context(nc.Block())

        @block.tensor
        def _(e):
            PE.play(e)

        @block.vector
        def _(e):
            DVE.play(e)

        @block.scalar
        def _(e):
            ACTE.play(e)

        @block.gpsimd
        def _(e):
            POOL.play(e)

        @block.sync
        def _(e):
            SP.play(e)


def layout(np, v):
    f = {k: np.asarray(a) for k, a in v.items()}
    cat = np.concatenate
    z = np.float32(0)

    def rows(a, n):
        return np.broadcast_to(a.reshape(1, -1), (n, a.size))

    def column(a):
        return a.reshape(-1, 1)

    x = f["x"]
    ins = {
        "xT": x.reshape(NTOK, P).T,
        "x_tok": x.transpose(1, 0, 2),
        "p64": cat([f["L0_cond_k_aff_w"].T, f["L0_cond_o_aff_w"].T, f["cond_512"].T], 1),
        "p0": cat([f["L0_cond_k_w"].T, f["L0_cond_o_w"].T, column(f["L0_cond_k_aff_b"]), column(f["L0_cond_k_b"]),
                   column(f["L0_cond_o_aff_b"]), column(f["L0_cond_o_b"]), rows(f["L0_ffn_gates"], P),
                   rows(f["L1_cond_aw"], P), f["L0_ffn_sim_matrix"]], 1),
        "w_qkv": np.stack([f["L0_ffn_q_proj"], f["L0_ffn_k_proj"], f["L0_ffn_v_proj"]], 1)
                   .transpose(2, 0, 1, 3).reshape(P, -1),
        "w_o": f["L0_ffn_o_proj"].transpose(1, 0, 2).reshape(P, -1),
        "w_gu": np.stack([f["L1_ffn_w_gate"].reshape(CH1, P, P), f["L1_ffn_w_up"].reshape(CH1, P, P)], 0)
                  .transpose(3, 0, 1, 2),
        "w_dn": f["L1_ffn_w_down"].reshape(E1, P, 2, P).transpose(3, 0, 2, 1).reshape(P, CH1, P),
    }
    pre = "L1_cond_"
    mlps = ("mem", "noi", "res")
    ins["p1"] = cat(
        [f[pre + "int_W1"].reshape(6, P, P).transpose(1, 0, 2).reshape(P, -1), f[pre + "int_W2"],
         f["L1_ffn_router_w"].T, rows(f[pre + "int_b2"], P)]
        + [f[pre + m + "_W2"] for m in mlps] + [rows(f[pre + m + "_b2"], P) for m in mlps]
        + [column(f[pre + n]) for n in ("int_b1", "int_g", "int_be", "mem_b1", "noi_b1", "res_b1", "mem_g", "mem_be",
                                        "noi_g", "noi_be", "res_g", "res_be")]
        + [f[pre + "cp_b"].T, f[pre + "tm_b"].T, f[pre + "ms_b"].T, np.zeros((P, 8), np.float32)], 1)
    tabs = np.zeros((LO + 8, 3, P), np.float32)
    ids = np.zeros((LO + 8, NTOK), f["itok_BxS_0_4"].dtype)
    for o in (0, LO):
        tabs[o:o + 5, 0], tabs[o:o + 5, 1], tabs[o + 5:o + 8, 2] = f[pre + "cp_g"], f[pre + "tm_g"], f[pre + "ms_g"]
        ids[o:o + 5], ids[o + 5:o + 8] = f["itok_BxS_0_4"].reshape(-1), f["mask_BxS_ik0"].reshape(-1)
    ins["tabs"], ins["ids"] = tabs, ids
    ins["pw"] = cat([f[pre + "pw_g"], f[pre + "pw_b"]], 1)
    ins["tok_ids"] = f["itok_BxS_0_999"].T
    ins["pm64"] = cat([f[pre + "mem_W1"], f[pre + "noi_W1"], f["cond_512"].T, f["cond_64"].T], 1)
    ins["pm32"] = cat([f[pre + "res_W1"], f["fside_Bx32_0"].T], 1)
    ins["c_const"] = cat([np.eye(P), np.ones((P, P)), np.broadcast_to(np.arange(16.0), (P, 16))], 1) \
        .astype(np.float32)
    sel = np.zeros((LO + E0, E0), np.float32)
    sel[np.arange(E0), np.arange(E0)] = sel[LO + np.arange(E0), np.arange(E0)] = 1
    val = np.full((LO + 8, 1), -1, np.float32)
    for o in (0, LO):
        val[o:o + 8, 0] = [0, 1, 2, 3, 4, 0, 1, 2]
    ins["c_sel"], ins["c_idval"] = sel, val
    return {k: np.ascontiguousarray(a) for k, a in ins.items()}


def kernel(**inputs):
    import numpy as np
    import concourse.bacc as bacc
    from concourse.bass_utils import run_bass_kernel_spmd

    nc = bacc.Bacc("TRN2", target_bir_lowering=False, num_devices=1)
    arrays = layout(np, inputs)
    ins = {k: nc.dram_tensor("in_" + k, a.shape, mybir.dt.from_np(a.dtype), kind="ExternalInput").ap()
           for k, a in arrays.items()}
    out = nc.dram_tensor("out_0", (NBATCH, P, P), F32, kind="ExternalOutput").ap()
    build_program(nc, ins, out)
    r = run_bass_kernel_spmd(nc, [{"in_" + k: a for k, a in arrays.items()}], core_ids=[0])
    return r.results[0]["out_0"]
```

```python
from contextlib import ExitStack

import concourse.bass as bass
from concourse import mybir

F32 = mybir.dt.float32
F32R = mybir.dt.float32r
I32 = mybir.dt.int32
U32 = mybir.dt.uint32
ALU = mybir.AluOpType
ACT = mybir.ActivationFunctionType
AX = mybir.AxisListType.X

P = 128
NBATCH = 32
NTOK = NBATCH * P
TILES = 4
BLK = TILES * P
NBLK = NTOK // BLK
HEADS = 16
HD = P // HEADS
E0 = 16
E1 = 8
HID = 256
CH1 = E1 * HID // P
RING = 5
QH = 4
LO = 32
RSQRT_SEED = 0x5F3759DF


class Stream:

    expected = {}
    latest = 0.0

    def __init__(self, sem, fixed=0.0, per=0.0, warms=False, dma=0.1, latency=0.17):
        self.warms, self.warm_at, self.dma_cost, self.latency = warms, WARM_UP, dma, latency
        self.sem, self.count, self.queue = sem, 0, []
        self.fixed, self.per, self.clock = fixed, per, 0.0

    def do(self, call, *after, signal=True, n=16):
        self.queue.append((after, call, signal))
        begin = max([self.clock] + [Stream.expected.get(m, 0.0) + (LATENCY if m[0] is self.sem else self.latency)
                                    for m in after if m is not None])
        slow = 1
        if self.warms:
            if begin > self.clock + 2.0:
                self.warm_at = begin + WARM_UP
            slow = 2 if begin < self.warm_at else 1
        self.clock = begin + (self.fixed + self.per * n) * slow
        if signal:
            self.count += 1
            mark = (self.sem, self.count)
            Stream.expected[mark] = self.clock
            Stream.latest = max(Stream.latest, self.clock)
            return mark
        return None

    def mark(self):
        return (self.sem, self.count)

    def dma(self, call, sem_mark, *after):
        self.queue.append((after, call, sem_mark[0]))
        begin = max([self.clock] + [Stream.expected.get(m, 0.0) for m in after if m is not None])
        self.clock = begin + self.dma_cost
        Stream.expected[sem_mark] = begin + 3.0
        return sem_mark

    def play(self, eng):
        reached = {}
        for after, call, signal in self.queue:
            for m in after:
                if m is not None and m[1] > reached.get(id(m[0]), 0):
                    eng.wait_ge(m[0], m[1])
                    reached[id(m[0])] = m[1]
            if call is None:
                continue
            ins = call(eng)
            if signal is True:
                ins.then_inc(self.sem, 1)
            elif signal is not False:
                ins.then_inc(signal, 16)


class Place:

    def __init__(self, ap):
        self.ap, self.free, self.held = ap, (), False

    def __getitem__(self, key):
        return self.ap[key]

    def grab(self):
        yield lambda: not self.held
        self.held = True

    def drop(self, *marks):
        self.free, self.held = marks, False


WARM_UP = 3.4
LEAD = (0.82, 0.0, 0.0, -0.37, 0.58, -0.01, 0.0, 0.0, 0.0, 0.0,
        -0.04, 0.0, 0.08, 0.0, 1.41, 0.0, 4.02, 0.0, 1.48, 0.53,
        0.0, 4.47, -1.43, 0.0, 0.0, 0.0, 1.96, 1.55, 0.0)
LATENCY = 0.12
AHEAD = "ahead"


def view(ap, offset, dims):
    return bass.AP(ap.tensor, ap.offset + offset, [list(ap.ap[0])] + dims)


def weave(*emitters, lead=()):
    waiting = [[g, 0.0, None, None, n, lead[n] if lead else 0.0] for n, g in enumerate(emitters)]
    while waiting:
        open_now = []
        for w in waiting:
            met = w[2]() if w[2] else True
            if met:
                if met is not True:
                    w[1] = max(w[1], Stream.expected.get(met, 0.0))
                open_now.append(w)
        w = min(open_now, key=lambda w: (max(w[1], w[3].clock if w[3] else 0.0) - w[5], w[4]))
        Stream.latest = w[1]
        said = next(w[0], "end")
        if said == "end":
            waiting.remove(w)
        elif isinstance(said, tuple):
            w[2], w[3] = said[1:]
        elif isinstance(said, Stream):
            w[1], w[2], w[3] = Stream.latest, None, said
        else:
            w[1], w[2], w[3] = Stream.latest, said, None


def build_program(nc, ins, out):
    ctx = ExitStack()
    with ctx:
        region_words = {"heads": 11712, "projections": 15240, "outputs": 9552}
        region = {name: nc.bump_sbuf(4 * words)[0] for name, words in region_words.items()}
        where = [None, 0, 0]

        def sb(name, shape, dt=F32):
            if where[0] is None:
                return Place(ctx.enter_context(nc.sbuf_tensor(name, shape, dt))[:])
            words = 1
            for n in shape[1:]:
                words *= n
            byte = region[where[0]] + 4 * where[1]
            where[1] += -(-words // 8) * 8
            assert where[1] <= region_words[where[0]], (name, where)
            return at_byte(name, shape, dt, byte)

        def at_byte(name, shape, dt, byte):
            place = Place(nc.alloc_sbuf_tensor_at(f"l{where[2]}_{name}", shape, dt, offset=byte)[:])
            place.byte = byte
            return place

        at_word = {}

        def buffers_in(name, layer):
            at_word[where[0], where[2]] = where[1]
            where[:] = [name, at_word.get((name, layer), 0), layer]

        nsem = [0]

        def semaphore(name):
            nsem[0] += 1
            return ctx.enter_context(nc.semaphore(name))

        banks = [Place(ctx.enter_context(nc.psum_tensor(f"bank{i}", [P, 512], F32))[:]) for i in range(8)]

        PE = Stream(semaphore("pe_done"), 0.0, 0.000417, warms=True, latency=0.27)
        DVE = Stream(semaphore("dve_done"), 0.065, 0.00104)
        ACTE = Stream(semaphore("act_done"), 0.1, 0.00083)
        POOL = Stream(semaphore("pool_done"), 0.06, 0.00228, dma=1.04)
        SP = Stream(semaphore("sp_done"))

        def load(name, dst, src, *after):
            return SP.dma(lambda e: e.dma_start(dst, src), (semaphore("ld_" + name), 16), *after)

        def size(ap):
            n = 1
            for _, count in list(ap.ap)[1:]:
                n *= count
            return n

        def mm(dst, lhsT, rhs, *after, start=True, stop=True, signal=True):
            return PE.do(lambda e: e.matmul(dst, lhsT, rhs, start=start, stop=stop), *after, signal=signal,
                         n=size(dst) * (1 if rhs.dtype == F32R else 4))

        def turn(dst, src, eye, *after, signal=True):
            return PE.do(lambda e: e.transpose(dst, src, eye), *after, signal=signal, n=128)

        def turn_tiles(bank, src, t, *after):
            for j in range(TILES):
                m = turn(bank[:, j * P:(j + 1) * P], src[j], ident, t, *after, signal=j == TILES - 1)
            return m

        def tt(S, dst, a, b, op, *after):
            return S.do(lambda e: e.tensor_tensor(dst, a, b, op), *after, n=size(dst))

        def ts(S, dst, a, s1, op0, *after, s2=None, op1=None):
            if op1 is None:
                return S.do(lambda e: e.tensor_scalar(dst, a, s1, None, op0), *after, n=size(dst))
            return S.do(lambda e: e.tensor_scalar(dst, a, s1, s2, op0, op1), *after, n=size(dst))

        def act(dst, a, func, *after, bias=0.0, scale=1.0, accum=None):
            if accum is None:
                return ACTE.do(lambda e: e.activation(dst, a, func, bias=bias, scale=scale), *after,
                               n=size(dst) + (0 if isinstance(scale, float) else 130))
            return ACTE.do(lambda e: e.activation(dst, a, func, bias=bias, scale=scale, accum_out=accum), *after,
                           n=size(dst) + 100)

        def reduce(dst, a, op, *after):
            return DVE.do(lambda e: e.tensor_reduce(dst, a, AX, op), *after, n=size(a))

        def marks_now():
            return tuple(sorted((S.mark() for S in (PE, DVE, ACTE, POOL)), key=lambda m: -Stream.expected.get(m, 0.0)))

        def later(*marks):
            return None if None in marks else max(marks, key=lambda m: Stream.expected.get(m, 0.0))

        def hand_over(places, what):
            for place in places:
                place.free = over[what]

        def lighter(n):
            return DVE if DVE.clock + DVE.per * n + DVE.fixed < POOL.clock + POOL.per * n + POOL.fixed else POOL

        def squares(ap):
            return [ap[:, j * P:(j + 1) * P] for j in range(TILES)]

        def rows_of(ap):
            return [ap[:, j, :] for j in range(TILES)]

        def dup(n, name, shape, dt=F32):
            return [sb(f"{name}{i}", shape, dt) for i in range(n)]

        const = sb("const", [P, 272])
        ident, ones, iota = const[:, 0:128], const[:, 128:256], const[:, 256:272]
        sel_raw = sb("sel_raw", [LO + E0, E0])
        sel = sb("sel", [LO + E0, E0, P], F32R)
        x1 = sb("x1", [P, NBATCH, P])
        p0 = sb("p0", [P, 298])
        aw = sb("aw", [P, 6])
        p1 = sb("p1", [P, 1833])
        tabs_raw = sb("tabs_raw", [LO + 8, 3, P])
        idval = sb("idval", [LO + 8, 1])
        tok_ids = sb("tok_ids", [P, NBATCH], I32)

        z = dup(3, "z", [P, BLK])
        zh = dup(RING, "zh", [P, BLK], F32R)
        zl = dup(RING, "zl", [P, BLK], F32R)
        wT = dup(2, "wT", [LO + E0, BLK], F32R)
        buffers_in("projections", 0)
        p64 = sb("p64", [64, 288])
        over = {}

        ld_const = load("const", const.ap, ins["c_const"])
        ld_p64 = load("p64", p64.ap, ins["p64"])
        ld_p0 = load("p0", p0.ap, ins["p0"])
        buffers_in("heads", 0)
        xT = dup(2, "xT", [P, BLK])
        ld_x = [None] * NBLK

        def load_xT(b):
            dst = xT[b % 2]
            ld_x[b] = load(f"xT{b}", dst.ap, ins["xT"][:, b * BLK:(b + 1) * BLK], *dst.free)

        load_xT(0)
        ld_sel = load("sel", sel_raw.ap, ins["c_sel"])

        buffers_in("projections", 0)
        wqkv = [sb(f"wqkv{h}", [P, E0, 3, P], F32R) for h in ("hi", "lo")]
        buffers_in("outputs", 0)
        wo = [sb(f"wo{h}", [P, E0, P], F32R) for h in ("hi", "lo")]
        buffers_in("heads", 0)
        av = dup(4, "av", [P, QH * HD * HEADS])

        kwT, owT = p0[:, 0:128], p0[:, 128:256]
        k_aff_b, k_b, o_aff_b, o_b = (p0[:, 256 + i:257 + i] for i in range(4))
        gates_rows, aw_rows, sim = p0[:, 260:276], p0[:, 276:282], p0[:, 282:298]

        style = sb("style", [P, 2, NBATCH])
        sq_w = sb("sq_w", [P, 2, P])
        sq_style = sb("sq_style", [P, 2, NBATCH])
        sq_sim = sb("sq_sim", [P, E0])
        norms = sb("norms", [P, 80])
        nrm_tmp = sb("nrm_tmp", [P, 3, 80])
        buffers_in("projections", 0)
        sn = sb("sn", [P, E0])
        sig_gates = sb("sig_gates", [P, 2, E0])
        buffers_in("heads", 0)
        aw_tmp = sb("aw_tmp", [P, 4, 6])

        def rsqrt(S, x, tmp, *after):
            half, a, y = tmp
            t = DVE.do(lambda e: e.tensor_scalar(a.bitcast(I32), x.bitcast(I32), 1, None,
                                                 ALU.logical_shift_right), *after)
            t = ts(DVE, y.bitcast(I32), a.bitcast(I32), -1.0, ALU.mult, t, s2=float(RSQRT_SEED), op1=ALU.add)
            h = ts(S, half, x, -0.5, ALU.mult, t)
            for step in range(3):
                t = tt(S, a, y, y, ALU.mult, t, h)
                t = tt(S, a, a, half, ALU.mult, t)
                t = ts(S, a, a, 1.5, ALU.add, t)
                t = tt(S, x if step == 2 else y, y, a, ALU.mult, t)
            return t

        setup_bank = banks[6]
        for i in range(2):
            t = mm(setup_bank[:, 32 * i:32 * i + 32], p64[:, 128 * i:128 * i + 128], p64[:, 256:288],
                   ld_p64, signal=i == 1)
        for i, b in enumerate((k_aff_b, o_aff_b)):
            t_style = ts(DVE, style[:, i, :], setup_bank[:, 32 * i:32 * i + 32], b, ALU.add, t, ld_p0)
        tt(DVE, sq_w[:, 0, :], kwT, kwT, ALU.mult, ld_p0)
        tt(DVE, sq_w[:, 1, :], owT, owT, ALU.mult)
        tt(DVE, sq_sim.ap, sim, sim, ALU.mult)
        t_sq = tt(DVE, sq_style.ap, style.ap, style.ap, ALU.mult, t_style)
        for i in range(2):
            mm(setup_bank[:, 64 + 32 * i:96 + 32 * i], sq_w[:, i, :], sq_style[:, i, :], t_sq, signal=False)
        t = mm(setup_bank[:, 128:144], ones, sq_sim.ap, ld_const)
        t1 = ts(DVE, norms[:, 0:64], setup_bank[:, 64:128], 1e-8, ALU.add, t)
        t2 = ts(DVE, norms[:, 64:80], setup_bank[:, 128:144], 1e-24, ALU.max, t)
        setup_bank.free = (t2,)
        t_norms = rsqrt(DVE, norms.ap, [nrm_tmp[:, i, :] for i in range(3)], t1, t2)
        demod = [norms[:, 0:32], norms[:, 32:64]]
        t_sn = tt(DVE, sn.ap, sim, norms[:, 64:80], ALU.mult, t_norms)
        t = act(sig_gates[:, 1, :], gates_rows, ACT.Tanh, ld_p0, scale=0.5)
        t_sig = ts(DVE, sig_gates[:, 0, :], sig_gates[:, 1, :], 0.5, ALU.mult, t, s2=0.5, op1=ALU.add)
        t = reduce(aw_tmp[:, 0, 0:1], aw_rows, ALU.max, ld_p0)
        t = ts(DVE, aw_tmp[:, 1, :], aw_rows, aw_tmp[:, 0, 0:1], ALU.subtract, t)
        t = act(aw_tmp[:, 2, :], aw_tmp[:, 1, :], ACT.Exp, t, accum=aw_tmp[:, 3, 0:1])
        t = DVE.do(lambda e: e.reciprocal(aw_tmp[:, 3, 1:2], aw_tmp[:, 3, 0:1]), t)
        t_aw = ts(DVE, aw.ap, aw_tmp[:, 2, :], aw_tmp[:, 3, 1:2], ALU.mult, t)
        t_sel = DVE.do(lambda e: e.tensor_copy(
            sel.ap, sel_raw[:, :].unsqueeze(2).broadcast_to([LO + E0, E0, P])), ld_sel)

        xsT = sb("xsT", [P, BLK])
        kT = osT = sb("kT", [P, BLK])
        kks = dup(2, "kk", [P, TILES, 2 * P])
        prod = sb("prod", [P, 9, P])
        dbl = sb("dbl", [P, TILES, 7, 32])
        scs = dup(2, "sc", [P, TILES, HEADS, HEADS])
        mx = sb("mx", [P, TILES, HEADS])
        dens = dup(2, "den", [P, TILES, HEADS])
        osum = sb("osum", [P, TILES, P])
        buffers_in("projections", 0)
        x0T = dup(3, "x0T", [P, BLK])
        buffers_in("outputs", 0)
        x0sq = pT = sb("pT", [P, BLK])
        w_tok = dup(3, "w_tok", [P, TILES, E0])
        buffers_in("projections", 0)
        lg = sb("lg", [P, TILES, E0 + 1])
        rt = sb("rt", [P, TILES, 8, E0])
        rs = sb("rs", [P, 8, TILES])
        top = sb("top", [P, TILES, 8])
        topi = sb("topi", [P, TILES, 8], U32)
        whl = dup(2, "whl", [P, TILES, LO + E0])
        ready_x0T = [None] * NBLK
        ready_w = [None] * NBLK
        ready_wT = [None] * NBLK
        t_whl0 = [POOL.do(lambda e, w=w: e.memset(w.ap, 0.0)) for w in whl]

        def bc(ap, n):
            return ap.unsqueeze(2).broadcast_to([P, TILES, n])

        def across(ap, n):
            return ap.unsqueeze(1).broadcast_to([P, TILES, n])

        spread, scaled, rounded, split, consumed = {}, {}, {}, {}, {}
        x0_taken = [0]
        qkv_done = [None] * NBLK
        qkv_copied = [None] * NBLK
        o_ready = [None] * NBLK
        x1_done = [None] * NBLK
        ready_expert = {}

        head_weights = [None] * NBLK
        heads_done = [0]

        def head_scores():
            for b in range(NBLK):
                s1 = banks[7]
                yield lambda: heads_done[0] >= b - 1
                kk, sc, den = kks[b % 2], scs[b % 2], dens[b % 2]
                src = xT[b % 2]
                t_x = None
                for j in range(TILES):
                    col = TILES * b + j
                    t_x = act(xsT[:, j * P:(j + 1) * P], src[:, j * P:(j + 1) * P], ACT.Copy, ld_x[b], t_style,
                              *xsT.free, scale=style[:, 0, col:col + 1])
                src.free = (t_x,)
                if b + 1 < NBLK:
                    load_xT(b + 1)
                yield
                yield from s1.grab()
                t = mm(s1.ap, kwT, xsT.ap, t_x, *s1.free)
                xsT.free = (t,)
                yield ACTE
                for j in range(TILES):
                    col = TILES * b + j
                    t = act(kT[:, j * P:(j + 1) * P], s1[:, j * P:(j + 1) * P], ACT.Identity, t, t_norms, *kT.free,
                            scale=demod[0][:, col:col + 1], bias=k_b)
                yield PE
                t = turn_tiles(s1, squares(kT), t, ld_const)
                kT.free = (t,)
                yield ACTE
                s1v = s1[:, :].rearrange("p (t f) -> p t f", t=TILES)
                act(kk[:, :, 0:P], s1v, ACT.Copy, t, *kk.free)
                t_kk = act(kk[:, :, P:2 * P], s1v, ACT.Copy)
                s1.drop(t_kk)
                yield DVE
                for j in range(TILES):
                    k0 = kk[:, j, 0:P]
                    t = tt(DVE, prod.ap, view(k0, 0, [[0, 9], [1, P]]), view(k0, 0, [[HD, 9], [1, P]]), ALU.mult,
                           t_kk, *prod.free)
                    yield DVE
                    t_sc = reduce(sc[:, j, 0:9, :], prod[:, :, :].rearrange("p r (h d) -> p r h d", d=HD), ALU.add,
                                  t, *sc.free)
                    prod.free = (t_sc,)
                    yield ACTE
                act(dbl[:, :, :, 0:HEADS], sc[:, :, 1:8, :], ACT.Copy, t_sc, *dbl.free)
                t = act(dbl[:, :, :, HEADS:], sc[:, :, 1:8, :], ACT.Copy)
                yield ACTE
                t = act(sc[:, :, 9:16, :], view(dbl.ap, 6 * 32 + 9, [[7 * 32, TILES], [-31, 7], [1, HEADS]]),
                        ACT.Copy, t)
                dbl.free = (t,)
                yield DVE
                t = reduce(mx.ap, sc[:, :, :, :].rearrange("p t s h -> p t h s"), ALU.max, t, *mx.free)
                yield DVE
                t = tt(DVE, sc.ap, sc.ap, view(mx.ap, 0, [[HEADS, TILES], [0, HEADS], [1, HEADS]]), ALU.subtract, t)
                mx.free = (t,)
                yield ACTE
                t_e = act(sc.ap, sc.ap, ACT.Exp, t, scale=HD ** -0.5)
                yield DVE
                t = reduce(den.ap, sc[:, :, :, :].rearrange("p t s h -> p t h s"), ALU.add, t_e, *den.free)
                t_den = DVE.do(lambda e, den=den: e.reciprocal(den.ap, den.ap), t)
                head_weights[b] = (t_e, t_kk, t_den)
                yield

        def head_values():
            for b in range(NBLK):
                yield lambda: head_weights[b] and head_weights[b][0]
                s1 = banks[7]
                kk, sc, den = kks[b % 2], scs[b % 2], dens[b % 2]
                t_e, t_kk, t_den = head_weights[b]
                pending, last = [], {}

                def add_shifts(q, j, h0, t_q):
                    t = reduce(osum[:, j, HD * h0:HD * (h0 + QH)].rearrange("p (h d) -> p h d", d=HD),
                               q[:, :].rearrange("p (h s d) -> p h d s", s=HEADS, d=HD), ALU.add, t_q, *osum.free)
                    q.free = (t,)
                    return t

                def multiply(n):
                    j, h0, q = QH * n // HEADS, QH * n % HEADS, av[n % 4]
                    a = view(sc[:, j, 0, h0:h0 + 1], 0, [[1, QH], [HEADS, HEADS], [0, HD]])
                    v = view(kk[:, j, HD * h0:HD * h0 + 1], 0, [[HD, QH], [HD, HEADS], [1, HD]])
                    q4 = q[:, :].rearrange("p (h s d) -> p h s d", h=QH, d=HD)
                    S = lighter(QH * HD * HEADS) if b == 0 else POOL
                    last[S] = tt(S, q4, a, v, ALU.mult, t_e, t_kk, *q.free)
                    pending.append((q, j, h0, last[S]))

                steps = TILES * HEADS // QH
                for n in range(3):
                    multiply(n)
                for n in range(steps):
                    yield lambda: pending[0][3]
                    t = add_shifts(*pending.pop(0))
                    if n + 3 < steps:
                        multiply(n + 3)
                sc.free = kk.free = tuple(last.values())
                heads_done[0] += 1
                yield DVE
                on = osum[:, :, :].rearrange("p t (h d) -> p t h d", d=HD)
                t = tt(DVE, on, on, den[:, :, :].unsqueeze(3).broadcast_to([P, TILES, HEADS, HD]), ALU.mult, t,
                       t_den)
                den.free = (t,)
                yield
                yield from s1.grab()
                t = turn_tiles(s1, rows_of(osum), t, *s1.free)
                osum.free = (t,)
                yield ACTE
                for j in range(TILES):
                    col = TILES * b + j
                    t = act(osT[:, j * P:(j + 1) * P], s1[:, j * P:(j + 1) * P], ACT.Copy, t, *osT.free,
                            scale=style[:, 1, col:col + 1])
                yield PE
                t = mm(s1.ap, owT, osT.ap, t)
                osT.free = (t,)
                yield lambda: x0_taken[0] >= b - 2
                x0 = x0T[b % 3]
                for j in range(TILES):
                    col = TILES * b + j
                    t = act(x0[:, j * P:(j + 1) * P], s1[:, j * P:(j + 1) * P], ACT.Identity, t, *x0.free,
                            scale=demod[1][:, col:col + 1], bias=o_b)
                s1.drop(t)
                ready_x0T[b] = t
                if b == NBLK - 1:
                    over["heads"] = marks_now()
                yield

        def route():
            for b in range(NBLK):
                yield lambda: ready_x0T[b]
                bank = banks[6]
                x0 = x0T[b % 3]
                t_x0 = ready_x0T[b]
                yield from bank.grab()
                t = act(x0sq.ap, x0.ap, ACT.Square, t_x0, *x0sq.free)
                yield
                for j in range(TILES):
                    mm(bank[:, 32 * j:32 * j + E0], x0[:, j * P:(j + 1) * P], sn.ap, t, t_sn, *bank.free,
                       signal=False)
                    t_l = mm(bank[:, 32 * j + E0:32 * j + E0 + 1], x0sq[:, j * P:(j + 1) * P], ones[:, 0:1], t,
                             signal=j == TILES - 1)
                x0sq.free = (t_l,)
                yield DVE
                t = DVE.do(lambda e: e.tensor_copy(
                    lg.ap, bank[:, 0:128].rearrange("p (t n) -> p t n", t=TILES)[:, :, 0:E0 + 1]), t_l, *lg.free)
                bank.drop(t)
                yield DVE
                r = [rs[:, i, :] for i in range(8)]
                t = ts(DVE, r[0], lg[:, :, E0], 1e-24, ALU.max, t, *rs.free)
                yield DVE
                half, a, y = r[1], r[2], r[3]
                t1 = DVE.do(lambda e: e.tensor_scalar(a.bitcast(I32), r[0].bitcast(I32), 1, None,
                                                      ALU.logical_shift_right), t)
                ts(DVE, half, r[0], -0.5, ALU.mult, t)
                yield DVE
                t = ts(DVE, y.bitcast(I32), a.bitcast(I32), -1.0, ALU.mult, t1, s2=float(RSQRT_SEED), op1=ALU.add)
                yield DVE
                for step in range(3):
                    t = tt(DVE, a, y, y, ALU.mult, t)
                    yield DVE
                    t = tt(DVE, a, a, half, ALU.mult, t)
                    yield DVE
                    t = DVE.do(lambda e: e.scalar_tensor_tensor(out=y, in0=a, scalar=1.5, in1=y, op0=ALU.add,
                                                                op1=ALU.mult), t)
                    yield DVE
                R = [rt[:, :, i, :] for i in range(8)]
                t = tt(DVE, R[0], lg[:, :, 0:E0], bc(y, E0), ALU.mult, t, *rt.free)
                lg.free = (t,)
                yield DVE
                t_log = tt(DVE, R[0], R[0], across(sig_gates[:, 0, :], E0), ALU.subtract, t, t_sig)
                yield DVE
                for j in range(TILES):
                    t_top = DVE.do(lambda e, j=j: e.max(top[:, j, :], R[0][:, j, :]), t_log, *top.free)
                yield DVE
                for j in range(TILES):
                    t = DVE.do(lambda e, j=j: e.max_index(topi[:, j, :], top[:, j, :], R[0][:, j, :]), t_top)
                t_i = ts(DVE, r[6], top[:, :, 0], 0.0, ALU.is_le, t_top)
                t_g = ts(DVE, r[7], top[:, :, 0], 0.0, ALU.max, t_top)
                t = DVE.do(lambda e: e.tensor_copy(rs[:, 4:6, :], topi[:, :, 0:2].rearrange("p t k -> p k t")), t)
                top.free = (t_g, t)
                yield DVE
                t1 = tt(DVE, R[1], across(iota, E0), bc(r[4], E0), ALU.is_equal, t)
                t2 = tt(DVE, R[2], across(iota, E0), bc(r[5], E0), ALU.is_equal, t)
                t4 = DVE.do(lambda e: e.scalar_tensor_tensor(out=R[4], in0=R[0], scalar=0.0, in1=bc(r[7], E0),
                                                             op0=ALU.max, op1=ALU.subtract), t_g, n=64)
                t_e = act(R[5], R[4], ACT.Exp, t4)
                yield DVE
                t = tt(DVE, R[1], R[1], R[2], ALU.add, t1, t2)
                yield DVE
                t = tt(DVE, R[1], R[1], bc(r[6], E0), ALU.mult, t, t_i)
                yield DVE
                t_m = DVE.do(lambda e: e.scalar_tensor_tensor(out=R[1], in0=R[0], scalar=0.0, in1=R[1],
                                                              op0=ALU.is_gt, op1=ALU.add), t, n=64)
                yield DVE
                t = tt(DVE, R[5], R[5], R[1], ALU.mult, t_e, t_m)
                yield DVE
                t = reduce(r[1], R[5], ALU.add, t)
                yield DVE
                t = DVE.do(lambda e: e.reciprocal(r[2], r[1]), t)
                yield lambda: b < 3 or o_ready[b - 3]
                w = w_tok[b % 3]
                t = t_w = tt(DVE, w.ap, R[5], bc(r[2], E0), ALU.mult, t, *w.free)
                rt.free = rs.free = (t,)
                wp = whl[b % 2]
                yield ACTE
                t = act(wp[:, :, 0:E0].bitcast(F32R), w.ap, ACT.Copy, t, t_whl0[b % 2], *wp.free)
                yield DVE
                t = tt(DVE, wp[:, :, LO:LO + E0], w.ap, wp[:, :, 0:E0], ALU.subtract, t)
                yield
                yield from bank.grab()
                for j in range(TILES):
                    t1 = turn(bank[0:LO + E0, j * P:(j + 1) * P], wp[:, j, :], ident, t, *bank.free,
                              signal=j == TILES - 1)
                wp.free = (t1,)
                yield lambda: x0_taken[0] >= b - 1
                wst = wT[b % 2]
                t = act(wst.ap, bank[0:LO + E0, :], ACT.Copy, t1, *wst.free)
                bank.drop(t)
                ready_w[b] = t_w
                ready_wT[b] = t
                yield

        def spread_weights(wide, rows, weights, first, n_experts, pair):
            n = first
            for b in range(NBLK):
                for e in range(n_experts):
                    yield AHEAD, lambda: weights[b] and (n < first + len(pair) or scaled.get(n - len(pair))), PE
                    bank, w = pair[n % len(pair)], wide[b % 2]
                    spread[n] = mm(bank.ap, sel[rows, e, :], w[rows, :], weights[b], t_sel, *bank.free)
                    n += 1
                w.free = (spread[n - 1],)

        def scale_inputs(xs, ready, first, n_experts, pair, taken):
            n = first
            for b in range(NBLK):
                for e in range(n_experts):
                    yield AHEAD, lambda: (n < 3 or n - 3 in split) and spread.get(n), DVE
                    bank, zi, x = pair[n % len(pair)], z[n % 3], xs[b % len(xs)]
                    scaled[n] = tt(DVE, zi.ap, x.ap, bank.ap, ALU.mult, spread[n], ready[b], *zi.free)
                    bank.free = (scaled[n],)
                    n += 1
                x.free = (scaled[n - 1],)
                taken[0] += 1

        def round_inputs(first, count):
            for n in range(first, first + count):
                yield AHEAD, lambda: (n < RING or n - RING in consumed) and scaled.get(n), ACTE
                zi, hi = z[n % 3], zh[n % RING]
                rounded[n] = act(hi.ap, zi.ap, ACT.Copy, scaled[n], *hi.free)

        def rest_of_inputs(first, count):
            for n in range(first, first + count):
                yield AHEAD, lambda: rounded.get(n), POOL
                zi, hi, lo = z[n % 3], zh[n % RING], zl[n % RING]
                t_lo = tt(POOL, lo.ap, zi.ap, hi[:, :].bitcast(F32), ALU.subtract, rounded[n], *lo.free)
                zi.free = (t_lo,)
                split[n] = t_lo

        def project():
            n = 0
            for b in range(NBLK):
                yield lambda: b == 0 or qkv_copied[b - 1]
                for e in range(E0):
                    yield AHEAD, lambda: ready_expert.get(e) and rounded.get(n), PE
                    hi, lo = zh[n % RING], zl[n % RING]
                    for i in range(3):
                        first = banks[i].free if e == 0 else ()
                        mm(banks[i].ap, wqkv[0][:, e, i, :], hi.ap, rounded[n], ready_expert[e], *first,
                           start=e == 0, stop=False, signal=False)
                        mm(banks[i].ap, wqkv[1][:, e, i, :], hi.ap, start=False, stop=False, signal=False)
                    yield AHEAD, lambda: split.get(n), PE
                    for i in range(3):
                        t = mm(banks[i].ap, wqkv[0][:, e, i, :], lo.ap, split[n], start=False, stop=e == E0 - 1,
                               signal=i == 2)
                    hi.free = lo.free = (t,)
                    consumed[n] = t
                    n += 1
                qkv_done[b] = t

        buffers_in("outputs", 0)
        qT = dup(3, "qT", [P, BLK])
        pexp = sb("pexp", [P, TILES, P])
        stage = [*qT, Place(pexp.ap.rearrange("p t s -> p (t s)"))]
        v_tok = sb("v_tok", [P, TILES, P])
        oh = dup(2, "oh", [P, BLK], F32R)
        ol = dup(2, "ol", [P, BLK], F32R)
        sm = sb("sm", [P, 4, TILES])
        w_out = dup(2, "w_out", [P, TILES, E0])
        ld_x1 = load("x1", x1.ap, ins["x_tok"])
        w_out_done = [None] * NBLK

        def row_attention():
            for b in range(NBLK):
                at = banks[6]
                yield lambda: qkv_done[b] and ready_expert.get("o")
                if b == 0:
                    pexp.free = stage[3].free
                for i in range(3):
                    t = act(qT[i].ap, banks[i].ap, ACT.Copy, qkv_done[b], *qT[i].free)
                    banks[i].free = (t,)
                qkv_copied[b] = t
                if b == NBLK - 1:
                    over["projections"] = marks_now()
                yield
                yield from at.grab()
                for j, (q, k) in enumerate(zip(squares(qT[0]), squares(qT[1]))):
                    t1 = mm(at[:, j * P:(j + 1) * P], q, k, t, *at.free, signal=j == TILES - 1)
                qT[0].free = qT[1].free = (t1,)
                av4 = at[:, :].rearrange("p (t s) -> p t s", t=TILES)
                yield DVE
                t = reduce(sm[:, 0, :], av4, ALU.max, t1, *sm.free)
                yield DVE
                t = ts(DVE, sm[:, 1, :], sm[:, 0, :], -P ** -0.5, ALU.mult, t)
                yield ACTE
                for j in range(TILES):
                    t = act(pexp[:, j, :], av4[:, j, :], ACT.Exp, t, *pexp.free, scale=P ** -0.5,
                            bias=sm[:, 1, j:j + 1], accum=sm[:, 2, j:j + 1])
                yield DVE
                t1 = DVE.do(lambda e: e.reciprocal(sm[:, 3, :], sm[:, 2, :]), t)
                t = turn_tiles(at, rows_of(pexp), t)
                pexp.free = (t,)
                yield lambda: b < 2 or x1_done[b - 2]
                w = w_tok[b % 3]
                t_w = tt(DVE, w_out[b % 2].ap, w.ap, bc(sm[:, 3, :], E0), ALU.mult, t1, ready_w[b],
                         *w_out[b % 2].free)
                w.free = sm.free = (t_w,)
                t = act(pT.ap, at.ap, ACT.Copy, t, *pT.free)
                yield PE
                t = turn_tiles(at, squares(qT[2]), t)
                qT[2].free = (t,)
                yield ACTE
                t = act(v_tok[:, :, :].rearrange("p t h -> p (t h)"), at.ap, ACT.Copy, t, *v_tok.free)
                yield PE
                for j, pj in enumerate(squares(pT)):
                    t1 = mm(at[:, j * P:(j + 1) * P], v_tok[:, j, :], pj, t, signal=j == TILES - 1)
                pT.free = v_tok.free = (t1,)
                yield ACTE
                hi, lo = oh[b % 2], ol[b % 2]
                t = act(hi.ap, at.ap, ACT.Copy, t1, *hi.free)
                yield DVE
                t = tt(DVE, lo.ap, at.ap, hi[:, :].bitcast(F32), ALU.subtract, t, *lo.free)
                at.drop(t)
                w_out_done[b] = t_w
                o_ready[b] = t
                yield

        def project_out():
            for b in range(NBLK):
                yield lambda: o_ready[b] and "o" in ready_expert
                if b == NBLK - 1:
                    yield lambda: over["projections"][0]
                hi, lo, w = oh[b % 2], ol[b % 2], w_out[b % 2]
                for j in range(TILES):
                    acc = x1[:, TILES * b + j, :]
                    c = slice(j * P, (j + 1) * P)
                    t_acc = ld_x1
                    for g in range(E0 // 4):
                        es = slice(4 * g, 4 * g + 4)
                        ob = banks[3] if b == NBLK - 1 and g % 2 else banks[5]
                        mm(ob.ap, hi[:, c], wo[0][:, es, :], o_ready[b], *ob.free, ready_expert["o"], start=True,
                           stop=False, signal=False)
                        mm(ob.ap, hi[:, c], wo[1][:, es, :], start=False, stop=False, signal=False)
                        t_o = mm(ob.ap, lo[:, c], wo[0][:, es, :], start=False, stop=True)
                        yield DVE
                        for k in range(4):
                            ee = 4 * g + k
                            t_acc = DVE.do(lambda e, k=k, ee=ee, acc=acc, j=j, w=w, ob=ob: e.scalar_tensor_tensor(
                                out=acc, in0=ob[:, k * P:(k + 1) * P], scalar=w[:, j, ee:ee + 1], in1=acc,
                                op0=ALU.mult, op1=ALU.add), t_o, t_acc, w_out_done[b], n=190)
                        ob.free = (t_acc,)
                        yield
                hi.free = lo.free = (t_o,)
                w.free = (t_acc,)
                x1_done[b] = t_acc
            over["outputs"] = marks_now()

        def split_weights():
            n = 0
            for name, src, hl, cols in (("qkv", ins["w_qkv"], wqkv, E0 * 3 * P), ("o", ins["w_o"], wo, E0 * P)):
                flat = [h.ap.rearrange("p e i h -> p (e i h)") if name == "qkv" else
                        h.ap.rearrange("p e h -> p (e h)") for h in hl]
                step = 3 * P if name == "qkv" else 4 * P
                for c in range(0, cols, step):
                    s = stage[n % 4]
                    n += 1
                    t = load(f"{name}{c}", s[:, 0:step], src[:, c:c + step], *s.free)
                    t = act(flat[0][:, c:c + step], s[:, 0:step], ACT.Copy, t)
                    t = tt(POOL, flat[1][:, c:c + step], s[:, 0:step], flat[0][:, c:c + step].bitcast(F32),
                           ALU.subtract, t)
                    s.free = (t,)
                    if name == "qkv":
                        ready_expert[c // step] = t
                    elif c + step == cols:
                        ready_expert["o"] = t
                    yield

        ld_p1 = load("p1", p1.ap, ins["p1"])
        ld_tabs = load("tabs", tabs_raw.ap, ins["tabs"])
        ld_idval = load("idval", idval.ap, ins["c_idval"])
        ld_tok = load("tok", tok_ids.ap, ins["tok_ids"])

        buffers_in("projections", 1)
        wgu = [sb(f"wgu{h}", [P, 2, CH1, P], F32R) for h in ("hi", "lo")]
        wdn = [sb(f"wdn{h}", [P, CH1, P], F32R) for h in ("hi", "lo")]
        gu_raw = at_byte("gu_raw", [P, 2, CH1, P], F32, wgu[1].byte)
        dn_raw = at_byte("dn_raw", [P, CH1, P], F32, wdn[1].byte)
        buffers_in("heads", 1)
        W1 = p1[:, 0:768].rearrange("p (k o) -> p k o", k=6)
        W2, routerT, b2_rows = p1[:, 768:896], p1[:, 896:904], p1[:, 904:1032]
        mlp_W2 = [p1[:, 1032 + 128 * i:1160 + 128 * i] for i in range(3)]
        mlp_b2 = [p1[0:NBATCH, 1416 + 128 * i:1544 + 128 * i] for i in range(3)]
        col = {n: p1[:, 1800 + i:1801 + i] for i, n in enumerate(
            ("int_b1", "int_g", "int_be", "b1_0", "b1_1", "b1_2", "g_0", "be_0", "g_1", "be_1", "g_2", "be_2"))}
        cp_bT, tm_bT, ms_bT = p1[:, 1812:1817], p1[:, 1817:1822], p1[:, 1822:1825]

        pm64 = sb("pm64", [64, 320])
        pm32 = sb("pm32", [32, 160])
        ld_cond = {}
        cond_in = [(pm64[:, 0:128], pm64[:, 256:288], 0), (pm64[:, 128:256], pm64[:, 288:320], 0),
                   (pm32[:, 0:128], pm32[:, 128:160], 1)]

        mlp_h = sb("mlp_h", [P, 3, NBATCH])
        mlp_o = sb("mlp_o", [NBATCH, 3, P])
        mlp_st = sb("mlp_st", [NBATCH, 3, 6])
        mlp_mv = sb("mlp_mv", [NBATCH, 3, 2])
        mlp_var = sb("mlp_var", [NBATCH, 4, 3])
        mlp_T = sb("mlp_T", [P, 3, NBATCH])
        W1w = W1
        Wx = sb("Wx", [P, P])
        base = sb("base", [P, NBATCH])
        tabT = sb("tabT", [P, 3, LO + 8])
        s1T = sb("s1T", [P, BLK])
        tabs = [sb("tabs_hl", [LO + 8, 4, P], F32R),
                at_byte("tabs_tmp", [LO + 8, 4, P], F32R, s1T.byte)]
        bias_raw = sb("bias_raw", [LO + 8, P])

        marks = {}

        def setup_condition():
            yield lambda: over["heads"][0] if "heads" in over else None
            hand_over([pm64, pm32, mlp_h, mlp_o, mlp_st, mlp_mv, mlp_var, mlp_T, Wx, base, tabT, s1T, tabs[0],
                       bias_raw], "heads")
            ld_cond[0] = load("pm64", pm64.ap, ins["pm64"], *over["heads"])
            ld_cond[1] = load("pm32", pm32.ap, ins["pm32"], *over["heads"])
            for S in (PE, DVE, ACTE, POOL):
                S.do(None, *over["heads"], signal=False)
            for k in range(6):
                t = ts(DVE, W1w[:, k, :], W1[:, k, :], aw[:, k:k + 1], ALU.mult, t_aw, ld_p1)
            t = tt(DVE, Wx.ap, W1w[:, 2, :], W1w[:, 3, :], ALU.add, t)
            marks['W1'] = tt(DVE, Wx.ap, Wx.ap, W1w[:, 4, :], ALU.add, t)
            yield PE
            sb_bank = banks[7]
            yield from sb_bank.grab()
            for i, (w, s, ld) in enumerate(cond_in):
                t = mm(sb_bank[:, 32 * i:32 * i + 32], w, s, ld_cond[ld], *sb_bank.free, signal=i == 2)
            yield ACTE
            for i in range(3):
                t = act(mlp_h[:, i, :], sb_bank[:, 32 * i:32 * i + 32], ACT.Silu, t, ld_p1, bias=col[f"b1_{i}"])
            for i in range(3):
                t = mm(sb_bank[0:NBATCH, 128 * i:128 * i + 128], mlp_h[:, i, :], mlp_W2[i], t, signal=i == 2) or t
            yield DVE
            for i in range(3):
                t = tt(DVE, mlp_o[:, i, :], sb_bank[0:NBATCH, 128 * i:128 * i + 128], mlp_b2[i], ALU.add, t)
            for i in range(3):
                t = DVE.do(lambda e, i=i: e.bn_stats(mlp_st[:, i, :], mlp_o[:, i, :]), t)
            for i in range(3):
                t = DVE.do(lambda e, i=i: e.bn_aggr(mlp_mv[:, i, :], mlp_st[:, i, :]), t)
            yield DVE
            t = ts(DVE, mlp_var[:, 0, :], mlp_mv[:, :, 1], 1e-5, ALU.add, t)
            t = rsqrt(DVE, mlp_var[:, 0, :], [mlp_var[:, 1 + i, :] for i in range(3)], t)
            for i in range(3):
                t = ts(DVE, mlp_o[:, i, :], mlp_o[:, i, :], mlp_mv[:, i, 0:1], ALU.subtract, t,
                       s2=mlp_var[:, 0, i:i + 1], op1=ALU.mult)
            yield PE
            for i in range(3):
                t = PE.do(lambda e, i=i: e.transpose(sb_bank[:, 32 * i:32 * i + 32], mlp_o[:, i, :],
                                                     ident[0:NBATCH, 0:NBATCH]), t, signal=i == 2) or t
            yield ACTE
            for i in range(3):
                t = act(mlp_T[:, i, :], sb_bank[:, 32 * i:32 * i + 32], ACT.Identity, t, scale=col[f"g_{i}"],
                        bias=col[f"be_{i}"])
            for i in range(3):
                t = mm(sb_bank[:, 0:NBATCH], W1w[:, 2 + i, :], mlp_T[:, i, :], t, marks['W1'], start=i == 0, stop=i == 2,
                       signal=i == 2) or t
            marks['base'] = ts(DVE, base.ap, sb_bank[:, 0:NBATCH], col["int_b1"], ALU.add, t)
            yield POOL
            t = POOL.do(lambda e: e.memset(tabT.ap, 0.0))
            for k, (src, at, n) in enumerate(((cp_bT, 0, 5), (tm_bT, 0, 5), (ms_bT, 5, 3))):
                for o in (0, LO):
                    t = DVE.do(lambda e, k=k, src=src, at=at, n=n, o=o: e.tensor_copy(
                        tabT[:, k, o + at:o + at + n], src), t, ld_p1)
            for k, i in enumerate((0, 1, 5)):
                t = mm(sb_bank[0:LO + 8, 128:256], tabT[:, k, :], W1w[:, i, :], t, marks['W1'], marks['base'], start=k == 0, stop=k == 2,
                       signal=k == 2) or t
            t = DVE.do(lambda e: e.tensor_copy(bias_raw.ap, sb_bank[0:LO + 8, 128:256]), t)
            sb_bank.drop(t)
            yield DVE
            raws = [tabs_raw[:, k, :] for k in range(3)] + [bias_raw.ap]
            t_hi = t
            for k in range(4):
                t_hi = DVE.do(lambda e, k=k: e.tensor_copy(tabs[0][:, k, :], raws[k]), t, ld_tabs)
            for k in range(4):
                t1 = DVE.do(lambda e, k=k: e.tensor_copy(tabs[1][:, k, :], raws[k]), t_hi)
            for k in range(4):
                marks['tabs'] = tt(DVE, tabs[0][LO:LO + 8, k, :], raws[k][LO:LO + 8, :],
                            tabs[1][LO:LO + 8, k, :].bitcast(F32), ALU.subtract, t1)
            s1T.free = (marks['tabs'],)
        t_gu, t_dn = {}, {}

        def split_expert_weights():
            yield lambda: over["projections"][0] if "projections" in over else None
            parts = []
            for g in range(4):
                c = slice(4 * g, 4 * g + 4)
                for i in range(2):
                    t = load(f"gu{g}{i}", gu_raw[:, i, c, :], ins["w_gu"][:, i, c, :],
                             *over["projections"])
                    parts.append((t_gu, (g, i), gu_raw[:, i, c, :], wgu[0][:, i, c, :], wgu[1][:, i, c, :], t))
                t = load(f"dn{g}", dn_raw[:, c, :], ins["w_dn"][:, c, :], *over["projections"])
                parts.append((t_dn, g, dn_raw[:, c, :], wdn[0][:, c, :], wdn[1][:, c, :], t))
            for n, (done, key, raw, hi, lo, t) in enumerate(parts):
                yield lambda: t
                t = act(hi, raw, ACT.Copy, t, *over["projections"])
                S = POOL if n % 2 else DVE
                yield AHEAD, lambda: t, S
                done[key] = tt(S, lo, raw, hi.bitcast(F32), ALU.subtract, t)

        ids = dup(2, "ids", [LO + 8, BLK], I32)
        onehots = [at_byte(f"onehot{i}", [LO + 8, BLK], F32R, place.byte) for i, place in enumerate(ids)]
        pw = dup(2, "pw", [P, TILES, 2 * P])
        scratch_in, scratch_out = ([sb(f"stats{i}", [P, TILES, 6]), sb(f"mean_var{i}", [P, TILES, 2]),
                                    sb(f"rstd{i}", [P, 4, TILES])] for i in range(2))
        z1s = dup(2, "xn", [P, TILES, P])
        z2s = dup(2, "pn", [P, TILES, P])
        fT = dup(3, "fT", [P, BLK])
        gT = [fT[0], fT[1], sb("gT", [P, BLK])]
        h2s = dup(2, "h2", [P, TILES, P])
        buffers_in("projections", 1)
        yT = [sb("yT0", [P, BLK])]
        yh = dup(2, "yh", [P, BLK], F32R)
        yl = dup(2, "yl", [P, BLK], F32R)
        buffers_in("heads", 1)
        yT.append(sb("yT1", [P, BLK]))
        rl = sb("rl", [P, TILES, E1])
        top1 = sb("top1", [P, TILES, 8])
        topi1 = sb("topi1", [P, TILES, 8], U32)
        r1 = sb("r1", [P, 6, TILES])
        R1 = sb("R1", [P, TILES, 3, E1])
        chl = sb("chl", [P, TILES, LO + E1])
        ready_y = [None] * NBLK
        ready_yl = [None] * NBLK
        ready_cT = [None] * NBLK
        ld_ids, ld_pw = [None] * NBLK, [None] * NBLK

        def fetch(b):
            if b >= NBLK:
                return
            ld_ids[b] = load(f"ids{b}", ids[b % 2].ap, ins["ids"][:, b * BLK:(b + 1) * BLK], *ids[b % 2].free)
            s = semaphore(f"ld_pw{b}")
            for j in range(TILES):
                c = TILES * b + j
                ld_pw[b] = POOL.dma(lambda e, j=j, c=c: e.indirect_dma_start(
                    pw[b % 2][:, j, :], None, ins["pw"],
                    bass.IndirectOffsetOnAxis(ap=tok_ids[:, c:c + 1].bitcast(U32), axis=0)),
                    (s, 16 * (j + 1)), ld_tok, *pw[b % 2].free)

        def norm(scratch, src, dst, t, *free):
            st, mv, nr = scratch
            for j in range(TILES):
                t1 = DVE.do(lambda e, j=j: e.bn_stats(st[:, j, :], src[:, j, :]), t, *st.free, n=128)
            yield DVE
            for j in range(TILES):
                t1 = DVE.do(lambda e, j=j: e.bn_aggr(mv[:, j, :], st[:, j, :]), t1, *mv.free)
            yield DVE
            v, half, a, y = (nr[:, i, :] for i in range(4))
            t1 = ts(DVE, v, mv[:, :, 1], 1e-5, ALU.add, t1, *nr.free)
            yield DVE
            t2 = DVE.do(lambda e: e.tensor_scalar(a.bitcast(I32), v.bitcast(I32), 1, None,
                                                  ALU.logical_shift_right), t1)
            t1 = ts(DVE, half, v, -0.5, ALU.mult, t1)
            yield DVE
            t1 = ts(DVE, y.bitcast(I32), a.bitcast(I32), -1.0, ALU.mult, t1, t2, s2=float(RSQRT_SEED), op1=ALU.add)
            yield DVE
            for _ in range(3):
                t1 = tt(DVE, a, y, y, ALU.mult, t1)
                yield DVE
                t1 = tt(DVE, a, a, half, ALU.mult, t1)
                yield DVE
                t1 = DVE.do(lambda e: e.scalar_tensor_tensor(out=y, in0=a, scalar=1.5, in1=y, op0=ALU.add,
                                                             op1=ALU.mult), t1)
                yield DVE
            for j in range(TILES):
                t2 = ts(DVE, dst[:, j, :], src[:, j, :], mv[:, j, 0:1], ALU.subtract, t1, *free,
                        s2=nr[:, 3, j:j + 1], op1=ALU.mult)
            st.free = mv.free = nr.free = (t2,)
            yield
            return t2

        y_taken = [0]
        g_taken = [0]

        def to_features(bank, src, dst, t, **kw):
            yield from bank.grab()
            t = turn_tiles(bank, rows_of(src), t, *bank.free)
            yield ACTE
            t1 = act(dst.ap, bank.ap, kw.pop("func", ACT.Copy), t, *dst.free, **kw)
            bank.drop(t1)
            return t, t1

        z_done, h_done = [None] * NBLK, [None] * NBLK
        f_taken = [0]
        h_taken = [0]

        def normalise_input():
            yield lambda: over["heads"][0] if "heads" in over else None
            hand_over([*ids, *pw, *z1s, *z2s, *fT, gT[2], *h2s, *scratch_in, *scratch_out], "heads")
            fetch(0)
            for b in range(NBLK):
                yield lambda: f_taken[0] >= b - 1 and x1_done[b]
                x = x1[:, TILES * b:TILES * (b + 1), :]
                z1, z2, g = z1s[b % 2], z2s[b % 2], pw[b % 2]
                t_z1 = yield from norm(scratch_in, x, z1, x1_done[b], *z1.free)
                t = tt(POOL, z2.ap, z1.ap, g[:, :, 0:P], ALU.mult, t_z1, ld_pw[b], *z2.free)
                yield POOL
                t_p = tt(POOL, z2.ap, z2.ap, g[:, :, P:2 * P], ALU.add, t)
                g.free = (t_p,)
                yield DVE
                t = yield from norm(scratch_in, z2, z2, t_p)
                z_done[b] = (t, t_z1, t_p)

        def condition():
            A, B = banks[6], banks[7]
            for b in range(NBLK):
                yield lambda: z_done[b] and z_done[b][0]
                fetch(b + 1)
                t_z2, t_z1, t_p = z_done[b]
                z1, z2 = z1s[b % 2], z2s[b % 2]
                x = x1[:, TILES * b:TILES * (b + 1), :]
                onehot = onehots[b % 2]
                t_oh = ts(DVE, onehot.ap, ids[b % 2].ap, idval[:, 0:1], ALU.is_equal, ld_ids[b], ld_idval)
                t1, t_f1 = yield from to_features(A, z1, fT[1], t_z1)
                z1.free = (t_p, t1)
                t1, t_f0 = yield from to_features(B, z2, fT[0], t_z2)
                z2.free = (t1,)
                f_taken[0] += 1
                _, t_f2 = yield from to_features(A, x, fT[2], x1_done[b])
                yield lambda: "tabs" in marks and marks["tabs"]
                tg = [None] * 3
                for k, bank in ((2, B), (1, A), (0, B)):
                    f, t_f = (fT[0], t_f0) if k == 0 else (fT[1], t_f1)
                    yield from bank.grab()
                    t = mm(bank.ap, tabs[0][:, k, :], onehot.ap, t_oh, marks["tabs"], *bank.free)
                    yield DVE
                    tg[k] = tt(DVE, gT[k].ap, f.ap, bank.ap, ALU.mult, t, t_f, *(gT[2].free if k == 2 else ()))
                    bank.drop(tg[k])
                    yield
                yield from A.grab()
                mm(A.ap, tabs[0][:, 3, :], onehot.ap, *A.free, start=True, stop=False, signal=False)
                mm(A.ap, Wx.ap, fT[2].ap, t_f2, marks["W1"], start=False, stop=False, signal=False)
                mm(A.ap, W1w[:, 5, :], gT[2].ap, tg[2], start=False, stop=False, signal=False)
                yield PE
                mm(A.ap, W1w[:, 1, :], gT[1].ap, tg[1], start=False, stop=False, signal=False)
                yield lambda: "base" in marks and marks["base"]
                t = mm(A.ap, W1w[:, 0, :], gT[0].ap, tg[0], start=False, stop=True)
                ids[b % 2].free = fT[2].free = (t,)
                for k in range(3):
                    gT[k].free = (t,)
                yield ACTE
                for j in range(TILES):
                    c = TILES * b + j
                    t = act(s1T[:, j * P:(j + 1) * P], A[:, j * P:(j + 1) * P], ACT.Silu, t, marks["base"],
                            *s1T.free, bias=base[:, c:c + 1])
                A.drop(t)
                yield
                yield from B.grab()
                for j, sj in enumerate(squares(s1T)):
                    t1 = mm(B[:, j * P:(j + 1) * P], sj, W2, t, *B.free, signal=j == TILES - 1)
                s1T.free = (t1,)
                yield lambda: h_taken[0] >= b - 1
                h2 = h2s[b % 2]
                t = tt(DVE, h2.ap, B[:, :].rearrange("p (t f) -> p t f", t=TILES), across(b2_rows, P), ALU.add, t1,
                       *h2.free)
                B.drop(t)
                h_done[b] = t
                yield

        def normalise_output():
            A = banks[6]
            yield lambda: "projections" in over and over["projections"][0]
            hand_over([*yT, *yh, *yl], "projections")
            for b in range(NBLK):
                yield lambda: h_done[b]
                h2 = h2s[b % 2]
                t = yield from norm(scratch_out, h2, h2, h_done[b])
                yield lambda: y_taken[0] >= b - 1 and g_taken[0] >= b - 1
                y = yT[b % 2]
                t, t_y = yield from to_features(A, h2, y, t, func=ACT.Identity, scale=col["int_g"],
                                                bias=col["int_be"])
                h2.free = (t,)
                h_taken[0] += 1
                yield ACTE
                t_h = act(yh[b % 2].ap, y.ap, ACT.Copy, t_y, *yh[b % 2].free)
                ready_y[b] = t_y
                yield POOL
                ready_yl[b] = tt(POOL, yl[b % 2].ap, y.ap, yh[b % 2][:, :].bitcast(F32), ALU.subtract,
                                 t_h, *yl[b % 2].free)
                yield

        def choose():
            A, B = banks[6], banks[7]
            yield lambda: "projections" in over and over["projections"][0]
            t_chl0 = POOL.do(lambda e: e.memset(chl.ap, 0.0), *over["projections"])
            hand_over([rl, top1, topi1, r1, R1], "projections")
            for b in range(NBLK):
                yield lambda: ready_y[b]
                y = yT[b % 2]
                yield from B.grab()
                for j, yj in enumerate(squares(y)):
                    t = mm(B[:, E1 * j:E1 * (j + 1)], yj, routerT, ready_y[b], *B.free, signal=j == TILES - 1)
                yield DVE
                t = DVE.do(lambda e: e.tensor_copy(
                    rl.ap, B[:, 0:TILES * E1].rearrange("p (t n) -> p t n", t=TILES)), t, *rl.free)
                B.drop(t)
                yield DVE
                for j in range(TILES):
                    t_top = DVE.do(lambda e, j=j: e.max(top1[:, j, :], rl[:, j, :]), t, *top1.free)
                yield DVE
                for j in range(TILES):
                    t = DVE.do(lambda e, j=j: e.max_index(topi1[:, j, :], top1[:, j, :], rl[:, j, :]), t_top)
                t_d = tt(DVE, r1[:, 2, :], top1[:, :, 0], top1[:, :, 1], ALU.subtract, t_top, *r1.free)
                t = DVE.do(lambda e: e.tensor_copy(r1[:, 0:2, :], topi1[:, :, 0:2].rearrange("p t k -> p k t")), t)
                rl.free = (t,)
                top1.free = (t_d, t)
                t_d = act(r1[:, 3, :], r1[:, 2, :], ACT.Tanh, t_d, scale=0.5)
                yield DVE
                i8 = across(iota[:, 0:E1], E1)
                t3 = tt(DVE, R1[:, :, 0, :], i8, bc(r1[:, 0, :], E1), ALU.is_equal, t, *R1.free)
                t4 = tt(DVE, R1[:, :, 1, :], i8, bc(r1[:, 1, :], E1), ALU.is_equal, t)
                t1 = ts(DVE, r1[:, 4, :], r1[:, 3, :], 0.5, ALU.mult, t_d, s2=0.5, op1=ALU.add)
                t2 = ts(DVE, r1[:, 5, :], r1[:, 3, :], -0.5, ALU.mult, t_d, s2=0.5, op1=ALU.add)
                yield DVE
                t = tt(DVE, R1[:, :, 0, :], R1[:, :, 0, :], bc(r1[:, 4, :], E1), ALU.mult, t1, t3)
                t5 = tt(DVE, R1[:, :, 1, :], R1[:, :, 1, :], bc(r1[:, 5, :], E1), ALU.mult, t2, t4)
                yield DVE
                t = tt(DVE, R1[:, :, 2, :], R1[:, :, 0, :], R1[:, :, 1, :], ALU.add, t, t5)
                r1.free = (t,)
                yield ACTE
                t = act(chl[:, :, 0:E1].bitcast(F32R), R1[:, :, 2, :], ACT.Copy, t, t_chl0, *chl.free)
                yield DVE
                t = tt(DVE, chl[:, :, LO:LO + E1], R1[:, :, 2, :], chl[:, :, 0:E1], ALU.subtract, t)
                R1.free = (t,)
                yield
                yield from A.grab()
                for j in range(TILES):
                    t1 = turn(A[0:LO + E1, j * P:(j + 1) * P], chl[:, j, :], ident, t, *A.free,
                              signal=j == TILES - 1)
                chl.free = (t1,)
                yield lambda: y_taken[0] >= b - 1
                c = wT[b % 2]
                t = act(c[0:LO + E1, :], A[0:LO + E1, :], ACT.Copy, t1, *c.free)
                A.drop(t)
                ready_cT[b] = t
                yield

        buffers_in("outputs", 1)
        sg = dup(2, "sg", [P, BLK])
        hp = dup(3, "hp", [P, BLK])
        ffT = sb("ffT", [P, BLK])
        hh = dup(3, "hh", [P, BLK], F32R)
        hl = dup(3, "hl", [P, BLK], F32R)
        s_out = semaphore("out_written")
        first_made = NBLK * E0
        gated, silued, upped, hidden, h_rounded, h_split, downed = {}, {}, {}, {}, {}, {}, {}
        ff_copied = [None] * NBLK
        x_last = [None] * NBLK
        turned = [0]

        def gate():
            m = 0
            yield lambda: "outputs" in over and over["outputs"][0]
            hand_over([*sg, *hp, ffT, *hh, *hl], "outputs")
            for b in range(NBLK):
                yhi, ylo = yh[b % 2], yl[b % 2]
                for j in range(CH1):
                    yield AHEAD, lambda: ((j // 4, 0) in t_gu and (m < 2 or m - 2 in silued) and ready_yl[b]), PE
                    g = banks[m % 2]
                    mm(g.ap, wgu[0][:, 0, j, :], yhi.ap, ready_yl[b], t_gu[j // 4, 0], *g.free, start=True,
                       stop=False, signal=False)
                    mm(g.ap, wgu[1][:, 0, j, :], yhi.ap, start=False, stop=False, signal=False)
                    gated[m] = mm(g.ap, wgu[0][:, 0, j, :], ylo.ap, start=False, stop=True)
                    m += 1
                yhi.free = ylo.free = (gated[m - 1],)
                g_taken[0] += 1

        def up():
            m = 0
            for b in range(NBLK):
                for j in range(CH1):
                    n = first_made + m // 2
                    yield AHEAD, lambda: (m < 2 or m - 2 in hidden) and (j // 4, 1) in t_gu and "outputs" in over and rounded.get(n), PE
                    u = banks[2 + m % 2]
                    zhi, zlo = zh[n % RING], zl[n % RING]
                    mm(u.ap, wgu[0][:, 1, j, :], zhi.ap, rounded[n], t_gu[j // 4, 1], *u.free, start=True,
                       stop=False, signal=False)
                    mm(u.ap, wgu[1][:, 1, j, :], zhi.ap, start=False, stop=False, signal=False)
                    yield AHEAD, lambda: split.get(n), PE
                    upped[m] = mm(u.ap, wgu[0][:, 1, j, :], zlo.ap, split[n], start=False, stop=True)
                    if j % 2:
                        zhi.free = zlo.free = (upped[m],)
                        consumed[n] = upped[m]
                    m += 1

        def activate():
            for m in range(NBLK * CH1):
                yield AHEAD, lambda: (m < 2 or m - 2 in hidden) and gated.get(m), ACTE
                g, s = banks[m % 2], sg[m % 2]
                silued[m] = act(s.ap, g.ap, ACT.Silu, gated[m], *s.free)
                g.free = (silued[m],)

        def multiply_hidden():
            for m in range(NBLK * CH1):
                yield AHEAD, lambda: (m < 3 or m - 3 in h_split) and m in upped and later(silued.get(m), upped[m]), DVE
                u, s, h = banks[2 + m % 2], sg[m % 2], hp[m % 3]
                hidden[m] = tt(DVE, h.ap, s.ap, u.ap, ALU.mult, silued[m], upped[m], *h.free)
                s.free = u.free = (hidden[m],)

        def round_hidden():
            for m in range(NBLK * CH1):
                yield AHEAD, lambda: (m < 3 or m - 3 in downed) and hidden.get(m), ACTE
                h, hi = hp[m % 3], hh[m % 3]
                h_rounded[m] = act(hi.ap, h.ap, ACT.Copy, hidden[m], *hi.free)

        def rest_of_hidden():
            for m in range(NBLK * CH1):
                yield AHEAD, lambda: h_rounded.get(m), POOL
                h, hi, lo = hp[m % 3], hh[m % 3], hl[m % 3]
                h_split[m] = tt(POOL, lo.ap, h.ap, hi[:, :].bitcast(F32), ALU.subtract, h_rounded[m], *lo.free)
                h.free = (h_split[m],)

        def down():
            dn = banks[5]
            m = 0
            for b in range(NBLK):
                yield lambda: "outputs" in over and (b == 0 or ff_copied[b - 1])
                for j in range(CH1):
                    yield AHEAD, lambda: j // 4 in t_dn and h_rounded.get(m), PE
                    hi, lo = hh[m % 3], hl[m % 3]
                    first = dn.free if j == 0 else ()
                    mm(dn.ap, wdn[0][:, j, :], hi.ap, h_rounded[m], t_dn[j // 4], *first, start=j == 0, stop=False,
                       signal=False)
                    mm(dn.ap, wdn[1][:, j, :], hi.ap, start=False, stop=False, signal=False)
                    yield AHEAD, lambda: h_split.get(m), PE
                    t = mm(dn.ap, wdn[0][:, j, :], lo.ap, h_split[m], start=False, stop=j == CH1 - 1)
                    hi.free = lo.free = (t,)
                    downed[m] = t
                    m += 1
                yield lambda: turned[0] >= b and t
                t = act(ffT.ap, dn.ap, ACT.Copy, t, *ffT.free)
                dn.free = (t,)
                ff_copied[b] = t
                x_last[b] = t

        def finish():
            for b in range(NBLK):
                yield lambda: x_last[b]
                bank = banks[7]
                yield from bank.grab()
                t = turn_tiles(bank, squares(ffT), x_last[b], *bank.free)
                ffT.free = (t,)
                turned[0] += 1
                yield DVE
                rows = slice(TILES * b, TILES * (b + 1))
                t = tt(DVE, x1[:, rows, :], x1[:, rows, :], bank[:, :].rearrange("p (t f) -> p t f", t=TILES),
                       ALU.add, t)
                bank.drop(t)
                SP.dma(lambda e, rows=rows: e.dma_start(out[rows, :, :].rearrange("b p d -> p b d"), x1[:, rows, :]),
                       (s_out, 16 * (b + 1)), t)
                yield

        pair, single = banks[3:5], banks[4:5]
        weave(split_weights(), route(), row_attention(),
              spread_weights(wT, slice(0, LO + E0), ready_wT, 0, E0, pair),
              scale_inputs(x0T, ready_x0T, 0, E0, pair, x0_taken), round_inputs(0, NBLK * E0),
              rest_of_inputs(0, NBLK * E0), project_out(), head_values(), head_scores(), project(),
              setup_condition(), split_expert_weights(), choose(), normalise_output(),
              spread_weights(wT, slice(0, LO + E1), ready_cT, first_made, E1, single),
              scale_inputs(yT, ready_y, first_made, E1, single, y_taken), round_inputs(first_made, NBLK * E1),
              rest_of_inputs(first_made, NBLK * E1), activate(), multiply_hidden(), round_hidden(),
              rest_of_hidden(), condition(), normalise_input(), finish(), down(), up(), gate(),
              lead=LEAD)
        SP.do(None, (s_out, 16 * NBLK), signal=False)

        block = ctx.enter_context(nc.Block())

        @block.tensor
        def _(e):
            PE.play(e)

        @block.vector
        def _(e):
            DVE.play(e)

        @block.scalar
        def _(e):
            ACTE.play(e)

        @block.gpsimd
        def _(e):
            POOL.play(e)

        @block.sync
        def _(e):
            SP.play(e)


def layout(np, v):
    f = {k: np.asarray(a) for k, a in v.items()}
    cat = np.concatenate
    z = np.float32(0)

    def rows(a, n):
        return np.broadcast_to(a.reshape(1, -1), (n, a.size))

    def column(a):
        return a.reshape(-1, 1)

    x = f["x"]
    ins = {
        "xT": x.reshape(NTOK, P).T,
        "x_tok": x.transpose(1, 0, 2),
        "p64": cat([f["L0_cond_k_aff_w"].T, f["L0_cond_o_aff_w"].T, f["cond_512"].T], 1),
        "p0": cat([f["L0_cond_k_w"].T, f["L0_cond_o_w"].T, column(f["L0_cond_k_aff_b"]), column(f["L0_cond_k_b"]),
                   column(f["L0_cond_o_aff_b"]), column(f["L0_cond_o_b"]), rows(f["L0_ffn_gates"], P),
                   rows(f["L1_cond_aw"], P), f["L0_ffn_sim_matrix"]], 1),
        "w_qkv": np.stack([f["L0_ffn_q_proj"], f["L0_ffn_k_proj"], f["L0_ffn_v_proj"]], 1)
                   .transpose(2, 0, 1, 3).reshape(P, -1),
        "w_o": f["L0_ffn_o_proj"].transpose(1, 0, 2).reshape(P, -1),
        "w_gu": np.stack([f["L1_ffn_w_gate"].reshape(CH1, P, P), f["L1_ffn_w_up"].reshape(CH1, P, P)], 0)
                  .transpose(3, 0, 1, 2),
        "w_dn": f["L1_ffn_w_down"].reshape(E1, P, 2, P).transpose(3, 0, 2, 1).reshape(P, CH1, P),
    }
    pre = "L1_cond_"
    mlps = ("mem", "noi", "res")
    ins["p1"] = cat(
        [f[pre + "int_W1"].reshape(6, P, P).transpose(1, 0, 2).reshape(P, -1), f[pre + "int_W2"],
         f["L1_ffn_router_w"].T, rows(f[pre + "int_b2"], P)]
        + [f[pre + m + "_W2"] for m in mlps] + [rows(f[pre + m + "_b2"], P) for m in mlps]
        + [column(f[pre + n]) for n in ("int_b1", "int_g", "int_be", "mem_b1", "noi_b1", "res_b1", "mem_g", "mem_be",
                                        "noi_g", "noi_be", "res_g", "res_be")]
        + [f[pre + "cp_b"].T, f[pre + "tm_b"].T, f[pre + "ms_b"].T, np.zeros((P, 8), np.float32)], 1)
    tabs = np.zeros((LO + 8, 3, P), np.float32)
    ids = np.zeros((LO + 8, NTOK), f["itok_BxS_0_4"].dtype)
    for o in (0, LO):
        tabs[o:o + 5, 0], tabs[o:o + 5, 1], tabs[o + 5:o + 8, 2] = f[pre + "cp_g"], f[pre + "tm_g"], f[pre + "ms_g"]
        ids[o:o + 5], ids[o + 5:o + 8] = f["itok_BxS_0_4"].reshape(-1), f["mask_BxS_ik0"].reshape(-1)
    ins["tabs"], ins["ids"] = tabs, ids
    ins["pw"] = cat([f[pre + "pw_g"], f[pre + "pw_b"]], 1)
    ins["tok_ids"] = f["itok_BxS_0_999"].T
    ins["pm64"] = cat([f[pre + "mem_W1"], f[pre + "noi_W1"], f["cond_512"].T, f["cond_64"].T], 1)
    ins["pm32"] = cat([f[pre + "res_W1"], f["fside_Bx32_0"].T], 1)
    ins["c_const"] = cat([np.eye(P), np.ones((P, P)), np.broadcast_to(np.arange(16.0), (P, 16))], 1) \
        .astype(np.float32)
    sel = np.zeros((LO + E0, E0), np.float32)
    sel[np.arange(E0), np.arange(E0)] = sel[LO + np.arange(E0), np.arange(E0)] = 1
    val = np.full((LO + 8, 1), -1, np.float32)
    for o in (0, LO):
        val[o:o + 8, 0] = [0, 1, 2, 3, 4, 0, 1, 2]
    ins["c_sel"], ins["c_idval"] = sel, val
    return {k: np.ascontiguousarray(a) for k, a in ins.items()}


def kernel(**inputs):
    import numpy as np
    import concourse.bacc as bacc
    from concourse.bass_utils import run_bass_kernel_spmd

    nc = bacc.Bacc("TRN2", target_bir_lowering=False, num_devices=1)
    arrays = layout(np, inputs)
    ins = {k: nc.dram_tensor("in_" + k, a.shape, mybir.dt.from_np(a.dtype), kind="ExternalInput").ap()
           for k, a in arrays.items()}
    out = nc.dram_tensor("out_0", (NBATCH, P, P), F32, kind="ExternalOutput").ap()
    build_program(nc, ins, out)
    r = run_bass_kernel_spmd(nc, [{"in_" + k: a for k, a in arrays.items()}], core_ids=[0])
    return r.results[0]["out_0"]
```
